# Optimizing a Trainium2 kernel written in Bass

```python
import numpy as np
import jax
import jax.numpy as jnp

def _softmax(x, axis=-1):
    return jax.nn.softmax(x, axis=axis)

def _gelu(x):
    return jax.nn.gelu(x, approximate=True)

def _silu(x):
    return jax.nn.silu(x)

def _sigmoid(x):
    return jax.nn.sigmoid(x)

def _layernorm(x, axis=-1, eps=1e-05):
    m = jnp.mean(x, axis=axis, keepdims=True)
    v = jnp.var(x, axis=axis, keepdims=True)
    return (x - m) / jnp.sqrt(v + eps)

def _scatter_add(tgt, idx, src, axis=0):
    return tgt.at[idx].add(src)

def _segment_sum(src, seg, n):
    return jax.ops.segment_sum(src, seg, n)
kernel_name = 'mk_perceiver_d2_seqx_r4_5033ef'

def setup_inputs(seed: int=0):
    np.random.seed(seed)
    _w = jnp.asarray

    def _rec_inputs():
        import jax
        import jax.numpy as jnp
        _rk = jax.random.key(seed)
        x = -0.0003929 + 0.9999 * jax.random.normal(jax.random.fold_in(_rk, 1), (32, 64, 256), jnp.float32)
        _lenS = 64 - jax.random.randint(jax.random.fold_in(_rk, 7), (32,), 0, max(1, 64 // 4) + 1, jnp.int32)
        _lenS2 = 1601 - jax.random.randint(jax.random.fold_in(_rk, 8), (32,), 0, max(1, 1601 // 4) + 1, jnp.int32)
        _ctx_512P = jax.random.normal(jax.random.fold_in(_rk, 11), (32, 16, 128), jnp.float32)
        _ctx_512c = jax.random.dirichlet(jax.random.fold_in(_rk, 511), 0.3 * jnp.ones((16,), jnp.float32), (32, 1601))
        _ctx_512t = jnp.einsum('bsk,bkd->bsd', _ctx_512c, _ctx_512P)
        _ctx_512t = _ctx_512t * jax.lax.rsqrt(jnp.mean(jnp.square(_ctx_512t)) + 1e-12) * 0.953939
        ctx_512 = -1.39393e-06 + 0.999914 * (_ctx_512t + 0.3 * jax.random.normal(jax.random.fold_in(_rk, 611), (32, 1601, 128), jnp.float32))
        return (x, ctx_512)
    x, ctx_512 = _rec_inputs()

    def _L0_xattn_setup():
        import jax, jax.numpy as jnp
        import numpy as np
        HEADS = 16
        D_MODEL = 256
        IMG_MODEL = 128
        D_K = D_MODEL // HEADS
        key = jax.random.key(seed)
        ks = jax.random.split(key, 12)
        B, LQ, LKV = (8, 512, 256)
        s_dm = 1.0 / np.sqrt(D_MODEL)
        s_im = 1.0 / np.sqrt(IMG_MODEL)
        return {'q': jax.random.normal(ks[0], (B, LQ, D_MODEL), jnp.float32), 'k': jax.random.normal(ks[1], (B, LKV, IMG_MODEL), jnp.float32), 'v': jax.random.normal(ks[2], (B, LKV, IMG_MODEL), jnp.float32), 'Wq': jax.random.normal(ks[3], (D_MODEL, D_MODEL), jnp.float32) * s_dm, 'bq': jnp.zeros((D_MODEL,), jnp.float32), 'Wk': jax.random.normal(ks[4], (IMG_MODEL, D_MODEL), jnp.float32) * s_im, 'bk': jnp.zeros((D_MODEL,), jnp.float32), 'Wv': jax.random.normal(ks[5], (IMG_MODEL, D_MODEL), jnp.float32) * s_im, 'bv': jnp.zeros((D_MODEL,), jnp.float32), 'Wo': jax.random.normal(ks[6], (D_MODEL, D_MODEL), jnp.float32) * s_dm, 'bo': jnp.zeros((D_MODEL,), jnp.float32)}
    _L0_xattn_all = _L0_xattn_setup()
    _L0_xattn_in = {k: v for k, v in _L0_xattn_all.items() if k in ('Wq', 'bq', 'Wk', 'bk', 'Wv', 'bv', 'Wo', 'bo')}
    del _L0_xattn_all

    def _L0_attn_setup():
        import jax, jax.numpy as jnp
        import numpy as np
        NUM_HEADS = 16
        HIDDEN = 256
        HEAD = HIDDEN // NUM_HEADS
        key = jax.random.key(seed)
        k1, k2 = jax.random.split(key)
        embeddings = jax.random.normal(k1, (4, 512, HIDDEN), dtype=jnp.float32)
        w_qkv = jax.random.normal(k2, (HIDDEN, 3 * HIDDEN), dtype=jnp.float32) * (1.0 / np.sqrt(HIDDEN))
        return {'embeddings': embeddings, 'w_qkv': w_qkv}
    _L0_attn_all = _L0_attn_setup()
    _L0_attn_in = {k: v for k, v in _L0_attn_all.items() if k in ('w_qkv',)}
    del _L0_attn_all

    def _L0_ffn_setup():
        import jax, jax.numpy as jnp
        import numpy as np
        E, K = (8, 2)
        DM, DE = (256, 704)
        B, S = (1, 512)
        EPS = 1e-06

        def _rmsnorm(x, w):
            var = jnp.mean(jnp.square(x), axis=-1, keepdims=True)
            return x * jax.lax.rsqrt(var + EPS) * w
        key = jax.random.key(seed)
        kx, kg, k1, k2, k3 = jax.random.split(key, 5)

        def kaiming_uniform(k, shape, fan_in):
            bound = 1.0 / np.sqrt(fan_in)
            return jax.random.uniform(k, shape, jnp.float32, -bound, bound)
        return {'x': jax.random.normal(kx, (B, S, DM), jnp.float32), 'gate_w': kaiming_uniform(kg, (E, DM), DM), 'rms_w': jnp.ones((DM,), jnp.float32), 'W1': kaiming_uniform(k1, (E, DE, DM), DE * DM), 'W2': kaiming_uniform(k2, (E, DE, DM), DE * DM), 'W3': kaiming_uniform(k3, (E, DM, DE), DM * DE)}
    _L0_ffn_all = _L0_ffn_setup()
    _L0_ffn_in = {k: v for k, v in _L0_ffn_all.items() if k in ('gate_w', 'rms_w', 'W1', 'W2', 'W3')}
    del _L0_ffn_all

    def _L1_xattn_setup():
        import jax, jax.numpy as jnp
        import numpy as np
        DIM = 256
        LATENT_DIM = 128
        NUM_HEADS = 16
        HEAD_DIM = DIM // NUM_HEADS
        SCALE = HEAD_DIM ** (-0.5)
        key = jax.random.key(seed)
        k1, k2, k3, k4, k5 = jax.random.split(key, 5)
        B, xN, zN = (2, 512, 512)
        x = jax.random.normal(k1, (B, xN, DIM), dtype=jnp.float32)
        z = jax.random.normal(k2, (B, zN, LATENT_DIM), dtype=jnp.float32)
        Wq = jax.random.normal(k3, (DIM, DIM), dtype=jnp.float32) * DIM ** (-0.5)
        Wkv = jax.random.normal(k4, (2 * DIM, LATENT_DIM), dtype=jnp.float32) * LATENT_DIM ** (-0.5)
        Wo = jax.random.normal(k5, (DIM, DIM), dtype=jnp.float32) * DIM ** (-0.5)
        return {'x': x, 'z': z, 'Wq': Wq, 'Wkv': Wkv, 'Wo': Wo}
    _L1_xattn_all = _L1_xattn_setup()
    _L1_xattn_in = {k: v for k, v in _L1_xattn_all.items() if k in ('Wq', 'Wkv', 'Wo')}
    del _L1_xattn_all

    def _L1_attn_setup():
        import jax, jax.numpy as jnp
        import numpy as np

        def _silu(x):
            return x * jax.nn.sigmoid(x)

        def _mamba_dir(h, W_in, conv_w, conv_b, Wx, Wdt, bdt, A_log, Dp, W_out):
            Bsz, L, Dm = h.shape
            Di = W_in.shape[0] // 2
            N = A_log.shape[1]
            K = conv_w.shape[1]
            dt_rank = Wdt.shape[1]
            xz = jnp.einsum('bld,ed->ble', h, W_in)
            x, z = (xz[..., :Di], xz[..., Di:])
            xc = jnp.transpose(x, (0, 2, 1))
            xc = jax.lax.conv_general_dilated(xc, conv_w[:, None, :], window_strides=(1,), padding=[(K - 1, 0)], dimension_numbers=('NCH', 'OIH', 'NCH'), feature_group_count=Di)
            x = _silu(jnp.transpose(xc, (0, 2, 1)) + conv_b[None, None, :])
            x_dbl = jnp.einsum('bld,ed->ble', x, Wx)
            dt = x_dbl[..., :dt_rank]
            Bm = x_dbl[..., dt_rank:dt_rank + N]
            Cm = x_dbl[..., dt_rank + N:]
            dt = jax.nn.softplus(jnp.einsum('blr,dr->bld', dt, Wdt) + bdt)
            A = -jnp.exp(A_log)
            dA = jnp.exp(dt[..., None] * A)
            dBx = (dt * x)[..., None] * Bm[:, :, None, :]

            def step(hc, inp):
                dA_t, dBx_t, C_t = inp
                hc = dA_t * hc + dBx_t
                return (hc, jnp.einsum('bdn,bn->bd', hc, C_t))
            h0 = jnp.zeros((Bsz, Di, N), dtype=x.dtype)
            _, ys = jax.lax.scan(step, h0, (jnp.moveaxis(dA, 1, 0), jnp.moveaxis(dBx, 1, 0), jnp.moveaxis(Cm, 1, 0)))
            y = jnp.moveaxis(ys, 0, 1) + x * Dp
            y = y * _silu(z)
            return jnp.einsum('bld,ed->ble', y, W_out)
        key = jax.random.key(seed)
        ks = jax.random.split(key, 16)
        B, L, Dm = (1, 512, 256)
        Di, N, Kc, R = (512, 16, 4, 64)
        s = 0.02
        inp = {'hidden_states': jax.random.normal(ks[0], (B, L, Dm), jnp.float32), 'W_in': jax.random.normal(ks[1], (2 * Di, Dm), jnp.float32) * s, 'W_out': jax.random.normal(ks[2], (Dm, Di), jnp.float32) * s}
        a_log = jnp.log(jnp.broadcast_to(jnp.arange(1, N + 1, dtype=jnp.float32), (Di, N)))
        for i, d in enumerate(['fwd', 'rev']):
            o = 3 + 6 * i
            inp[f'conv_w_{d}'] = jax.random.normal(ks[o + 0], (Di, Kc), jnp.float32) * 0.2
            inp[f'conv_b_{d}'] = jnp.zeros((Di,), jnp.float32)
            inp[f'Wx_{d}'] = jax.random.normal(ks[o + 1], (R + 2 * N, Di), jnp.float32) * s
            inp[f'Wdt_{d}'] = jax.random.normal(ks[o + 2], (Di, R), jnp.float32) * s
            inp[f'bdt_{d}'] = jnp.full((Di,), -4.6, jnp.float32)
            inp[f'A_log_{d}'] = a_log
            inp[f'D_{d}'] = jnp.ones((Di,), jnp.float32)
        return inp
    _L1_attn_all = _L1_attn_setup()
    _L1_attn_in = {k: v for k, v in _L1_attn_all.items() if k in ('W_in', 'W_out', 'conv_w_fwd', 'conv_b_fwd', 'Wx_fwd', 'Wdt_fwd', 'bdt_fwd', 'A_log_fwd', 'D_fwd', 'conv_w_rev', 'conv_b_rev', 'Wx_rev', 'Wdt_rev', 'bdt_rev', 'A_log_rev', 'D_rev')}
    del _L1_attn_all

    def _L1_ffn_setup():
        import jax, jax.numpy as jnp
        import numpy as np
        D_MODEL, D_FF, NUM_EXPERTS, RANK, TOP_K = (256, 1024, 8, 16, 2)
        B, S = (8, 512)

        def _expert_ffn(h, wi_w, wo_w, A, Bm):
            inter = jnp.einsum('bsd,fd->bsf', h, wi_w)
            lora = jnp.einsum('bsr,fr->bsf', jnp.einsum('bsd,rd->bsr', h, A), Bm)
            inter = jax.nn.relu(inter + lora)
            return jnp.einsum('bsf,df->bsd', inter, wo_w)
        key = jax.random.key(seed)
        ks = jax.random.split(key, 8)
        hidden_states = jax.random.normal(ks[0], (B, S, D_MODEL), dtype=jnp.float32)
        wi_w = jax.random.normal(ks[1], (D_FF, D_MODEL), dtype=jnp.float32) * (1.0 / np.sqrt(D_MODEL))
        wo_w = jax.random.normal(ks[2], (D_MODEL, D_FF), dtype=jnp.float32) * (1.0 / np.sqrt(D_FF))
        lora_As = jax.random.uniform(ks[3], (NUM_EXPERTS, RANK, D_MODEL), dtype=jnp.float32, minval=-1.0, maxval=1.0) / np.sqrt(D_MODEL)
        lora_Bs = jax.random.normal(ks[4], (NUM_EXPERTS, D_FF, RANK), dtype=jnp.float32) * 0.02
        top_k_indices = jnp.arange(TOP_K, dtype=jnp.int32)
        top_k_values = jax.random.uniform(ks[5], (TOP_K,), dtype=jnp.float32)
        return {'hidden_states': hidden_states, 'wi_w': wi_w, 'wo_w': wo_w, 'lora_As': lora_As, 'lora_Bs': lora_Bs, 'top_k_indices': top_k_indices, 'top_k_values': top_k_values}
    _L1_ffn_all = _L1_ffn_setup()
    _L1_ffn_in = {k: v for k, v in _L1_ffn_all.items() if k in ('wi_w', 'wo_w', 'lora_As', 'lora_Bs', 'top_k_indices', 'top_k_values')}
    del _L1_ffn_all
    return {'x': x, 'ctx_512': ctx_512, 'L0_xattn_Wq': _L0_xattn_in['Wq'], 'L0_xattn_bq': _L0_xattn_in['bq'], 'L0_xattn_Wk': _L0_xattn_in['Wk'], 'L0_xattn_bk': _L0_xattn_in['bk'], 'L0_xattn_Wv': _L0_xattn_in['Wv'], 'L0_xattn_bv': _L0_xattn_in['bv'], 'L0_xattn_Wo': _L0_xattn_in['Wo'], 'L0_xattn_bo': _L0_xattn_in['bo'], 'L0_attn_w_qkv': _L0_attn_in['w_qkv'], 'L0_ffn_gate_w': _L0_ffn_in['gate_w'], 'L0_ffn_rms_w': _L0_ffn_in['rms_w'], 'L0_ffn_W1': _L0_ffn_in['W1'], 'L0_ffn_W2': _L0_ffn_in['W2'], 'L0_ffn_W3': _L0_ffn_in['W3'], 'L1_xattn_Wq': _L1_xattn_in['Wq'], 'L1_xattn_Wkv': _L1_xattn_in['Wkv'], 'L1_xattn_Wo': _L1_xattn_in['Wo'], 'L1_attn_W_in': _L1_attn_in['W_in'], 'L1_attn_W_out': _L1_attn_in['W_out'], 'L1_attn_conv_w_fwd': _L1_attn_in['conv_w_fwd'], 'L1_attn_conv_b_fwd': _L1_attn_in['conv_b_fwd'], 'L1_attn_Wx_fwd': _L1_attn_in['Wx_fwd'], 'L1_attn_Wdt_fwd': _L1_attn_in['Wdt_fwd'], 'L1_attn_bdt_fwd': _L1_attn_in['bdt_fwd'], 'L1_attn_A_log_fwd': _L1_attn_in['A_log_fwd'], 'L1_attn_D_fwd': _L1_attn_in['D_fwd'], 'L1_attn_conv_w_rev': _L1_attn_in['conv_w_rev'], 'L1_attn_conv_b_rev': _L1_attn_in['conv_b_rev'], 'L1_attn_Wx_rev': _L1_attn_in['Wx_rev'], 'L1_attn_Wdt_rev': _L1_attn_in['Wdt_rev'], 'L1_attn_bdt_rev': _L1_attn_in['bdt_rev'], 'L1_attn_A_log_rev': _L1_attn_in['A_log_rev'], 'L1_attn_D_rev': _L1_attn_in['D_rev'], 'L1_ffn_wi_w': _L1_ffn_in['wi_w'], 'L1_ffn_wo_w': _L1_ffn_in['wo_w'], 'L1_ffn_lora_As': _L1_ffn_in['lora_As'], 'L1_ffn_lora_Bs': _L1_ffn_in['lora_Bs'], 'L1_ffn_top_k_indices': _L1_ffn_in['top_k_indices'], 'L1_ffn_top_k_values': _L1_ffn_in['top_k_values']}

def reference(x, ctx_512, L0_xattn_Wq, L0_xattn_bq, L0_xattn_Wk, L0_xattn_bk, L0_xattn_Wv, L0_xattn_bv, L0_xattn_Wo, L0_xattn_bo, L0_attn_w_qkv, L0_ffn_gate_w, L0_ffn_rms_w, L0_ffn_W1, L0_ffn_W2, L0_ffn_W3, L1_xattn_Wq, L1_xattn_Wkv, L1_xattn_Wo, L1_attn_W_in, L1_attn_W_out, L1_attn_conv_w_fwd, L1_attn_conv_b_fwd, L1_attn_Wx_fwd, L1_attn_Wdt_fwd, L1_attn_bdt_fwd, L1_attn_A_log_fwd, L1_attn_D_fwd, L1_attn_conv_w_rev, L1_attn_conv_b_rev, L1_attn_Wx_rev, L1_attn_Wdt_rev, L1_attn_bdt_rev, L1_attn_A_log_rev, L1_attn_D_rev, L1_ffn_wi_w, L1_ffn_wo_w, L1_ffn_lora_As, L1_ffn_lora_Bs, L1_ffn_top_k_indices, L1_ffn_top_k_values):
    import jax
    import jax.numpy as jnp

    def _L0_xattn_ref(q, k, v, Wq, bq, Wk, bk, Wv, bv, Wo, bo):
        import jax, jax.numpy as jnp
        import numpy as np
        HEADS = 16
        D_MODEL = 256
        IMG_MODEL = 128
        D_K = D_MODEL // HEADS
        B, LQ, _ = q.shape
        LKV = k.shape[1]
        qh = (q @ Wq + bq).reshape(B, LQ, HEADS, D_K).transpose(0, 2, 1, 3)
        kh = (k @ Wk + bk).reshape(B, LKV, HEADS, D_K).transpose(0, 2, 1, 3)
        vh = (v @ Wv + bv).reshape(B, LKV, HEADS, D_K).transpose(0, 2, 1, 3)
        scale = 1.0 / np.sqrt(D_K)
        scores = jnp.einsum('bhqd,bhkd->bhqk', qh, kh) * scale
        attn = jax.nn.softmax(scores, axis=-1)
        out = jnp.einsum('bhqk,bhkd->bhqd', attn, vh)
        concat = out.transpose(0, 2, 1, 3).reshape(B, LQ, D_MODEL)
        return concat @ Wo + bo

    def _L0_attn_ref(embeddings, w_qkv):
        import jax, jax.numpy as jnp
        import numpy as np
        NUM_HEADS = 16
        HIDDEN = 256
        HEAD = HIDDEN // NUM_HEADS
        b, s, h = embeddings.shape
        result = embeddings @ w_qkv
        result = result.reshape(b, s, 3, NUM_HEADS, HEAD)
        q = jnp.transpose(result[:, :, 0], (0, 2, 1, 3))
        k = jnp.transpose(result[:, :, 1], (0, 2, 1, 3))
        v = jnp.transpose(result[:, :, 2], (0, 2, 1, 3))
        scores = jnp.einsum('bnqd,bnkd->bnqk', q, k) / jnp.sqrt(jnp.float32(h))
        probs = jax.nn.softmax(scores, axis=-1)
        ctx = jnp.einsum('bnqk,bnkd->bnqd', probs, v)
        out = jnp.transpose(ctx, (0, 2, 1, 3)).reshape(b, s, h)
        return out

    def _L0_ffn_ref(x, gate_w, rms_w, W1, W2, W3):
        import jax, jax.numpy as jnp
        import numpy as np
        E, K = (8, 2)
        DM, DE = (256, 704)
        B, S = (1, 512)
        EPS = 1e-06

        def _rmsnorm(x, w):
            var = jnp.mean(jnp.square(x), axis=-1, keepdims=True)
            return x * jax.lax.rsqrt(var + EPS) * w
        y = _rmsnorm(x, rms_w)
        logits = jnp.einsum('bsd,ed->bse', y, gate_w)
        vals, idx = jax.lax.top_k(logits, K)
        w = jax.nn.softmax(vals, axis=-1)
        w_full = jnp.einsum('bsk,bske->bse', w, jax.nn.one_hot(idx, E, dtype=x.dtype))
        up = jnp.einsum('bsd,end->bsen', y, W1)
        gate = jnp.einsum('bsd,end->bsen', y, W2)
        h = jax.nn.silu(up) * gate
        out = jnp.einsum('bsen,emn->bsem', h, W3)
        comb = jnp.einsum('bsem,bse->bsm', out, w_full)
        return x + comb

    def _L1_xattn_ref(x, z, Wq, Wkv, Wo):
        import jax, jax.numpy as jnp
        import numpy as np
        DIM = 256
        LATENT_DIM = 128
        NUM_HEADS = 16
        HEAD_DIM = DIM // NUM_HEADS
        SCALE = HEAD_DIM ** (-0.5)
        B, xN, _ = x.shape
        _, zN, _ = z.shape
        Q = (x @ Wq.T).reshape(B, xN, NUM_HEADS, HEAD_DIM)
        KV = (z @ Wkv.T).reshape(B, zN, 2, NUM_HEADS, HEAD_DIM)
        K = KV[:, :, 0]
        V = KV[:, :, 1]
        attn = jnp.einsum('bqhd,bkhd->bhqk', Q, K) * SCALE
        attn = jax.nn.softmax(attn, axis=-1)
        O = jnp.einsum('bhqk,bkhd->bqhd', attn, V).reshape(B, xN, DIM)
        return O @ Wo.T

    def _L1_attn_ref(hidden_states, W_in, W_out, conv_w_fwd, conv_b_fwd, Wx_fwd, Wdt_fwd, bdt_fwd, A_log_fwd, D_fwd, conv_w_rev, conv_b_rev, Wx_rev, Wdt_rev, bdt_rev, A_log_rev, D_rev):
        import jax, jax.numpy as jnp
        import numpy as np

        def _silu(x):
            return x * jax.nn.sigmoid(x)

        def _mamba_dir(h, W_in, conv_w, conv_b, Wx, Wdt, bdt, A_log, Dp, W_out):
            Bsz, L, Dm = h.shape
            Di = W_in.shape[0] // 2
            N = A_log.shape[1]
            K = conv_w.shape[1]
            dt_rank = Wdt.shape[1]
            xz = jnp.einsum('bld,ed->ble', h, W_in)
            x, z = (xz[..., :Di], xz[..., Di:])
            xc = jnp.transpose(x, (0, 2, 1))
            xc = jax.lax.conv_general_dilated(xc, conv_w[:, None, :], window_strides=(1,), padding=[(K - 1, 0)], dimension_numbers=('NCH', 'OIH', 'NCH'), feature_group_count=Di)
            x = _silu(jnp.transpose(xc, (0, 2, 1)) + conv_b[None, None, :])
            x_dbl = jnp.einsum('bld,ed->ble', x, Wx)
            dt = x_dbl[..., :dt_rank]
            Bm = x_dbl[..., dt_rank:dt_rank + N]
            Cm = x_dbl[..., dt_rank + N:]
            dt = jax.nn.softplus(jnp.einsum('blr,dr->bld', dt, Wdt) + bdt)
            A = -jnp.exp(A_log)
            dA = jnp.exp(dt[..., None] * A)
            dBx = (dt * x)[..., None] * Bm[:, :, None, :]

            def step(hc, inp):
                dA_t, dBx_t, C_t = inp
                hc = dA_t * hc + dBx_t
                return (hc, jnp.einsum('bdn,bn->bd', hc, C_t))
            h0 = jnp.zeros((Bsz, Di, N), dtype=x.dtype)
            _, ys = jax.lax.scan(step, h0, (jnp.moveaxis(dA, 1, 0), jnp.moveaxis(dBx, 1, 0), jnp.moveaxis(Cm, 1, 0)))
            y = jnp.moveaxis(ys, 0, 1) + x * Dp
            y = y * _silu(z)
            return jnp.einsum('bld,ed->ble', y, W_out)
        out = _mamba_dir(hidden_states, W_in, conv_w_fwd, conv_b_fwd, Wx_fwd, Wdt_fwd, bdt_fwd, A_log_fwd, D_fwd, W_out)
        h_rev = jnp.flip(hidden_states, axis=-2)
        out_rev = _mamba_dir(h_rev, W_in, conv_w_rev, conv_b_rev, Wx_rev, Wdt_rev, bdt_rev, A_log_rev, D_rev, W_out)
        return out + jnp.flip(out_rev, axis=-2)

    def _L1_ffn_ref(hidden_states, wi_w, wo_w, lora_As, lora_Bs, top_k_indices, top_k_values):
        import jax, jax.numpy as jnp
        import numpy as np
        D_MODEL, D_FF, NUM_EXPERTS, RANK, TOP_K = (256, 1024, 8, 16, 2)
        B, S = (8, 512)

        def _expert_ffn(h, wi_w, wo_w, A, Bm):
            inter = jnp.einsum('bsd,fd->bsf', h, wi_w)
            lora = jnp.einsum('bsr,fr->bsf', jnp.einsum('bsd,rd->bsr', h, A), Bm)
            inter = jax.nn.relu(inter + lora)
            return jnp.einsum('bsf,df->bsd', inter, wo_w)
        out = jnp.zeros_like(hidden_states)
        for k in range(top_k_values.shape[0]):
            A = jnp.take(lora_As, top_k_indices[k], axis=0)
            Bm = jnp.take(lora_Bs, top_k_indices[k], axis=0)
            out = out + top_k_values[k] * _expert_ffn(hidden_states, wi_w, wo_w, A, Bm)
        return out
    x = x + _L0_xattn_ref(_layernorm(x, axis=-1), ctx_512, ctx_512, L0_xattn_Wq, L0_xattn_bq, L0_xattn_Wk, L0_xattn_bk, L0_xattn_Wv, L0_xattn_bv, L0_xattn_Wo, L0_xattn_bo)
    x = x + _L0_attn_ref(_layernorm(x, axis=-1), L0_attn_w_qkv)
    x = x + _L0_ffn_ref(_layernorm(x, axis=-1), L0_ffn_gate_w, L0_ffn_rms_w, L0_ffn_W1, L0_ffn_W2, L0_ffn_W3)
    x = x + _L1_xattn_ref(_layernorm(x, axis=-1), ctx_512, L1_xattn_Wq, L1_xattn_Wkv, L1_xattn_Wo)
    x = x + _L1_attn_ref(_layernorm(x, axis=-1), L1_attn_W_in, L1_attn_W_out, L1_attn_conv_w_fwd, L1_attn_conv_b_fwd, L1_attn_Wx_fwd, L1_attn_Wdt_fwd, L1_attn_bdt_fwd, L1_attn_A_log_fwd, L1_attn_D_fwd, L1_attn_conv_w_rev, L1_attn_conv_b_rev, L1_attn_Wx_rev, L1_attn_Wdt_rev, L1_attn_bdt_rev, L1_attn_A_log_rev, L1_attn_D_rev)
    x = x + _L1_ffn_ref(_layernorm(x, axis=-1), L1_ffn_wi_w, L1_ffn_wo_w, L1_ffn_lora_As, L1_ffn_lora_Bs, L1_ffn_top_k_indices, L1_ffn_top_k_values)
    return x

_drawn_inputs = setup_inputs


def setup_inputs(seed=0):
    import zlib

    import numpy as np

    out = dict(_drawn_inputs(seed))
    spreads = {'L0_xattn_bq': (0.0, 0.1),
     'L0_xattn_bk': (0.0, 0.1),
     'L0_xattn_bv': (0.0, 0.1),
     'L0_xattn_bo': (0.0, 0.1),
     'L0_ffn_rms_w': (1.0, 0.2),
     'L1_attn_conv_b_fwd': (0.0, 0.1),
     'L1_attn_bdt_fwd': (-4.599999904632568, 0.2),
     'L1_attn_D_fwd': (1.0, 0.2),
     'L1_attn_conv_b_rev': (0.0, 0.1),
     'L1_attn_bdt_rev': (-4.599999904632568, 0.2),
     'L1_attn_D_rev': (1.0, 0.2)}
    factors = {}
    for name, (base, spread) in spreads.items():
        noise = np.random.default_rng([zlib.crc32(name.encode()), seed]).standard_normal(out[name].shape)
        drawn = base * np.exp(spread * noise) if base else spread * noise
        out[name] = jnp.asarray(drawn.astype(out[name].dtype))
    for name, factor in factors.items():
        out[name] = (out[name] * factor).astype(out[name].dtype)
    return out
```

```python
import concourse.bass as bass
from concourse import mybir
from concourse.alu_op_type import AluOpType as ALU
from contextlib import ExitStack

F32 = mybir.dt.float32
F32R = mybir.dt.float32r
U32 = mybir.dt.uint32
I32 = mybir.dt.int32
ACT = mybir.ActivationFunctionType
AX = mybir.AxisListType
ds = bass.ds

P = 128
B, LQ, D = 32, 64, 256
LKV, DC = 1601, 128
H, DH = 16, 16
TOK = B * LQ
NT = TOK // P
KD = D // P
NB = 512
NBLK = TOK // NB
TPB = NB // P
LN_EPS, RMS_EPS = 1e-5, 1e-6

KT = -(-LKV // P)
KLAST = LKV - (KT - 1) * P
GROUPS = [6, 6, 4]
G0 = [0, 6, 12]
NG = len(GROUPS)
VW = 98
PAIRS = H // 2
WINDOWS = [(0, 512), (512, 512), (1024, 512), (LKV - 256, 256)]
NE, DE = 8, 704
FLT_MAX = 3.4028234663852886e38
SLOT_BLOCKS = (2 * TOK + NE * (P - 1)) // P
M_CONST_PARTS = [("rows_before", P), ("ones", P), ("experts", NE), ("tile_chain", NE * NT), ("whole_blocks", NT),
                 ("blocks", SLOT_BLOCKS)]
M_CONST = sum(n for _, n in M_CONST_PARTS)
EC = -(-DE // P)
ELAST = DE - (EC - 1) * P
DI, NS, KC, R = 512, 16, 4, 64
CI = DI // P
PADL = LQ + 2 * (KC - 1)
HALF = TOK // 2
FF, RANK = 1024, 16
CF = FF // P


def alloc(nc, ctx):
    def sb(name, shape, dt=F32):
        return ctx.enter_context(nc.sbuf_tensor(name, shape, dt))

    def ps(name, shape, dt=F32):
        return ctx.enter_context(nc.psum_tensor(name, shape, dt))

    def sem(name):
        s = ctx.enter_context(nc.semaphore(name))
        sem.taken.append(s)
        return s

    sem.taken = []
    return sb, ps, sem


def open_block(nc, ctx, sem):
    def clear():
        with nc.Block() as block:
            @block.sync
            def _(sp):
                for s in sem.taken:
                    sp.sem_clear(s)

    ctx.callback(clear)
    return ctx.enter_context(nc.Block())


def normed(nc, ctx, tag):
    return ctx.enter_context(nc.sbuf_tensor(f"{tag}_xnT", [P, KD, TOK + P], F32))


def layer_norm(nc, tag, x_sb, xnT, ident, rms=None, residual=False, rows=None):
    with ExitStack() as ctx:
        sb, ps, sem = alloc(nc, ctx)
        stats = sb(f"{tag}_stats", [P, NT, 6])
        moments = sb(f"{tag}_moments", [P, NT, 2])
        std = sb(f"{tag}_std", [P, NT])
        rstd = sb(f"{tag}_rstd", [P, NT])
        eps = sb(f"{tag}_eps", [P, 2])
        xn = sb(f"{tag}_xn", [P, 2, D])
        yn = sb(f"{tag}_yn", [P, 2, D])
        square = sb(f"{tag}_square", [P, D])
        sumsq = sb(f"{tag}_sumsq", [P, 2])
        rms_sb = sb(f"{tag}_rms", [P, 2, 2])
        xT = ps(f"{tag}_xT", [P, 2, NB])
        stats_done = sem(f"{tag}_stats_done")
        moments_done = sem(f"{tag}_moments_done")
        std_done = sem(f"{tag}_std_done")
        rstd_done = sem(f"{tag}_rstd_done")
        eps_done = sem(f"{tag}_eps_done")
        xn_done = sem(f"{tag}_xn_done")
        x_added = sem(f"{tag}_x_added")
        sum_done = sem(f"{tag}_sum_done")
        root_done = sem(f"{tag}_root_done")
        recip_done = sem(f"{tag}_recip_done")
        yn_done = sem(f"{tag}_yn_done")
        transposed = sem(f"{tag}_transposed")
        xT_free = sem(f"{tag}_xT_free")
        block = open_block(nc, ctx, sem)
        src = yn if rms is not None else xn
        src_done = yn_done if rms is not None else xn_done

        @block.vector
        def _(dve):
            nc.vector.memset(xnT[:, :, TOK:], 0.0)
            nc.vector.memset(eps[:, 0:1], LN_EPS)
            nc.vector.memset(eps[:, 1:2], RMS_EPS).then_inc(eps_done, 1)
            with dve.Fori(0, NT) as t:
                nc.vector.bn_stats(stats[:, ds(t, 1), :].rearrange("p a s -> p (a s)"),
                                   x_sb[:, ds(t, 1), :].rearrange("p a d -> p (a d)")).then_inc(stats_done, 1)
            dve.wait_ge(stats_done, NT)
            for t in range(NT):
                ins = nc.vector.bn_aggr(moments[:, t, :], stats[:, t, :])
            ins.then_inc(moments_done, 1)
            dve.wait_ge(std_done, 1)
            nc.vector.reciprocal(rstd[:, :], std[:, :]).then_inc(rstd_done, 1)
            dve.wait_ge(rstd_done, 1)
            with dve.Fori(0, NT // 2) as t2:
                for j in range(2):
                    t = t2 * 2 + j
                    x_t = x_sb[:, ds(t, 1), :].rearrange("p a d -> p (a d)")
                    if rms is None:
                        dve.wait_ge(transposed, t2 * 2 + 2)
                    nc.vector.tensor_scalar(xn[:, j, :], x_t, moments[:, ds(t, 1), 0:1].rearrange("p a s -> p (a s)"),
                                            rstd[:, ds(t, 1)], ALU.subtract, ALU.mult).then_inc(xn_done, 1)
                    if rms is not None:
                        dve.wait_ge(root_done, t2 * 2 + j + 2)
                        nc.vector.reciprocal(rms_sb[:, j, 1:2], rms_sb[:, j, 0:1]).then_inc(recip_done, 1)
                        dve.wait_ge(recip_done, t2 * 2 + j + 1)
                        dve.wait_ge(transposed, t2 * 2 + 2)
                        nc.vector.tensor_scalar(rows[:, ds(t, 1), :].rearrange("p a d -> p (a d)"), xn[:, j, :],
                                                rms_sb[:, j, 1:2], None, ALU.mult)
                        nc.vector.tensor_scalar(yn[:, j, :], xn[:, j, :], rms_sb[:, j, 1:2], None,
                                                ALU.mult).then_inc(yn_done, 1)
                    if residual:
                        dve.wait_ge(xn_done, t2 * 2 + j + 1)
                        nc.vector.tensor_tensor(x_t, x_t, xn[:, j, :], ALU.add).then_inc(x_added, 1)
                        dve.wait_ge(x_added, t2 * 2 + j + 1)

        @block.scalar
        def _(act):
            act.sem_inc(root_done, 1)
            act.sem_inc(yn_done, 2)
            act.wait_ge(eps_done, 1)
            act.wait_ge(moments_done, 1)
            nc.scalar.activation(std[:, :], moments[:, :, 1], ACT.Sqrt, bias=eps[:, 0:1]).then_inc(std_done, 1)
            if rms is not None:
                with act.Fori(0, NT // 2) as t2:
                    for j in range(2):
                        act.wait_ge(xn_done, t2 * 2 + j + 1)
                        act.wait_ge(root_done, t2 * 2 + j + 1)
                        act.wait_ge(yn_done, t2 * 2 + 2)
                        nc.scalar.activation(square[:, :], xn[:, j, :], ACT.Square,
                                             accum_out=sumsq[:, j:j + 1]).then_inc(sum_done, 1)
                        act.wait_ge(sum_done, t2 * 2 + j + 1)
                        nc.scalar.activation(rms_sb[:, j, 0:1], sumsq[:, j:j + 1], ACT.Sqrt, bias=eps[:, 1:2],
                                             scale=1.0 / D).then_inc(root_done, 1)
                        for_t = t2 * 2 + j
                        act.wait_ge(transposed, t2 * 2 + j + 3)
                        for c in range(KD):
                            ins = nc.scalar.activation(xnT[:, c, ds(for_t * P, P)], xT[:, j, c * P:(c + 1) * P],
                                                       ACT.Copy, scale=rms[:, c:c + 1])
                        ins.then_inc(xT_free, 1)
            else:
                with act.Fori(0, NT // 2) as t2:
                    for j in range(2):
                        t = t2 * 2 + j
                        act.wait_ge(transposed, t2 * 2 + j + 3)
                        nc.scalar.activation(xnT[:, :, ds(t * P, P)],
                                             xT[:, j, 0:KD * P].rearrange("p (c n) -> p c n", c=KD),
                                             ACT.Copy).then_inc(xT_free, 1)

        @block.tensor
        def _(pe):
            pe.sem_inc(transposed, 2)
            pe.sem_inc(xT_free, 2)
            with pe.Fori(0, NT // 2) as t2:
                for j in range(2):
                    pe.wait_ge(src_done, t2 * 2 + j + (3 if rms is not None else 1))
                    pe.wait_ge(xT_free, t2 * 2 + 2)
                    for c in range(KD):
                        ins = nc.tensor.transpose(xT[:, j, c * P:(c + 1) * P], src[:, j, c * P:(c + 1) * P],
                                                  ident[:, :])
                    ins.then_inc(transposed, 1)


def cross_attention(nc, tag, x_sb, ident, pair_mask, ctxT, wq, wk, wv, wo, bq, bv, bo):
    UN = 4
    PLAN = {}
    for u in range(UN):
        rows = [[("V", i)] for i in range(KT)] + [[]]
        if u % 2 == 0:
            rows[0] += [("Q", k) for k in range(4)]
        for m in range(PAIRS * len(WINDOWS)):
            rows[1 + m // 4].append(("M", m // 4, m % 4))
        rows[10] += [("T",)]
        if u > 0:
            rows[9] += [("X", g) for g in range(NG)]
            rows[10] += [("Y",)]
            rows[11] += [("Z",)]
        PLAN[u] = rows
    ROUND_END = [("X", g) for g in range(NG)] + [("Y",), ("Z",)]
    PROLOGUE = ([("J", c, n) for c in range(KD) for n in range(NBLK)] + [("Q", k) for k in range(4)]
                + [("M", p, w) for p in range(PAIRS) for w in range(len(WINDOWS))] + [("T",)])
    FIRST = {}
    n = len(PROLOGUE)
    for u in range(UN):
        FIRST[u] = n
        n += sum(len(r) for r in PLAN[u])
    END_FIRST = n
    ROUND = n + len(ROUND_END) - len(PROLOGUE)
    assert ROUND % 2 == 0 and B % UN == 0
    UNITS = KT * NG

    with ExitStack() as ctx:
        sb, ps, sem = alloc(nc, ctx)
        xnT = normed(nc, ctx, tag)
        layer_norm(nc, f"ln_{tag}", x_sb, xnT, ident)
        wq_sb = sb(f"{tag}_wq", [P, KD, D])
        wk_sb = sb(f"{tag}_wk", [P, H, DC])
        wv_sb = sb(f"{tag}_wv", [P, NG * VW])
        wv_hi = sb(f"{tag}_wv_hi", [P, NG * VW], F32R)
        wv_lo = sb(f"{tag}_wv_lo", [P, NG * VW], F32R)
        bv_sb = sb(f"{tag}_bv", [P, NG * VW])
        wo_sb = sb(f"{tag}_wo", [P, 2, D])
        bq_sb = sb(f"{tag}_bq", [P, KD])
        bo_sb = sb(f"{tag}_bo", [P, D])
        ones = sb(f"{tag}_ones", [PAIRS, P], F32R)
        qT = sb(f"{tag}_qT", [P, KD, TOK + 2 * LQ])
        q_hi = sb(f"{tag}_q_hi", [P, 2, 2, H, LQ], F32R)
        q_lo = sb(f"{tag}_q_lo", [P, 2, 2, H, LQ], F32R)
        raw = sb(f"{tag}_raw", [P, 2, LKV])
        c_hi = sb(f"{tag}_c_hi", [P, 2, LKV], F32R)
        c_lo = sb(f"{tag}_c_lo", [P, 2, LKV], F32R)
        maxes = sb(f"{tag}_maxes", [P, PAIRS, len(WINDOWS)])
        neg_max = sb(f"{tag}_neg_max", [P, PAIRS])
        shift = sb(f"{tag}_shift", [PAIRS, 2, PAIRS, P], F32R)
        v_sb = sb(f"{tag}_v", [P, 2, NG * VW])
        probs = sb(f"{tag}_probs", [P, 2, H * LQ])
        u_sb = sb(f"{tag}_u", [97, H * LQ])
        recip = sb(f"{tag}_recip", [P, PAIRS])
        o_sb = sb(f"{tag}_o", [P, PAIRS, DH])
        oT = sb(f"{tag}_oT", [P, P])
        score_ps = ps(f"{tag}_score_ps", [P, NG, NB])
        pv_ps = ps(f"{tag}_pv_ps", [P, NG, NB])
        misc_ps = ps(f"{tag}_misc_ps", [P, 2, NB])

        w_in = sem(f"{tag}_w_in")
        ctx_in = [sem(f"{tag}_ctx_in{j}") for j in range(2)]
        const_done = sem(f"{tag}_const_done")
        wv_hi_done = sem(f"{tag}_wv_hi_done")
        wv_done = sem(f"{tag}_wv_done")
        x_biased = sem(f"{tag}_x_biased")
        hi_done = sem(f"{tag}_hi_done")
        lo_done = sem(f"{tag}_lo_done")
        q_hi_done = sem(f"{tag}_q_hi_done")
        misc_ready = sem(f"{tag}_misc_ready")
        misc_free = sem(f"{tag}_misc_free")
        max_done = sem(f"{tag}_max_done")
        score_ready = sem(f"{tag}_score_ready")
        score_free = sem(f"{tag}_score_free")
        pv_done = sem(f"{tag}_pv_done")
        u_done = sem(f"{tag}_u_done")
        recip_done = sem(f"{tag}_recip_done")
        o_half = sem(f"{tag}_o_half")
        block = open_block(nc, ctx, sem)
        NW = 8 if bo is not None else 7

        def unit_cols(g):
            return slice(G0[g] * LQ, (G0[g] + GROUPS[g]) * LQ)

        def keys(i):
            return KLAST if i == KT - 1 else P

        @block.sync
        def _(sp):
            sp.dma_start(wq_sb[:, :, :], wq).then_inc(w_in, 16)
            sp.dma_start(wk_sb[:, :, :], wk).then_inc(w_in, 16)
            sp.dma_start(wv_sb[:, :], wv).then_inc(w_in, 16)
            sp.dma_start(bv_sb[:, :], bv.partition_broadcast(P)).then_inc(w_in, 16)
            sp.dma_start(wo_sb[:, :, :], wo).then_inc(w_in, 16)
            sp.dma_start(bq_sb[:, :], bq).then_inc(w_in, 16)
            if bo is not None:
                sp.dma_start(bo_sb[:, :], bo.partition_broadcast(P)).then_inc(w_in, 16)
            for j in range(2):
                sp.dma_start(raw[:, j, :], ctxT[j, :, :]).then_inc(ctx_in[j], 16)
            with sp.Fori(0, B // UN) as t:
                for u in range(UN):
                    sp.wait_ge(lo_done, t * UN + u + 1)
                    sp.dma_start(raw[:, u % 2, :],
                                 ctxT[ds(t * UN + u + 2, 1), :, :].rearrange("b p k -> p (b k)")
                                 ).then_inc(ctx_in[u % 2], 16)
            for j in range(2):
                sp.wait_ge(ctx_in[j], 16 * (B // 2 + 1))

        @block.tensor
        def _(pe):
            def small(op, u, n, b):
                bank = misc_ps[:, n % 2, :]
                nxt = (u + 1) % UN
                if op[0] == "J":
                    _, c, blk = op
                    for k in range(KD):
                        ins = nc.tensor.matmul(bank, wq_sb[:, k, c * P:(c + 1) * P],
                                               xnT[:, k, blk * NB:(blk + 1) * NB], start=k == 0, stop=k == KD - 1)
                elif op[0] == "Q":
                    for j in range(4):
                        h = 4 * op[1] + j
                        ins = nc.tensor.matmul(bank[:, j * P:(j + 1) * P], wk_sb[:, h, :],
                                               qT[:, h // 8, ds((b + 2) * LQ, P)],
                                               start=True, stop=True)
                elif op[0] == "V":
                    i = op[1]
                    for m, (a, w) in enumerate(((c_hi, wv_hi), (c_hi, wv_lo), (c_lo, wv_hi))):
                        ins = nc.tensor.matmul(bank[0:keys(i), 0:NG * VW], a[:, u % 2, i * P:i * P + keys(i)],
                                               w[:, :], start=m == 0, stop=m == 2)
                elif op[0] == "M":
                    _, p, w = op
                    k0, kn = WINDOWS[w]
                    q = q_hi[:, nxt // 2, nxt % 2, 2 * p:2 * p + 2, :].rearrange("p h q -> p (h q)")
                    ins = nc.tensor.matmul(bank[:, 0:kn], q, c_hi[:, nxt % 2, k0:k0 + kn], start=True, stop=True)
                elif op[0] == "T":
                    ins = nc.tensor.transpose(bank[0:PAIRS, 0:P], neg_max[:, :], ident[:, :])
                elif op[0] == "X":
                    g = op[1]
                    for k in range(GROUPS[g] // 2):
                        ins = nc.tensor.transpose(bank[:, k * VW:k * VW + 97],
                                                  u_sb[:, (G0[g] + 2 * k) * LQ:(G0[g] + 2 * k + 2) * LQ],
                                                  ident[0:97, 0:97])
                elif op[0] == "Y":
                    ins = nc.tensor.transpose(bank[:, 0:P], o_sb[:, :, :].rearrange("p a d -> p (a d)"), ident[:, :])
                elif op[0] == "Z":
                    half = (u - 1) % 2
                    for j in range(2):
                        ins = nc.tensor.matmul(bank[half * LQ:(half + 1) * LQ, 0:D], oT[:, j * LQ:(j + 1) * LQ],
                                               wo_sb[:, j, :], start=j == 0, stop=j == 1)
                ins.then_inc(misc_ready, 1)

            def small_waits(op, u, n, t, b):
                pe.wait_ge(misc_free, t * ROUND + n + 1)
                if op[0] == "Q":
                    pe.wait_ge(misc_free, t * ROUND + n + 1)
                elif op[0] == "M":
                    pe.wait_ge(hi_done, b + 2)
                elif op[0] == "T":
                    pe.wait_ge(max_done, b + 2)
                elif op[0] == "X":
                    pe.wait_ge(u_done, (b - 1) * NG + NG + op[1] + 1)
                elif op[0] in "YZ":
                    pe.wait_ge(misc_free, t * ROUND + n + 2)

            def do(op, u, n, t, b):
                small_waits(op, u, n, t, b)
                small(op, u, n, b)

            pe.sem_inc(score_ready, 1)
            pe.wait_ge(w_in, 16 * (NW - 1))
            pe.wait_ge(const_done, 1)
            for n, op in enumerate(PROLOGUE):
                if op == ("Q", 0):
                    pe.wait_ge(misc_free, n + 2)
                if op == ("M", 0, 0):
                    pe.wait_ge(misc_free, n + 2)
                do(op, -1, n, 0, -2 if op[0] == "Q" else -1)
            pe.wait_ge(wv_done, 1)
            with pe.Fori(0, B // UN) as t:
                for u in range(UN):
                    b = t * UN + u
                    n = FIRST[u]

                    def pv(i, g):
                        tile = KT * u + i
                        pe.wait_ge(score_free, b * UNITS + NG + i * NG + g + 1)
                        if i == 0:
                            pe.wait_ge(u_done, b * NG + g + 1)
                        if g == 0:
                            at = FIRST[u] + sum(len(r) for r in PLAN[u][:i])
                            pe.wait_ge(misc_free, t * ROUND + at + 3)
                        nc.tensor.matmul(pv_ps[0:97, g, 0:GROUPS[g] * LQ], v_sb[0:keys(i), tile % 2, g * VW:g * VW + 97],
                                         probs[0:keys(i), tile % 2, unit_cols(g)], start=i == 0, stop=i == KT - 1
                                         ).then_inc(pv_done, 1)

                    for i in range(KT):
                        slots = list(PLAN[u][i])
                        for g in range(NG):
                            if i == 0 and g == 0:
                                pe.wait_ge(hi_done, b + 1)
                                pe.wait_ge(lo_done, b + 1)
                                pe.wait_ge(misc_free, t * ROUND + n + 2)
                            pe.wait_ge(score_free, b * UNITS + i * NG + g + 1)
                            out = score_ps[0:keys(i), g, 0:GROUPS[g] * LQ]
                            cols = slice(i * P, i * P + keys(i))
                            heads = slice(G0[g], G0[g] + GROUPS[g])
                            for m, (a, q) in enumerate(((c_hi, q_hi), (c_hi, q_lo), (c_lo, q_hi))):
                                nc.tensor.matmul(out, a[:, u % 2, cols],
                                                 q[:, u // 2, u % 2, heads, :].rearrange("p h q -> p (h q)"),
                                                 start=m == 0, stop=False)
                            nc.tensor.matmul(out, ones[:, 0:keys(i)],
                                             shift[:, u % 2, :, :].rearrange("r a c -> r (a c)")[:, unit_cols(g)],
                                             start=False, stop=True).then_inc(score_ready, 1)
                            if slots:
                                do(slots.pop(0), u, n, t, b)
                                n += 1
                        for g in range(NG):
                            if i > 0:
                                pv(i - 1, g)
                            if slots:
                                do(slots.pop(0), u, n, t, b)
                                n += 1
                        assert not slots
                    for g in range(NG):
                        pv(KT - 1, g)
                for k, op in enumerate(ROUND_END):
                    do(op, UN, END_FIRST + k, t, t * UN + UN)

        @block.scalar
        def _(act):
            act.sem_inc(score_free, NG)
            act.sem_inc(u_done, NG)
            act.wait_ge(w_in, 16 * (NW - 1))
            nc.scalar.activation(wv_hi[:, :], wv_sb[:, :], ACT.Copy).then_inc(wv_hi_done, 1)

            def split(j, arrived):
                act.wait_ge(ctx_in[j], arrived)
                nc.scalar.activation(c_hi[:, j, :], raw[:, j, :], ACT.Copy).then_inc(hi_done, 1)

            def queries(k, s, n, t):
                act.wait_ge(misc_ready, t * ROUND + n + 1)
                nc.scalar.activation(
                    q_hi[:, s, :, 4 * k:4 * k + 4, :],
                    misc_ps[:, n % 2, :].rearrange("p (h s q) -> p s h q", h=4, s=2), ACT.Copy).then_inc(q_hi_done, 1)

            def out(b):
                for g in range(NG):
                    act.wait_ge(pv_done, b * UNITS + 2 * NG + UNITS - NG + g + 1)
                    nc.scalar.activation(u_sb[:, unit_cols(g)], pv_ps[0:97, g, 0:GROUPS[g] * LQ],
                                         ACT.Copy).then_inc(u_done, 1)

            split(0, 16)
            for n, op in enumerate(PROLOGUE):
                if op[0] == "Q":
                    queries(op[1], 0, n, 0)
            with act.Fori(0, B // UN) as t:
                for u in range(UN):
                    b = t * UN + u
                    if u > 0:
                        out(b - 1)
                    act.wait_ge(score_ready, b * UNITS + 1)
                    split((u + 1) % 2, (t * 2 + (u + 1) // 2) * 16 + 16)
                    n = FIRST[u]
                    for i in range(KT):
                        tile = KT * u + i
                        for g in range(NG):
                            act.wait_ge(score_ready, b * UNITS + i * NG + g + 2)
                            act.wait_ge(pv_done, b * UNITS + i * NG + g + 1)
                            nc.scalar.activation(probs[0:keys(i), tile % 2, unit_cols(g)],
                                                 score_ps[0:keys(i), g, 0:GROUPS[g] * LQ], ACT.Exp
                                                 ).then_inc(score_free, 1)
                        for op in PLAN[u][i]:
                            if op[0] == "Q":
                                queries(op[1], (u // 2 + 1) % 2, n, t)
                            n += 1
                out(t * UN + UN - 1)

        @block.vector
        def _(dve):
            dve.sem_inc(misc_free, 2)
            dve.sem_inc(pv_done, 2 * NG)
            nc.vector.memset(ones[:, :].bitcast(F32), 1.0)
            nc.vector.memset(qT[:, :, TOK:], 0.0).then_inc(const_done, 1)
            dve.wait_ge(w_in, 16 * (NW - 1))
            dve.wait_ge(wv_hi_done, 1)
            nc.vector.tensor_tensor(wv_lo[:, :], wv_sb[:, :], wv_hi[:, :].bitcast(F32), ALU.subtract
                                    ).then_inc(wv_done, 1)
            if bo is not None:
                nc.vector.tensor_tensor(x_sb[:, :, :], x_sb[:, :, :],
                                        bo_sb[:, :].rearrange("p (a d) -> p a d", a=1).broadcast_to([P, NT, D]),
                                        ALU.add).then_inc(x_biased, 1)
                dve.wait_ge(x_biased, 1)

            def lo(j, need):
                dve.wait_ge(hi_done, need)
                nc.vector.tensor_tensor(c_lo[:, j, :], raw[:, j, :], c_hi[:, j, :].bitcast(F32), ALU.subtract
                                        ).then_inc(lo_done, 1)

            def use(op, u, n, t, b):
                bank = misc_ps[:, n % 2, :]
                dve.wait_ge(misc_ready, t * ROUND + n + 1)
                if op[0] == "J":
                    _, c, blk = op
                    ins = nc.vector.tensor_scalar(qT[:, c, blk * NB:(blk + 1) * NB], bank, bq_sb[:, c:c + 1],
                                                  DH ** -0.5, ALU.add, ALU.mult)
                elif op[0] == "Q":
                    s = 0 if u < 0 else (u // 2 + 1) % 2
                    k = op[1]
                    if u < 0:
                        dve.wait_ge(q_hi_done, k + 1)
                    else:
                        dve.wait_ge(q_hi_done, t * 8 + 4 + (u // 2) * 4 + k + 1)
                    ins = nc.vector.tensor_tensor(q_lo[:, s, :, 4 * k:4 * k + 4, :],
                                                  bank.rearrange("p (h s q) -> p s h q", h=4, s=2),
                                                  q_hi[:, s, :, 4 * k:4 * k + 4, :].bitcast(F32), ALU.subtract)
                elif op[0] == "V":
                    i = op[1]
                    tile = KT * u + i
                    dve.wait_ge(pv_done, b * UNITS + i * NG + NG)
                    ins = nc.vector.tensor_tensor(v_sb[0:keys(i), tile % 2, :], bank[0:keys(i), 0:NG * VW],
                                                  bv_sb[0:keys(i), :], ALU.add)
                elif op[0] == "M":
                    _, p, w = op
                    ins = nc.vector.tensor_reduce(maxes[:, p, w:w + 1], bank[:, 0:WINDOWS[w][1]], AX.X, ALU.max)
                elif op[0] == "T":
                    ins = nc.vector.tensor_tensor(
                        shift[:, (u + 1) % 2, :, :],
                        bank[0:PAIRS, 0:P].rearrange("r (a c) -> r a c", a=1).broadcast_to([PAIRS, PAIRS, P]),
                        pair_mask[:, :].rearrange("r (a c) -> r a c", c=1).broadcast_to([PAIRS, PAIRS, P]), ALU.mult)
                elif op[0] == "X":
                    g = op[1]
                    k = GROUPS[g] // 2
                    p0 = G0[g] // 2
                    nc.vector.reciprocal(recip[:, p0:p0 + k],
                                         bank[:, 0:k * VW].rearrange("p (k s) -> p k s", s=VW)[:, :, 96]
                                         ).then_inc(recip_done, 1)
                    dve.wait_ge(recip_done, (b - 1) * NG + g + 1)
                    view = bank[:, 0:k * (VW + 2 * DH)].rearrange("p (k s) -> p k s", s=VW + 2 * DH)
                    for j in range(2):
                        rows = slice(j * LQ, (j + 1) * LQ)
                        ins = nc.vector.tensor_tensor(
                            o_sb[rows, p0:p0 + k, :], view[rows, :, j * DH:(j + 1) * DH],
                            recip[rows, p0:p0 + k].rearrange("p (k s) -> p k s", s=1).broadcast_to([LQ, k, DH]),
                            ALU.mult)
                elif op[0] == "Y":
                    ins = nc.vector.tensor_copy(oT[:, :], bank[:, 0:P])
                elif op[0] == "Z":
                    half = (u - 1) % 2
                    rows = slice(half * LQ, (half + 1) * LQ)
                    tile = t * (UN // 2) + (u - 1) // 2
                    x_t = x_sb[rows, ds(tile, 1), :].rearrange("p a d -> p (a d)")
                    ins = nc.vector.tensor_tensor(x_t, bank[rows, 0:D], x_t, ALU.add)
                ins.then_inc(misc_free, 1)
                if op[0] == "M" and (op[1], op[2]) == (PAIRS - 1, len(WINDOWS) - 1):
                    dve.wait_ge(misc_free, t * ROUND + n + 3)
                    nc.vector.tensor_reduce(neg_max[:, :], maxes[:, :, :], AX.X, ALU.max, negate=True
                                            ).then_inc(max_done, 1)

            lo(0, 1)
            for n, op in enumerate(PROLOGUE):
                use(op, -1, n, 0, -1)
            with dve.Fori(0, B // UN) as t:
                for u in range(UN):
                    b = t * UN + u
                    n = FIRST[u]
                    dve.wait_ge(score_ready, b * UNITS + 1)
                    lo((u + 1) % 2, b + 2)
                    for op in [op for row in PLAN[u] for op in row]:
                        use(op, u, n, t, b)
                        n += 1
                for k, op in enumerate(ROUND_END):
                    use(op, UN, END_FIRST + k, t, t * UN + UN)


def self_attention(nc, x_sb, ident, a):
    with ExitStack() as ctx:
        sb, ps, sem = alloc(nc, ctx)
        xnT = normed(nc, ctx, "s")
        layer_norm(nc, "ln_s", x_sb, xnT, ident)
        w_sb = sb("s_w", [P, KD, 3 * D])
        mask = sb("s_mask", [P, 8])
        xt = sb("s_xt", [P, 2, KD, P])
        qz = sb("s_qz", [P, 2, 2, 8, LQ])
        kT = sb("s_kT", [P, 2, KD, P])
        v_sb = sb("s_v", [P, 2, D])
        neg_max = sb("s_neg_max", [P, PAIRS])
        shifted = sb("s_shifted", [P, PAIRS, LQ])
        probs = sb("s_probs", [P, 2, PAIRS, P])
        pT = sb("s_pT", [P, PAIRS, P])
        total = sb("s_total", [P, 2, PAIRS])
        recip = sb("s_recip", [P, PAIRS])
        o_sb = sb("s_o", [P, H, DH])
        proj_ps = ps("s_proj_ps", [P, 2, NB])
        score_ps = ps("s_score_ps", [P, PAIRS, P])
        pT_ps = ps("s_pT_ps", [P, PAIRS, P])
        pv_ps = ps("s_pv_ps", [P, 2, 4 * P])
        w_in = sem("s_w_in")
        zeroed = sem("s_zeroed")
        xt_done = sem("s_xt_done")
        proj_done = sem("s_proj_done")
        kv_done = sem("s_kv_done")
        q_done = sem("s_q_done")
        score_done = sem("s_score_done")
        max_done = sem("s_max_done")
        shift_done = sem("s_shift_done")
        probs_done = sem("s_probs_done")
        sum_done = sem("s_sum_done")
        trans_done = sem("s_trans_done")
        pT_done = sem("s_pT_done")
        pv_done = sem("s_pv_done")
        recip_done = sem("s_recip_done")
        o_done = sem("s_o_done")
        x_done = sem("s_x_done")
        block = open_block(nc, ctx, sem)

        @block.sync
        def _(sp):
            sp.dma_start(w_sb[:, :, :], a["s_w"]).then_inc(w_in, 16)
            sp.dma_start(mask[:, :], a["s_mask"]).then_inc(w_in, 16)

        @block.gpsimd
        def _(pool):
            nc.gpsimd.memset(probs[:, :, :, :], 0.0).then_inc(zeroed, 1)

            def stage(tile, j, n):
                if n is not None:
                    pool.wait_ge(proj_done, n + 1)
                nc.gpsimd.tensor_copy(xt[:, j, :, :], xnT[:, :, tile]).then_inc(xt_done, 1)

            stage(slice(0, P), 0, None)
            with pool.Fori(0, NT // 2) as t:
                for j in range(2):
                    stage(ds((t * 2 + j + 1) * P, P), (j + 1) % 2, t * 2 + j)

        @block.tensor
        def _(pe):
            def project(j, n):
                pe.wait_ge(xt_done, n)
                pe.wait_ge(q_done, (n - 1) * 2)
                pe.wait_ge(kv_done, n - 1)
                for c in range(2 * KD):
                    for k in range(KD):
                        nc.tensor.matmul(proj_ps[:, 0, c * P:(c + 1) * P], w_sb[:, k, c * P:(c + 1) * P],
                                         xt[:, j, k, :], start=k == 0, stop=k == KD - 1)
                for k in range(KD):
                    ins = nc.tensor.matmul(proj_ps[:, 1, 0:D], xt[:, j, k, :], w_sb[:, k, 2 * D:3 * D],
                                           start=k == 0, stop=k == KD - 1)
                ins.then_inc(proj_done, 1)

            def scores(s, j, n):
                pe.wait_ge(q_done, n)
                pe.wait_ge(shift_done, n - 1)
                for p in range(PAIRS):
                    c, r = p // 4, 2 * (p % 4)
                    ins = nc.tensor.matmul(score_ps[:, p, :],
                                           qz[:, s, c, r:r + 2, :].rearrange("p h q -> p (h q)"),
                                           kT[:, j, c, :], start=True, stop=True)
                ins.then_inc(score_done, 1)

            pe.sem_inc(proj_done, 1)
            pe.sem_inc(pv_done, 1)
            pe.sem_inc(pT_done, 1)
            pe.sem_inc(o_done, 2)
            pe.wait_ge(w_in, 32)
            project(0, 1)
            pe.wait_ge(kv_done, 1)
            scores(0, 0, 1)
            with pe.Fori(0, NT // 2) as t:
                for j in range(2):
                    for s in range(2):
                        b = t * 4 + j * 2 + s
                        pe.wait_ge(probs_done, b + 1)
                        pe.wait_ge(pT_done, b + 1)
                        for p in range(PAIRS):
                            ins = nc.tensor.transpose(pT_ps[:, p, :], probs[:, s, p, :], ident[:, :])
                        ins.then_inc(trans_done, 1)
                        if s == 0:
                            scores(1, j, b + 2)
                            project((j + 1) % 2, t * 2 + j + 2)
                        else:
                            pe.wait_ge(kv_done, t * 2 + j + 2)
                            scores(0, (j + 1) % 2, b + 2)
                        pe.wait_ge(pT_done, b + 2)
                        pe.wait_ge(o_done, b * 2 + 2)
                        for p in range(PAIRS):
                            c = p // 4
                            ins = nc.tensor.matmul(pv_ps[:, c, (p % 4) * P:(p % 4 + 1) * P], pT[:, p, :],
                                                   v_sb[:, j, c * P:(c + 1) * P], start=True, stop=True)
                        ins.then_inc(pv_done, 1)

        @block.scalar
        def _(act):
            def keys_values(j, n):
                act.wait_ge(proj_done, n + 1)
                nc.scalar.activation(kT[:, j, :, :].rearrange("p c n -> p (c n)"), proj_ps[:, 0, D:2 * D], ACT.Copy)
                nc.scalar.activation(v_sb[:, j, :], proj_ps[:, 1, 0:D], ACT.Copy).then_inc(kv_done, 1)

            def exps(s, n):
                act.wait_ge(shift_done, n)
                act.wait_ge(trans_done, n - 1)
                act.wait_ge(sum_done, n - 1)
                nc.scalar.activation(probs[:, s, :, s * LQ:(s + 1) * LQ], shifted[:, :, :], ACT.Exp
                                     ).then_inc(probs_done, 1)

            act.wait_ge(zeroed, 1)
            keys_values(0, 1)
            exps(0, 1)
            with act.Fori(0, NT // 2) as t:
                for j in range(2):
                    for s in range(2):
                        b = t * 4 + j * 2 + s
                        act.wait_ge(trans_done, b + 1)
                        act.wait_ge(pv_done, b + 1)
                        nc.scalar.activation(pT[:, :, :], pT_ps[:, :, :], ACT.Copy).then_inc(pT_done, 1)
                        if s == 0:
                            exps(1, b + 2)
                            keys_values((j + 1) % 2, t * 2 + j + 2)
                        else:
                            exps(0, b + 2)

        @block.vector
        def _(dve):
            def queries(s, n):
                for c in range(KD):
                    ins = nc.vector.tensor_tensor(
                        qz[:, s, c, :, :],
                        proj_ps[:, 0, c * P + s * LQ:c * P + (s + 1) * LQ].rearrange("p (h q) -> p h q", h=1)
                        .broadcast_to([P, 8, LQ]),
                        mask[:, :].rearrange("p (h q) -> p h q", q=1).broadcast_to([P, 8, LQ]), ALU.mult)
                ins.then_inc(q_done, 1)

            def shift(s, n):
                dve.wait_ge(score_done, n)
                own = score_ps[:, :, s * LQ:(s + 1) * LQ]
                nc.vector.tensor_reduce(neg_max[:, :], own, AX.X, ALU.max).then_inc(max_done, 1)
                dve.wait_ge(max_done, n)
                dve.wait_ge(probs_done, n - 1)
                nc.vector.tensor_tensor(shifted[:, :, :], own,
                                        neg_max[:, :].rearrange("p (a q) -> p a q", q=1).broadcast_to([P, PAIRS, LQ]),
                                        ALU.subtract).then_inc(shift_done, 1)

            def sums(s, n):
                dve.wait_ge(probs_done, n)
                nc.vector.tensor_reduce(total[:, s, :], probs[:, s, :, s * LQ:(s + 1) * LQ], AX.X, ALU.add
                                        ).then_inc(sum_done, 1)

            dve.sem_inc(x_done, 1)
            dve.wait_ge(w_in, 32)
            dve.wait_ge(kv_done, 1)
            queries(0, 1)
            queries(1, 2)
            shift(0, 1)
            with dve.Fori(0, NT // 2) as t:
                for j in range(2):
                    for s in range(2):
                        b = t * 4 + j * 2 + s
                        sums(s, b + 1)
                        shift((s + 1) % 2, b + 2)
                        if s == 0:
                            dve.wait_ge(kv_done, t * 2 + j + 2)
                            queries(0, b + 3)
                            queries(1, b + 4)
                        dve.wait_ge(sum_done, b + 1)
                        nc.vector.reciprocal(recip[:, :], total[:, s, :]).then_inc(recip_done, 1)
                        dve.wait_ge(recip_done, b + 1)
                        dve.wait_ge(pv_done, b + 2)
                        dve.wait_ge(x_done, b + 1)
                        for half in range(2):
                            rows = slice(half * LQ, (half + 1) * LQ)
                            for c in range(KD):
                                base = half * DH
                                for p in range(4):
                                    col = p * (P + 2 * DH) + base
                                    q = 4 * c + p
                                    ins = nc.vector.tensor_scalar(
                                        o_sb[s * LQ:(s + 1) * LQ, 2 * q + half, :], pv_ps[rows, c, col:col + DH],
                                        recip[rows, q:q + 1], None, ALU.mult)
                            ins.then_inc(o_done, 1)
                        dve.wait_ge(o_done, b * 2 + 4)
                        rows = slice(s * LQ, (s + 1) * LQ)
                        x_t = x_sb[rows, ds(t * 2 + j, 1), :].rearrange("p a d -> p (a d)")
                        nc.vector.tensor_tensor(x_t, x_t, o_sb[rows, :, :].rearrange("p h d -> p (h d)"), ALU.add
                                                ).then_inc(x_done, 1)


def experts(nc, x_sb, ident, a):
    with ExitStack() as ctx:
        sb, ps, sem = alloc(nc, ctx)
        w1 = sb("m_w1", [P, NE, KD, DE])
        w2 = sb("m_w2", [P, NE, KD, DE])
        w3 = sb("m_w3", [P, NE, EC, D])
        rms_w = sb("m_rms_w", [P, KD])
        prob = sb("m_prob", [P, 2, NT])
        slot = sb("m_slot", [P, 2, NT], U32)
        block_expert = sb("m_block_expert", [P, SLOT_BLOCKS], I32)
        slot_rows = nc.dram_tensor("m_slot_rows", (SLOT_BLOCKS * P, D), F32, kind="Internal").ap()
        slot_out = nc.dram_tensor("m_slot_out", (SLOT_BLOCKS * P, D), F32, kind="Internal").ap()
        rms_in = sem("m_rms_in")
        w_in = sem("m_w_in")
        zeroed = sem("m_zeroed")
        zero_out = sem("m_zero_out")
        scattered = sem("m_scattered")
        stored = [sem(f"m_stored{j}") for j in range(2)]
        with ExitStack() as inner:
            route(nc, inner, x_sb, ident, a, w1, w2, w3, rms_w, prob, slot, block_expert, slot_rows,
                  rms_in, w_in, zeroed, zero_out, scattered)
        with ExitStack() as inner:
            expert_blocks(nc, inner, ident, w1, w2, w3, rms_w, block_expert, slot_rows, slot_out,
                          w_in, scattered, stored)
        sb, ps, inner_sem = alloc(nc, ctx)
        back = sb("m_back", [P, NT, 2, D])
        GROUP = 4
        gathered = [sem(f"m_gathered{g}") for g in range(NT // GROUP)]
        first_added = sem("m_first_added")
        block = open_block(nc, ctx, sem)

        @block.gpsimd
        def _(pool):
            for j in range(2):
                pool.wait_ge(stored[j], 16 * ((SLOT_BLOCKS + 1 - j) // 2))
            for t in range(NT):
                for i in range(2):
                    nc.gpsimd.indirect_dma_start(back[:, t, i, :], None, slot_out,
                                                 bass.IndirectOffsetOnAxis(ap=slot[:, i, t:t + 1], axis=0)
                                                 ).then_inc(gathered[t // GROUP], 16)

        @block.vector
        def _(dve):
            for t in range(NT):
                if t % GROUP == 0:
                    dve.wait_ge(gathered[t // GROUP], 16 * 2 * GROUP)
                nc.vector.scalar_tensor_tensor(x_sb[:, t, :], back[:, t, 0, :], prob[:, 0, t:t + 1], x_sb[:, t, :],
                                               ALU.mult, ALU.add).then_inc(first_added, 1)
                if t > 0:
                    dve.wait_ge(first_added, t)
                    nc.vector.scalar_tensor_tensor(x_sb[:, t - 1, :], back[:, t - 1, 1, :], prob[:, 1, t - 1:t],
                                                   x_sb[:, t - 1, :], ALU.mult, ALU.add)
            dve.wait_ge(first_added, NT)
            nc.vector.scalar_tensor_tensor(x_sb[:, NT - 1, :], back[:, NT - 1, 1, :], prob[:, 1, NT - 1:NT],
                                           x_sb[:, NT - 1, :], ALU.mult, ALU.add)


def route(nc, ctx, x_sb, ident, a, w1, w2, w3, rms_w, prob, slot, block_expert, slot_rows,
          rms_in, w_in, zeroed, zero_out, scattered):
    sb, ps, sem = alloc(nc, ctx)
    xnT = normed(nc, ctx, "m")
    rows = sb("m_rows", [P, NT, D])
    zero = sb("m_zero", [P, D])
    gate_w = sb("m_gate_w", [P, KD, NE])
    const = sb("m_const", [P, M_CONST])
    cols = {}
    at = 0
    for name, n in M_CONST_PARTS:
        cols[name] = const[:, at:at + n]
        at += n
    c_in = sem("m_c_in")
    with nc.Block() as block:
        @block.vector
        def _(dve):
            nc.vector.memset(zero[:, :], 0.0).then_inc(zeroed, 1)

        @block.sync
        def _(sp):
            sp.dma_start(rms_w[:, :], a["m_rms_w"]).then_inc(rms_in, 16)
            sp.dma_start(gate_w[:, :, :], a["m_gate_w"]).then_inc(c_in, 16)
            sp.dma_start(const[:, :], a["m_const"]).then_inc(c_in, 16)
            sp.wait_ge(zeroed, 1)
            sp.dma_start(slot_rows.rearrange("(b p) d -> p b d", p=P),
                         zero[:, :].rearrange("p (b d) -> p b d", b=1).broadcast_to([P, SLOT_BLOCKS, D])
                         ).then_inc(zero_out, 16)
            for e in range(NE):
                for dst, src in ((w1, a["m_w1"]), (w2, a["m_w2"]), (w3, a["m_w3"])):
                    sp.dma_start(dst[:, e, :, :], src[e, :, :, :]).then_inc(w_in, 16)
            sp.wait_ge(rms_in, 16)
            sp.wait_ge(c_in, 32)
    layer_norm(nc, "ln_m", x_sb, xnT, ident, rms=rms_w, residual=True, rows=rows)

    logits = sb("m_logits", [P, NT, NE])
    top = sb("m_top", [P, 2, NT])
    best_at = sb("m_best_at", [P, 2, NT])
    first = sb("m_first", [P, NT, NE])
    second = sb("m_second", [P, NT, NE])
    cand = sb("m_cand", [P, NT, NE])
    gap = sb("m_gap", [P, NT])
    expo = sb("m_expo", [P, NT])
    denom = sb("m_denom", [P, NT])
    both = sb("m_both", [P, NE, NT])
    upto = sb("m_upto", [P, NE, NT])
    before = sb("m_before", [P, NE, NT])
    count = sb("m_count", [P, NE])
    over = sb("m_over", [P, NE, NT])
    blocks = sb("m_blocks", [P, NE])
    block_end = sb("m_block_end", [P, NE])
    base = sb("m_base", [P, NE])
    place = sb("m_place", [P, NE, NT])
    mine = sb("m_mine", [P, 2, NE, NT])
    slot_f = sb("m_slot_f", [P, 2, NT])
    ended = sb("m_ended", [P, SLOT_BLOCKS, NE])
    expert_f = sb("m_expert_f", [P, SLOT_BLOCKS])
    gate_ps = ps("m_gate_ps", [P, NB])
    prefix_ps = ps("m_prefix_ps", [P, NB])
    count_ps = ps("m_count_ps", [P, NB])
    logits_done = sem("m_logits_done")
    gap_done = sem("m_gap_done")
    e_done = sem("m_e_done")
    before_done = sem("m_before_done")
    prefix_done = sem("m_prefix_done")
    slot_done = sem("m_slot_done")
    seq = sem("m_seq")
    block = open_block(nc, ctx, sem)

    @block.tensor
    def _(pe):
        for t in range(NT):
            for k in range(KD):
                ins = nc.tensor.matmul(gate_ps[:, t * NE:(t + 1) * NE], xnT[:, k, t * P:(t + 1) * P],
                                       gate_w[:, k, :], start=k == 0, stop=k == KD - 1)
        ins.then_inc(logits_done, 1)
        pe.wait_ge(before_done, 1)
        nc.tensor.matmul(prefix_ps[:, 0:NE * NT], cols["rows_before"], both[:, :, :].rearrange("p e t -> p (e t)"),
                         start=True, stop=False)
        nc.tensor.matmul(prefix_ps[:, 0:NE * NT], cols["ones"], before[:, :, :].rearrange("p e t -> p (e t)"),
                         start=False, stop=True)
        nc.tensor.matmul(count_ps[:, 0:NE], cols["ones"], upto[:, :, NT - 1], start=True, stop=True
                         ).then_inc(prefix_done, 1)

    @block.scalar
    def _(act):
        act.wait_ge(gap_done, 1)
        nc.scalar.activation(expo[:, :], gap[:, :], ACT.Exp).then_inc(e_done, 1)

    @block.vector
    def _(dve):
        n = 0

        def link(ins):
            nonlocal n
            n += 1
            ins.then_inc(seq, 1)
            dve.wait_ge(seq, n)

        def over_experts(v):
            return v.rearrange("p (t e) -> p t e", e=1).broadcast_to([P, NT, NE])

        def over_tiles(v):
            return v.rearrange("p (e t) -> p e t", t=1).broadcast_to([P, NE, NT])

        def best(values, i, hot):
            link(nc.vector.tensor_reduce(top[:, i, :], values[:, :, :], AX.X, ALU.max))
            link(nc.vector.tensor_tensor(cand[:, :, :], values[:, :, :], over_experts(top[:, i, :]), ALU.is_equal))
            link(nc.vector.tensor_tensor(cand[:, :, :], cand[:, :, :], experts_all, ALU.mult))
            link(nc.vector.tensor_reduce(best_at[:, i, :], cand[:, :, :], AX.X, ALU.min))
            link(nc.vector.tensor_tensor(hot[:, :, :], experts_all, over_experts(best_at[:, i, :]), ALU.is_equal))

        experts_all = cols["experts"].rearrange("p (t e) -> p t e", t=1).broadcast_to([P, NT, NE])
        dve.wait_ge(logits_done, 1)
        link(nc.vector.tensor_copy(logits[:, :, :].rearrange("p t e -> p (t e)"), gate_ps[:, 0:NT * NE]))
        best(logits, 0, first)
        link(nc.vector.scalar_tensor_tensor(logits[:, :, :], first[:, :, :], -FLT_MAX, logits[:, :, :],
                                            ALU.mult, ALU.add))
        best(logits, 1, second)
        nc.vector.tensor_tensor(gap[:, :], top[:, 1, :], top[:, 0, :], ALU.subtract).then_inc(gap_done, 1)
        link(nc.vector.tensor_tensor(both[:, :, :].rearrange("p e t -> p t e"), first[:, :, :], second[:, :, :], ALU.add))
        link(nc.vector.tensor_tensor_scan(upto[:, :, :].rearrange("p e t -> p (e t)"), cols["tile_chain"],
                                          both[:, :, :].rearrange("p e t -> p (e t)"), 0.0, ALU.mult, ALU.add))
        nc.vector.tensor_tensor(before[:, :, :], upto[:, :, :], both[:, :, :], ALU.subtract).then_inc(before_done, 1)
        dve.wait_ge(e_done, 1)
        link(nc.vector.tensor_scalar(denom[:, :], expo[:, :], 1.0, None, ALU.add))
        link(nc.vector.reciprocal(prob[:, 0, :], denom[:, :]))
        link(nc.vector.tensor_tensor(prob[:, 1, :], expo[:, :], prob[:, 0, :], ALU.mult))
        dve.wait_ge(prefix_done, 1)
        link(nc.vector.tensor_copy(count[:, :], count_ps[:, 0:NE]))
        link(nc.vector.tensor_tensor(over[:, :, :], over_tiles(count[:, :]),
                                     cols["whole_blocks"].rearrange("p (e t) -> p e t", e=1).broadcast_to([P, NE, NT]),
                                     ALU.is_gt))
        link(nc.vector.tensor_reduce(blocks[:, :], over[:, :, :], AX.X, ALU.add))
        link(nc.vector.tensor_tensor_scan(block_end[:, :], cols["ones"][:, 0:NE], blocks[:, :], 0.0, ALU.mult, ALU.add))
        link(nc.vector.tensor_tensor(base[:, :], block_end[:, :], blocks[:, :], ALU.subtract))
        link(nc.vector.tensor_scalar(base[:, :], base[:, :], float(P), None, ALU.mult))
        link(nc.vector.tensor_tensor(place[:, :, :], prefix_ps[:, 0:NE * NT].rearrange("p (e t) -> p e t", e=NE),
                                     over_tiles(base[:, :]), ALU.add))
        for i, hot in enumerate((first, second)):
            link(nc.vector.tensor_tensor(mine[:, i, :, :], place[:, :, :], hot[:, :, :].rearrange("p t e -> p e t"),
                                         ALU.mult))
            link(nc.vector.tensor_reduce(slot_f[:, i, :], mine[:, i, :, :].rearrange("p e t -> p t e"), AX.X, ALU.add))
        nc.vector.tensor_copy(slot[:, :, :], slot_f[:, :, :]).then_inc(slot_done, 1)
        link(nc.vector.tensor_tensor(
            ended[:, :, :], block_end[:, :].rearrange("p (b e) -> p b e", b=1).broadcast_to([P, SLOT_BLOCKS, NE]),
            cols["blocks"].rearrange("p (b e) -> p b e", e=1).broadcast_to([P, SLOT_BLOCKS, NE]), ALU.is_le))
        link(nc.vector.tensor_reduce(expert_f[:, :], ended[:, :, :], AX.X, ALU.add))
        link(nc.vector.tensor_scalar(expert_f[:, :], expert_f[:, :], float(NE - 1), None, ALU.min))
        nc.vector.tensor_copy(block_expert[:, :], expert_f[:, :])

    @block.gpsimd
    def _(pool):
        pool.wait_ge(zero_out, 16)
        pool.wait_ge(slot_done, 1)
        for t in range(NT):
            for i in range(2):
                nc.gpsimd.indirect_dma_start(slot_rows, bass.IndirectOffsetOnAxis(ap=slot[:, i, t:t + 1], axis=0),
                                             rows[:, t, :], None).then_inc(scattered, 16)
        pool.wait_ge(scattered, 16 * 2 * NT)


def expert_blocks(nc, ctx, ident, w1, w2, w3, rms_w, block_expert, slot_rows, slot_out, w_in, scattered, stored):
    sb, ps, sem = alloc(nc, ctx)
    HN = DE // 2
    rows = sb("m_block_rows", [P, 2, D])
    yT = sb("m_yT", [P, 2, KD, P])
    gate = sb("m_gate", [P, 2, HN])
    h = sb("m_h", [P, 2, HN])
    hT = sb("m_hT", [P, EC, P])
    out = sb("m_out", [P, 2, D])
    yT_ps = ps("m_yT_ps", [P, NB])
    up_ps = ps("m_up_ps", [P, 2, NB])
    mul_ps = ps("m_mul_ps", [P, 2, NB])
    hT_ps = ps("m_hT_ps", [P, 2, NB])
    out_ps = ps("m_out_ps", [P, NB])
    rows_in = [sem(f"m_rows_in{j}") for j in range(2)]
    rows_turned = sem("m_rows_turned")
    yT_done = sem("m_yT_done")
    up_done = sem("m_up_done")
    gate_done = sem("m_gate_done")
    h_done = sem("m_h_done")
    h_turned = sem("m_h_turned")
    hT_done = sem("m_hT_done")
    out_made = sem("m_out_made")
    out_done = sem("m_out_done")
    block = open_block(nc, ctx, sem)
    LAST = SLOT_BLOCKS - 1
    LOOPED = (SLOT_BLOCKS - 2) // 2
    CB = NB // P

    def steps(engine, step):
        for b in range(2):
            step(0, b, b)
        with engine.Fori(1, LOOPED) as pair:
            for j in range(2):
                step(pair, j, None)
        for b in range(2 * LOOPED, SLOT_BLOCKS):
            step(b // 2, b % 2, b)

    def exists(b, ahead):
        return b is None or b + ahead <= LAST

    @block.sync
    def _(sp):
        def load(first, j):
            sp.dma_start(rows[:, j, :], slot_rows.rearrange("(b p) d -> b p d", p=P)[ds(first + j, 1), :, :]
                         .rearrange("b p d -> p (b d)")).then_inc(rows_in[j], 16)

        def step(pair, j, b):
            n = pair * 2 + j
            if exists(b, 2):
                sp.wait_ge(rows_turned, n + 1)
                load(pair * 2 + 2, j)
            sp.wait_ge(out_done, n + 1)
            sp.dma_start(slot_out.rearrange("(b p) d -> b p d", p=P)[ds(n, 1), :, :].rearrange("b p d -> p (b d)"),
                         out[:, j, :]).then_inc(stored[j], 16)

        for j in range(2):
            load(0, j)
        steps(sp, step)

    @block.tensor
    def _(pe):
        def turn_rows(pair, j):
            n = pair * 2 + j
            pe.wait_ge(rows_in[j], pair * 16 + 16)
            pe.wait_ge(yT_done, n)
            for c in range(KD):
                ins = nc.tensor.transpose(yT_ps[:, c * P:(c + 1) * P], rows[:, j, c * P:(c + 1) * P], ident[:, :])
            ins.then_inc(rows_turned, 1)

        def products(pair, j):
            n = pair * 2 + j
            e = pe.value_load(block_expert[0:1, ds(n, 1)], min_val=0, max_val=NE - 1)
            pe.wait_ge(yT_done, n + 1)
            pe.wait_ge(h_done, n)
            for dst, w in ((up_ps, w1), (mul_ps, w2)):
                for half in range(2):
                    for k in range(KD):
                        ins = nc.tensor.matmul(
                            dst[:, half, 0:HN], yT[:, j, k, :],
                            w[:, ds(e, 1), k, half * HN:(half + 1) * HN].rearrange("p e n -> p (e n)"),
                            start=k == 0, stop=k == KD - 1)
            ins.then_inc(up_done, 1)

        def step(pair, j, b):
            n = pair * 2 + j
            pe.wait_ge(h_done, n + 1)
            pe.wait_ge(hT_done, n * 2)
            for c in range(EC):
                m = ELAST if c == EC - 1 else P
                ins = nc.tensor.transpose(hT_ps[0:m, c // CB, c % CB * P:(c % CB + 1) * P],
                                          h[:, :, :].rearrange("p a n -> p (a n)")[:, c * P:c * P + m], ident[:, :])
                if c in (CB - 1, EC - 1):
                    ins.then_inc(h_turned, 1)
            if exists(b, 1):
                products(pair + (1 if j else 0), 1 - j)
            if exists(b, 2):
                turn_rows(pair + 1, j)
            e = pe.value_load(block_expert[0:1, ds(n, 1)], min_val=0, max_val=NE - 1)
            pe.wait_ge(hT_done, n * 2 + 2)
            pe.wait_ge(out_done, n)
            for c in range(EC):
                m = ELAST if c == EC - 1 else P
                ins = nc.tensor.matmul(out_ps[:, 0:D], hT[0:m, c, :],
                                       w3[0:m, ds(e, 1), c, :].rearrange("p e n -> p (e n)"),
                                       start=c == 0, stop=c == EC - 1)
            ins.then_inc(out_made, 1)

        turn_rows(0, 0)
        turn_rows(0, 1)
        pe.wait_ge(w_in, 16 * 3 * NE)
        products(0, 0)
        steps(pe, step)

    @block.scalar
    def _(act):
        def take_rows(n, j):
            act.wait_ge(rows_turned, n + 1)
            for c in range(KD):
                ins = nc.scalar.activation(yT[:, j, c, :], yT_ps[:, c * P:(c + 1) * P], ACT.Copy, scale=rms_w[:, c:c + 1])
            ins.then_inc(yT_done, 1)

        def silu(n):
            act.wait_ge(up_done, n + 1)
            act.wait_ge(h_done, n)
            nc.scalar.activation(gate[:, :, :], up_ps[:, :, 0:HN], ACT.Silu).then_inc(gate_done, 1)

        def step(pair, j, b):
            n = pair * 2 + j
            act.wait_ge(h_turned, n * 2 + 1)
            act.wait_ge(out_made, n)
            nc.scalar.activation(hT[:, 0:CB, :].rearrange("p c n -> p (c n)"), hT_ps[:, 0, :], ACT.Copy
                                 ).then_inc(hT_done, 1)
            if exists(b, 1):
                silu(n + 1)
            if exists(b, 2):
                take_rows(n + 2, j)

        take_rows(0, 0)
        take_rows(1, 1)
        silu(0)
        steps(act, step)

    @block.vector
    def _(dve):
        def hidden(n):
            dve.wait_ge(gate_done, n + 1)
            dve.wait_ge(h_turned, n * 2)
            nc.vector.tensor_tensor(h[:, :, :], mul_ps[:, :, 0:HN], gate[:, :, :], ALU.mult).then_inc(h_done, 1)

        def step(pair, j, b):
            n = pair * 2 + j
            dve.wait_ge(h_turned, n * 2 + 2)
            dve.wait_ge(out_made, n)
            nc.vector.tensor_copy(hT[:, CB, :], hT_ps[:, 1, 0:P])
            nc.vector.tensor_copy(hT[0:ELAST, CB + 1, :], hT_ps[0:ELAST, 1, P:2 * P]).then_inc(hT_done, 1)
            if exists(b, 1):
                hidden(n + 1)
            dve.wait_ge(out_made, n + 1)
            if b is None or b > 1:
                dve.wait_ge(stored[j], pair * 16)
            nc.vector.tensor_copy(out[:, j, :], out_ps[:, 0:D]).then_inc(out_done, 1)

        hidden(0)
        steps(dve, step)


def mamba(nc, x_sb, ident, a):
    SEQ = B // 2
    HB = HALF // NB
    with ExitStack() as ctx:
        sb, ps, sem = alloc(nc, ctx)
        xpad = sb("b_xpad", [P, CI, B, PADL])
        zs = sb("b_zs", [P, CI, TOK])
        with ExitStack() as inner:
            sb, ps, sem = alloc(nc, inner)
            xnT = normed(nc, inner, "b")
            layer_norm(nc, "ln_b", x_sb, xnT, ident)
            win = sb("b_win", [P, KD, 2 * DI])
            xz_ps = ps("b_xz_ps", [P, 2, 2, NB])
            w_in = sem("b_win_in")
            zeroed = sem("b_zeroed")
            x_done = sem("b_x_done")
            z_done = sem("b_z_done")
            x_free = sem("b_x_free")
            z_free = sem("b_z_free")
            block = open_block(nc, inner, sem)
            seq_blk = NB // LQ

            @block.sync
            def _(sp):
                sp.dma_start(win[:, :, :], a["b_win"]).then_inc(w_in, 16)

            @block.vector
            def _(dve):
                nc.vector.memset(xpad[:, :, :, 0:KC - 1], 0.0)
                nc.vector.memset(xpad[:, :, :, KC - 1 + LQ:], 0.0).then_inc(zeroed, 1)
                for c in range(CI):
                    with dve.Fori(0, NBLK // 2) as pair:
                        for j in range(2):
                            blk = pair * 2 + j
                            dve.wait_ge(x_done, pair * 2 + c * NBLK + j + 1)
                            nc.vector.tensor_copy(xpad[:, c, ds(blk * seq_blk, seq_blk), KC - 1:KC - 1 + LQ],
                                                  xz_ps[:, j, 0, :].rearrange("p (s l) -> p s l", l=LQ)
                                                  ).then_inc(x_free, 1)

            @block.scalar
            def _(act):
                for c in range(CI):
                    with act.Fori(0, NBLK // 2) as pair:
                        for j in range(2):
                            act.wait_ge(z_done, pair * 2 + c * NBLK + j + 1)
                            nc.scalar.activation(zs[:, c, ds((pair * 2 + j) * NB, NB)], xz_ps[:, j, 1, :], ACT.Silu
                                                 ).then_inc(z_free, 1)

            @block.tensor
            def _(pe):
                pe.wait_ge(w_in, 16)
                pe.sem_inc(x_free, 2)
                pe.sem_inc(z_free, 2)
                for c in range(CI):
                    with pe.Fori(0, NBLK // 2) as pair:
                        for j in range(2):
                            for i, (free, done) in enumerate(((x_free, x_done), (z_free, z_done))):
                                pe.wait_ge(free, pair * 2 + c * NBLK + j + 1)
                                for k in range(KD):
                                    ins = nc.tensor.matmul(
                                        xz_ps[:, j, i, :], win[:, k, i * DI + c * P:i * DI + (c + 1) * P],
                                        xnT[:, k, ds((pair * 2 + j) * NB, NB)], start=k == 0, stop=k == KD - 1)
                                ins.then_inc(done, 1)

        for d, tag in enumerate(("f", "r")):
            with ExitStack() as inner:
                sb, ps, sem = alloc(nc, inner)
                wx = sb(f"b{tag}_wx", [P, CI, R + 2 * NS])
                wdt = sb(f"b{tag}_wdt", [R, DI])
                wout = sb(f"b{tag}_wout", [P, CI, D])
                vecs = sb(f"b{tag}_vecs", [P, CI, KC + 3])
                a_log = sb(f"b{tag}_a_log", [P, CI, NS])
                a_neg = sb(f"b{tag}_a_neg", [P, CI, NS])
                xc = sb(f"b{tag}_xc", [P, CI, HALF])
                dt = sb(f"b{tag}_dt", [P, CI, HALF])
                dtx = sb(f"b{tag}_dtx", [P, CI, HALF])
                xdbl = sb(f"b{tag}_xdbl", [R + 2 * NS, HALF])
                b_all = sb(f"b{tag}_b_all", [P, 2, HALF])
                c_all = sb(f"b{tag}_c_all", [P, 2, HALF])
                decay = sb(f"b{tag}_decay", [P, 2, HALF])
                drive = sb(f"b{tag}_drive", [P, 2, HALF])
                state = sb(f"b{tag}_state", [P, 2, HALF])
                read = sb(f"b{tag}_read", [P, 2, HALF])
                zero = sb(f"b{tag}_zero", [P, NB])
                scratch = nc.dram_tensor(f"b{tag}_scratch", (2, 2 * NS, HALF), F32, kind="Internal").ap()
                acc_ps = ps(f"b{tag}_acc_ps", [P, CI * HB, NB])
                w_in = sem(f"b{tag}_w_in")
                rows_out = sem(f"b{tag}_rows_out")
                bc_in = [sem(f"b{tag}_bc_in{j}") for j in range(2)]
                seq = sem(f"b{tag}_seq")
                conv_done = sem(f"b{tag}_conv_done")
                xc_done = sem(f"b{tag}_xc_done")
                dbl_done = sem(f"b{tag}_dbl_done")
                xdbl_done = sem(f"b{tag}_xdbl_done")
                step_done = sem(f"b{tag}_step_done")
                abs_done = sem(f"b{tag}_abs_done")
                exp_done = sem(f"b{tag}_exp_done")
                soft_done = sem(f"b{tag}_soft_done")
                relu_done = sem(f"b{tag}_relu_done")
                dt_done = sem(f"b{tag}_dt_done")
                decay_done = sem(f"b{tag}_decay_done")
                drive_done = sem(f"b{tag}_drive_done")
                state_done = sem(f"b{tag}_state_done")
                read_done = sem(f"b{tag}_read_done")
                acc_done = sem(f"b{tag}_acc_done")
                y_done = sem(f"b{tag}_y_done")
                out_done = sem(f"b{tag}_out_done")
                x_done = sem(f"b{tag}_x_done")
                a_done = sem(f"b{tag}_a_done")
                block = open_block(nc, inner, sem)
                NSTEP = CI * HB
                NCH = NS * CI
                taps = range(KC)
                rev = tag == "r"
                inside = slice(0, LQ - 1) if rev else slice(1, LQ)
                edge = slice(LQ - 1, LQ) if rev else slice(0, 1)
                HT = HALF // P

                def order(ap):
                    return ap[:, ::-1] if rev else ap

                @block.sync
                def _(sp):
                    for dst, name in ((wx, "wx"), (wdt, "wdt"), (wout, "wout"), (vecs, "vecs"), (a_log, "a_log")):
                        src = a["b_wout"] if name == "wout" else a[f"b{tag}_{name}"]
                        sp.dma_start(dst[:], src).then_inc(w_in, 16)
                    with sp.Fori(0, 2) as hf:
                        sp.wait_ge(xdbl_done, hf * HB + HB)
                        sp.dma_start(scratch[ds(hf, 1), :, :].rearrange("h r n -> r (h n)"),
                                     xdbl[R:R + 2 * NS, :]).then_inc(rows_out, 16)
                        with sp.Fori(0, NS // 2) as n2:
                            for j in range(2):
                                if j == 0:
                                    sp.wait_ge(rows_out, hf * 16 + 16)
                                sp.wait_ge(read_done, hf * NCH + n2 * (2 * CI) + j * CI + CI)
                                for dst, row in ((b_all, n2 * 2 + j), (c_all, n2 * 2 + j + NS)):
                                    sp.dma_start(dst[:, j, :],
                                                 scratch[ds(hf, 1), ds(row, 1), :].rearrange("h r n -> (h r n)")
                                                 .partition_broadcast(P)).then_inc(bc_in[j], 16)

                @block.tensor
                def _(pe):
                    pe.wait_ge(w_in, 80)
                    pe.wait_ge(conv_done, 1)
                    pe.sem_inc(out_done, 1)
                    pe.sem_inc(acc_done, 2)
                    with pe.Fori(0, 2) as hf:
                        pe.wait_ge(x_done, hf * HT + 2)
                        pe.wait_ge(xc_done, hf * CI + CI)
                        for blk in range(HB):
                            for c in range(CI):
                                ins = nc.tensor.matmul(acc_ps[0:R + 2 * NS, blk, :], wx[:, c, :],
                                                       xc[:, c, blk * NB:(blk + 1) * NB], start=c == 0, stop=c == CI - 1)
                            ins.then_inc(dbl_done, 1)
                        pe.wait_ge(xdbl_done, hf * HB + HB)
                        for s in range(NSTEP):
                            c, blk = s // HB, s % HB
                            ins = nc.tensor.matmul(acc_ps[:, s, :], wdt[:, c * P:(c + 1) * P],
                                                   xdbl[0:R, blk * NB:(blk + 1) * NB], start=True, stop=True)
                            if blk == HB - 1:
                                ins.then_inc(step_done, 1)
                        pe.wait_ge(dt_done, hf * CI + CI)
                        for s in range(NSTEP):
                            nc.tensor.matmul(acc_ps[:, s, :], ident[:, :], zero[:, :], start=True, stop=True)
                        with pe.Fori(0, NS // 2) as n2:
                            for j in range(2):
                                for c in range(CI):
                                    k = hf * NCH + n2 * (2 * CI) + j * CI + c
                                    pe.wait_ge(read_done, k + 2 * CI + 1)
                                    for blk in range(HB):
                                        ins = nc.tensor.matmul(acc_ps[:, c * HB + blk, :], ident[:, :],
                                                               read[:, c % 2, blk * NB:(blk + 1) * NB],
                                                               start=False, stop=True, skip_group_check=True)
                                    ins.then_inc(acc_done, 1)
                        pe.wait_ge(y_done, hf * CI + CI)
                        for i in range(HT):
                            pe.wait_ge(x_done, hf * HT + i + 1)
                            for c in range(CI):
                                ins = nc.tensor.matmul(acc_ps[:, i % 2, 0:D], dtx[:, c, i * P:(i + 1) * P], wout[:, c, :],
                                                       start=c == 0, stop=c == CI - 1)
                            ins.then_inc(out_done, 1)

                @block.scalar
                def _(act):
                    act.wait_ge(w_in, 80)
                    nc.scalar.activation(a_neg[:, :, :], a_log[:, :, :], ACT.Exp).then_inc(a_done, 1)
                    with act.Fori(0, 2) as hf:
                        for c in range(CI):
                            act.wait_ge(conv_done, hf * CI + 1 + c + 1)
                            nc.scalar.activation(xc[:, c, :], dt[:, c, :], ACT.Silu).then_inc(xc_done, 1)
                        for blk in range(HB):
                            act.wait_ge(dbl_done, hf * HB + blk + 1)
                            nc.scalar.activation(xdbl[:, blk * NB:(blk + 1) * NB], acc_ps[0:R + 2 * NS, blk, :],
                                                 ACT.Copy).then_inc(xdbl_done, 1)
                        act.wait_ge(out_done, hf * HT + 1)
                        for c in range(CI):
                            act.wait_ge(step_done, hf * CI + c + 1)
                            nc.scalar.activation(dtx[:, c, :], acc_ps[:, c * HB:(c + 1) * HB, :].rearrange("p b n -> p (b n)"),
                                                 ACT.Abs, bias=vecs[:, c, KC + 1:KC + 2]).then_inc(abs_done, 1)
                        for c in range(CI):
                            act.wait_ge(abs_done, hf * CI + c + 1)
                            nc.scalar.activation(dtx[:, c, :], dtx[:, c, :], ACT.Exp, scale=-1.0).then_inc(exp_done, 1)
                        for c in range(CI):
                            act.wait_ge(exp_done, hf * CI + c + 1)
                            nc.scalar.activation(dtx[:, c, :], dtx[:, c, :], ACT.Ln, bias=1.0).then_inc(soft_done, 1)
                        act.wait_ge(a_done, 3)
                        act.wait_ge(dt_done, hf * CI + CI)
                        with act.Fori(0, NS // 2) as n2:
                            for j in range(2):
                                for c in range(CI):
                                    k = hf * NCH + n2 * (2 * CI) + j * CI + c
                                    act.wait_ge(state_done, k + 1)
                                    nc.scalar.activation(
                                        decay[:, c % 2, :].rearrange("p (s l) -> p s l", l=LQ)[:, :, inside],
                                        dt[:, c, :].rearrange("p (s l) -> p s l", l=LQ)[:, :, inside], ACT.Exp,
                                        scale=a_neg[:, c, ds(n2 * 2 + j, 1)]).then_inc(decay_done, 1)

                @block.vector
                def _(dve):
                    dve.wait_ge(w_in, 80)
                    for j in range(2):
                        nc.vector.memset(decay[:, j, :].rearrange("p (s l) -> p s l", l=LQ)[:, :, edge], 0.0)
                    nc.vector.memset(zero[:, :], 0.0).then_inc(conv_done, 1)
                    dve.sem_inc(read_done, 2 * CI)
                    dve.sem_inc(state_done, 2)
                    dve.sem_inc(x_done, 2)
                    dve.wait_ge(a_done, 1)
                    nc.vector.tensor_scalar(a_neg[:, :, :], a_neg[:, :, :], -1.0, None, ALU.mult).then_inc(a_done, 2)
                    with dve.Fori(0, 2) as hf:
                        k = [0]
                        CHAIN = CI * (KC - 1) + 2 * CI

                        def link(ins):
                            k[0] += 1
                            ins.then_inc(seq, 1)
                            dve.wait_ge(seq, hf * CHAIN + k[0])

                        for c in range(CI):
                            if c == 0:
                                dve.wait_ge(out_done, hf * HT + 1)
                            acc = dt[:, c, :].rearrange("p (s l) -> p s l", l=LQ)

                            def window(tap):
                                off = KC - 1 + (KC - 1 - tap if rev else tap - (KC - 1))
                                return xpad[:, c, ds(hf * SEQ, SEQ), off:off + LQ]

                            link(nc.vector.tensor_scalar(acc, window(0), vecs[:, c, 0:1], vecs[:, c, KC:KC + 1],
                                                         ALU.mult, ALU.add))
                            for tap in range(1, KC):
                                ins = nc.vector.scalar_tensor_tensor(acc, window(tap), vecs[:, c, tap:tap + 1], acc,
                                                                     ALU.mult, ALU.add)
                                if tap < KC - 1:
                                    link(ins)
                                else:
                                    ins.then_inc(conv_done, 1)
                        dve.wait_ge(xc_done, hf * CI + CI)
                        for c in range(CI):
                            dve.wait_ge(abs_done, hf * CI + c + 1)
                            nc.vector.tensor_scalar(dt[:, c, :],
                                                    acc_ps[:, c * HB:(c + 1) * HB, :].rearrange("p b n -> p (b n)"),
                                                    vecs[:, c, KC + 1:KC + 2], 0.0, ALU.add, ALU.max
                                                    ).then_inc(relu_done, 1)
                        for c in range(CI):
                            dve.wait_ge(relu_done, hf * CI + c + 1)
                            dve.wait_ge(soft_done, hf * CI + c + 1)
                            nc.vector.tensor_tensor(dt[:, c, :], dt[:, c, :], dtx[:, c, :], ALU.add
                                                    ).then_inc(dt_done, 1)
                        for c in range(CI):
                            dve.wait_ge(dt_done, hf * CI + c + 1)
                            k[0] += 1
                            nc.vector.tensor_tensor(dtx[:, c, :], dt[:, c, :], xc[:, c, :], ALU.mult).then_inc(seq, 1)
                        DTX = k[0]

                        def make_drive(n2, j, c):
                            if c == 0:
                                if j == 0:
                                    dve.wait_ge(seq, hf * CHAIN + DTX)
                                dve.wait_ge(bc_in[j], n2 * 32 + hf * (NS // 2 * 32) + 32)
                            nc.vector.tensor_tensor(drive[:, c % 2, :], dtx[:, c, :], b_all[:, j, :], ALU.mult
                                                    ).then_inc(drive_done, 1)

                        def turn(n2, last):
                            for j in range(2):
                                for c in range(CI):
                                    kk = n2 * (2 * CI) + hf * NCH + j * CI + c
                                    dve.wait_ge(drive_done, kk + 1)
                                    dve.wait_ge(decay_done, kk + 1)
                                    nc.vector.tensor_tensor_scan(order(state[:, c % 2, :]), order(decay[:, c % 2, :]),
                                                                 order(drive[:, c % 2, :]), 0.0, ALU.mult, ALU.add
                                                                 ).then_inc(state_done, 1)
                                    if c < CI - 1:
                                        make_drive(n2, j, c + 1)
                                    elif j == 0:
                                        make_drive(n2, 1, 0)
                                    elif not last:
                                        make_drive(n2 + 1, 0, 0)
                                    dve.wait_ge(state_done, kk + 3)
                                    dve.wait_ge(acc_done, kk + 1)
                                    nc.vector.tensor_tensor(read[:, c % 2, :], state[:, c % 2, :], c_all[:, j, :],
                                                            ALU.mult).then_inc(read_done, 1)

                        make_drive(0, 0, 0)
                        with dve.Fori(0, NS // 2 - 1) as n2:
                            turn(n2, False)
                        turn(NS // 2 - 1, True)
                        dve.wait_ge(acc_done, hf * NCH + NCH + 2)
                        for c in range(CI):
                            link(nc.vector.scalar_tensor_tensor(
                                dtx[:, c, :], xc[:, c, :], vecs[:, c, KC + 2:KC + 3],
                                acc_ps[:, c * HB:(c + 1) * HB, :].rearrange("p b n -> p (b n)"), ALU.mult, ALU.add))
                            nc.vector.tensor_tensor(dtx[:, c, :], dtx[:, c, :], zs[:, c, ds(hf * HALF, HALF)], ALU.mult
                                                    ).then_inc(y_done, 1)
                        assert k[0] == CHAIN, (k[0], CHAIN)
                        for i in range(HT):
                            x_t = x_sb[:, ds(hf * HT + i, 1), :].rearrange("p a d -> p (a d)")
                            dve.wait_ge(out_done, hf * HT + i + 2)
                            nc.vector.tensor_tensor(x_t, acc_ps[:, i % 2, 0:D], x_t, ALU.add).then_inc(x_done, 1)


def feed_forward(nc, x_sb, ident, a):
    TOPK = 2
    with ExitStack() as ctx:
        sb, ps, sem = alloc(nc, ctx)
        xnT = normed(nc, ctx, "f")
        layer_norm(nc, "ln_f", x_sb, xnT, ident)
        wi = sb("f_wi", [P, KD, FF])
        wo = sb("f_wo", [P, CF, D])
        wk = sb("f_wk", [P, TOPK, KD, FF])
        lora_a = sb("f_lora_a", [RANK, TOPK, D])
        lora_b = sb("f_lora_b", [RANK, TOPK, FF])
        index = sb("f_index", [1, TOPK], I32)
        value = sb("f_value", [P, TOPK])
        h0 = sb("f_h0", [P, 2, NB])
        h1 = sb("f_h1", [P, 2, NB])
        h = sb("f_h", [P, CF, NB])
        first_ps = ps("f_first_ps", [P, 2, NB])
        second_ps = ps("f_second_ps", [P, 2, NB])
        out_ps = ps("f_out_ps", [P, 2, NB])
        i_in = sem("f_i_in")
        w_in = sem("f_w_in")
        lora_in = sem("f_lora_in")
        lora_done = sem("f_lora_done")
        wk_done = sem("f_wk_done")
        up_done = sem("f_up_done")
        h0_done = sem("f_h0_done")
        h1_done = sem("f_h1_done")
        h_done = sem("f_h_done")
        out_done = sem("f_out_done")
        x_done = sem("f_x_done")
        block = open_block(nc, ctx, sem)
        FB = FF // NB

        @block.sync
        def _(sp):
            sp.dma_start(index[:, :], a["f_index"]).then_inc(i_in, 16)
            sp.dma_start(wi[:, :, :], a["f_wi"]).then_inc(w_in, 16)
            sp.dma_start(wo[:, :, :], a["f_wo"]).then_inc(w_in, 16)
            sp.dma_start(value[:, :], a["f_value"].partition_broadcast(P)).then_inc(w_in, 16)
            sp.wait_ge(i_in, 16)
            for k in range(TOPK):
                e = sp.value_load(index[0:1, k:k + 1], min_val=0, max_val=NE - 1)
                sp.dma_start(lora_a[:, k, :], a["f_lora_a"][ds(e, 1), :, :].rearrange("e r d -> r (e d)")
                             ).then_inc(lora_in, 16)
                sp.dma_start(lora_b[:, k, :], a["f_lora_b"][ds(e, 1), :, :].rearrange("e r f -> r (e f)")
                             ).then_inc(lora_in, 16)

        @block.tensor
        def _(pe):
            for free, n in ((h0_done, 2), (h1_done, 2), (h_done, 2), (x_done, 2), (out_done, 1)):
                pe.sem_inc(free, n)
            pe.wait_ge(lora_in, 16 * 2 * TOPK)
            n = 0
            for k in range(TOPK):
                for c in range(KD):
                    for j in range(FB):
                        pe.wait_ge(wk_done, max(n - 1, 0))
                        nc.tensor.matmul(first_ps[:, n % 2, :], lora_a[:, k, c * P:(c + 1) * P],
                                         lora_b[:, k, j * NB:(j + 1) * NB], start=True, stop=True
                                         ).then_inc(lora_done, 1)
                        n += 1
            pe.wait_ge(wk_done, n)
            with pe.Fori(0, NBLK) as blk:
                for c in range(CF):
                    for k, dst in enumerate((first_ps, second_ps)):
                        pe.wait_ge(h0_done if k == 0 else h1_done, blk * CF + c + 1)
                        for i in range(KD):
                            ins = nc.tensor.matmul(dst[:, c % 2, :], wk[:, k, i, c * P:(c + 1) * P],
                                                   xnT[:, i, ds(blk * NB, NB)], start=i == 0, stop=i == KD - 1)
                        ins.then_inc(up_done, 1)
                pe.wait_ge(h_done, blk * CF + CF + 2)
                for i in range(TPB):
                    pe.wait_ge(x_done, blk * TPB + i + 1)
                    for c in range(CF):
                        ins = nc.tensor.matmul(out_ps[:, i % 2, 0:D], h[:, c, i * P:(i + 1) * P], wo[:, c, :],
                                               start=c == 0, stop=c == CF - 1)
                    ins.then_inc(out_done, 1)

        @block.scalar
        def _(act):
            with act.Fori(0, NBLK) as blk:
                for c in range(CF):
                    act.wait_ge(up_done, blk * (2 * CF) + 2 * c + 2)
                    act.wait_ge(h_done, blk * CF + c + 1)
                    nc.scalar.activation(h1[:, c % 2, :], second_ps[:, c % 2, :], ACT.Relu).then_inc(h1_done, 1)

        @block.vector
        def _(dve):
            dve.wait_ge(w_in, 48)
            n = 0
            for k in range(TOPK):
                for c in range(KD):
                    for j in range(FB):
                        cols = slice(j * NB, (j + 1) * NB)
                        dve.wait_ge(lora_done, n + 1)
                        nc.vector.tensor_tensor(wk[:, k, c, cols], first_ps[:, n % 2, :], wi[:, c, cols], ALU.add
                                                ).then_inc(wk_done, 1)
                        n += 1
            with dve.Fori(0, NBLK) as blk:
                dve.wait_ge(out_done, blk * TPB + 1)
                for c in range(CF):
                    dve.wait_ge(up_done, blk * (2 * CF) + 2 * c + 1)
                    nc.vector.tensor_scalar(h0[:, c % 2, :], first_ps[:, c % 2, :], 0.0, value[:, 0:1],
                                            ALU.max, ALU.mult).then_inc(h0_done, 1)
                    dve.wait_ge(h0_done, blk * CF + c + 3)
                    dve.wait_ge(h1_done, blk * CF + c + 3)
                    nc.vector.scalar_tensor_tensor(h[:, c, :], h1[:, c % 2, :], value[:, 1:2], h0[:, c % 2, :],
                                                   ALU.mult, ALU.add).then_inc(h_done, 1)
                for i in range(TPB):
                    x_t = x_sb[:, ds(blk * TPB + i, 1), :].rearrange("p a d -> p (a d)")
                    dve.wait_ge(out_done, blk * TPB + i + 2)
                    nc.vector.tensor_tensor(x_t, out_ps[:, i % 2, 0:D], x_t, ALU.add).then_inc(x_done, 1)


def program(nc, a, out, phases=6):
    with ExitStack() as ctx:
        sb, ps, sem = alloc(nc, ctx)
        x_sb = sb("x_sb", [P, NT, D])
        ident = sb("ident", [P, P])
        pair_mask = sb("pair_mask", [PAIRS, PAIRS])
        x_in = sem("x_in")
        x_out = sem("x_out")
        with nc.Block() as block:
            @block.sync
            def _(sp):
                sp.dma_start(x_sb[:, :, :], a["x"].rearrange("(t p) d -> p t d", p=P)).then_inc(x_in, 16)
                sp.dma_start(ident[:, :], a["ident"]).then_inc(x_in, 16)
                sp.dma_start(pair_mask[:, :], a["ident"][0:PAIRS, 0:PAIRS]).then_inc(x_in, 16)
                sp.wait_ge(x_in, 48)

        def xattn(i):
            w = {k: a[f"x{i}_{k}"] for k in ("wq", "wk", "wv", "wo", "bq", "bv")}
            cross_attention(nc, f"x{i}", x_sb, ident, pair_mask, a["ctxT"], bo=a["x0_bo"] if i == 0 else None, **w)

        steps = [lambda: xattn(0),
                 lambda: self_attention(nc, x_sb, ident, a),
                 lambda: experts(nc, x_sb, ident, a),
                 lambda: xattn(1),
                 lambda: mamba(nc, x_sb, ident, a),
                 lambda: feed_forward(nc, x_sb, ident, a)]
        for i in (phases if isinstance(phases, (list, tuple)) else range(phases)):
            steps[i]()
        with nc.Block() as block:
            @block.sync
            def _(sp):
                sp.dma_start(out.rearrange("(t p) d -> p t d", p=P), x_sb[:, :, :]).then_inc(x_out, 16)
                sp.wait_ge(x_out, 16)



def more_layouts(i, arr):
    import numpy as np
    f = np.float32
    arr["s_w"] = i["L0_attn_w_qkv"].reshape(KD, P, 3 * D).transpose(1, 0, 2)
    mask = np.zeros((P, 8), f)
    for r in range(P):
        mask[r, r // DH] = D ** -0.5
    arr["s_mask"] = mask
    arr["m_rms_w"] = i["L0_ffn_rms_w"].reshape(KD, P).T
    arr["m_gate_w"] = i["L0_ffn_gate_w"].T.reshape(KD, P, NE).transpose(1, 0, 2)
    const = {"rows_before": np.triu(np.ones((P, P), f), 1), "ones": np.ones(P, f), "experts": np.arange(NE, dtype=f) - NE,
             "tile_chain": np.tile(np.arange(NT) > 0, NE), "whole_blocks": P * np.arange(NT),
             "blocks": np.arange(SLOT_BLOCKS)}
    arr["m_const"] = np.concatenate([np.broadcast_to(const[k], (P, n)).astype(f) for k, n in M_CONST_PARTS], axis=1)
    for n in (1, 2):
        arr[f"m_w{n}"] = i[f"L0_ffn_W{n}"].transpose(0, 2, 1).reshape(NE, KD, P, DE).transpose(0, 2, 1, 3)
    w3 = np.zeros((NE, EC * P, D), f)
    w3[:, :DE] = i["L0_ffn_W3"].transpose(0, 2, 1)
    arr["m_w3"] = w3.reshape(NE, EC, P, D).transpose(0, 2, 1, 3)
    arr["b_win"] = i["L1_attn_W_in"].T.reshape(KD, P, 2 * DI).transpose(1, 0, 2)
    arr["b_wout"] = i["L1_attn_W_out"].T.reshape(CI, P, D).transpose(1, 0, 2)
    for tag, n in (("f", "fwd"), ("r", "rev")):
        def chunks(v):
            return v.reshape(CI, P, -1).transpose(1, 0, 2)
        arr[f"b{tag}_wx"] = chunks(i[f"L1_attn_Wx_{n}"].T)
        arr[f"b{tag}_wdt"] = i[f"L1_attn_Wdt_{n}"].T
        arr[f"b{tag}_a_log"] = chunks(i[f"L1_attn_A_log_{n}"])
        arr[f"b{tag}_vecs"] = np.concatenate(
            [chunks(i[f"L1_attn_{v}_{n}"]) for v in ("conv_w", "conv_b", "bdt", "D")], axis=2)
    arr["f_wi"] = i["L1_ffn_wi_w"].T.reshape(KD, P, FF).transpose(1, 0, 2)
    arr["f_wo"] = i["L1_ffn_wo_w"].T.reshape(CF, P, D).transpose(1, 0, 2)
    arr["f_lora_a"] = i["L1_ffn_lora_As"]
    arr["f_lora_b"] = i["L1_ffn_lora_Bs"].transpose(0, 2, 1)
    arr["f_index"] = i["L1_ffn_top_k_indices"].reshape(1, 2)
    arr["f_value"] = i["L1_ffn_top_k_values"]


def layouts(inputs):
    import numpy as np
    i = {k: np.asarray(v) for k, v in inputs.items()}
    f = np.float32
    arr = {"x": i["x"].reshape(TOK, D), "ident": np.eye(P, dtype=f)}
    ctxT = np.zeros((B + 2, DC, LKV), f)
    ctxT[:B] = i["ctx_512"].transpose(0, 2, 1)
    arr["ctxT"] = ctxT

    def xattn(n, wq, wk, wv, wo, bq, bv):
        arr[f"x{n}_wq"] = wq.reshape(KD, P, D).transpose(1, 0, 2)
        z = np.zeros((P, H, DC), f)
        for h in range(H):
            r = h % 8 * DH
            z[r:r + DH, h, :] = wk[:, h * DH:(h + 1) * DH].T
        arr[f"x{n}_wk"] = z
        v = np.zeros((DC, NG, VW), f)
        b = np.zeros((NG, VW), f)
        for g in range(NG):
            w = GROUPS[g] * DH
            v[:, g, :w] = wv[:, G0[g] * DH:G0[g] * DH + w]
            if bv is not None:
                b[g, :w] = bv[G0[g] * DH:G0[g] * DH + w]
            b[g, 96] = 1.0
        arr[f"x{n}_wv"] = v.reshape(DC, NG * VW)
        arr[f"x{n}_bv"] = b.reshape(NG * VW)
        arr[f"x{n}_wo"] = wo.reshape(PAIRS, 2, DH, D).transpose(0, 2, 1, 3).reshape(P, 2, D)
        arr[f"x{n}_bq"] = (bq if bq is not None else np.zeros(D, f)).reshape(KD, P).T

    xattn(0, i["L0_xattn_Wq"], i["L0_xattn_Wk"], i["L0_xattn_Wv"], i["L0_xattn_Wo"], i["L0_xattn_bq"], i["L0_xattn_bv"])
    arr["x0_bo"] = i["L0_xattn_bo"]
    kv = i["L1_xattn_Wkv"]
    xattn(1, i["L1_xattn_Wq"].T, kv[:D].T, kv[D:].T, i["L1_xattn_Wo"].T, None, None)
    more_layouts(i, arr)
    return {k: np.ascontiguousarray(v) for k, v in arr.items()}


def kernel(**inputs):
    import concourse.bacc as bacc
    from concourse.bass_utils import run_bass_kernel_spmd

    arrays = layouts(inputs)
    nc = bacc.Bacc("TRN2", target_bir_lowering=False, num_devices=1)
    a = {k: nc.dram_tensor(f"in_{k}", v.shape, mybir.dt.from_np(v.dtype), kind="ExternalInput").ap()
         for k, v in arrays.items()}
    out = nc.dram_tensor("out_x", (TOK, D), F32, kind="ExternalOutput").ap()
    program(nc, a, out)
    r = run_bass_kernel_spmd(nc, [{f"in_{k}": v for k, v in arrays.items()}], core_ids=[0])
    return r.results[0]["out_x"].reshape(B, LQ, D)
```

```python
import concourse.bass as bass
from concourse import mybir
from concourse.alu_op_type import AluOpType as ALU
from contextlib import ExitStack

F32 = mybir.dt.float32
F32R = mybir.dt.float32r
U32 = mybir.dt.uint32
I32 = mybir.dt.int32
ACT = mybir.ActivationFunctionType
AX = mybir.AxisListType
ds = bass.ds

P = 128
B, LQ, D = 32, 64, 256
LKV, DC = 1601, 128
H, DH = 16, 16
TOK = B * LQ
NT = TOK // P
KD = D // P
NB = 512
NBLK = TOK // NB
TPB = NB // P
LN_EPS, RMS_EPS = 1e-5, 1e-6

KT = -(-LKV // P)
KLAST = LKV - (KT - 1) * P
PAIRS = H // 2
WINDOWS = [(0, 402), (402, 402), (804, 402), (LKV - 402, 402)]
NE, DE = 8, 704
FLT_MAX = 3.4028234663852886e38
SLOT_BLOCKS = (2 * TOK + NE * (P - 1)) // P
M_CONST_PARTS = [("rows_before", P), ("ones", P), ("experts", NE), ("tile_chain", NE * NT), ("whole_blocks", NT),
                 ("blocks", SLOT_BLOCKS)]
M_CONST = sum(n for _, n in M_CONST_PARTS)
EC = -(-DE // P)
ELAST = DE - (EC - 1) * P
DI, NS, KC, R = 512, 16, 4, 64
CI = DI // P
PADL = LQ + 2 * (KC - 1)
HALF = TOK // 2
FF, RANK = 1024, 16
CF = FF // P


def alloc(nc, ctx):
    def sb(name, shape, dt=F32):
        return ctx.enter_context(nc.sbuf_tensor(name, shape, dt))

    def ps(name, shape, dt=F32):
        return ctx.enter_context(nc.psum_tensor(name, shape, dt))

    def sem(name):
        s = ctx.enter_context(nc.semaphore(name))
        sem.taken.append(s)
        return s

    sem.taken = []
    return sb, ps, sem


def open_block(nc, ctx, sem):
    def clear(error, *_):
        if error is None:
            with nc.Block() as block:
                @block.sync
                def _(sp):
                    for s in sem.taken:
                        sp.sem_clear(s)

    ctx.push(clear)
    return ctx.enter_context(nc.Block())


def normed(nc, ctx, tag):
    return ctx.enter_context(nc.sbuf_tensor(f"{tag}_xnT", [P, KD, TOK + P], F32))


def layer_norm(nc, tag, x_sb, xnT, ident, rms=None, rows=None, loads=None):
    UT = 4
    with ExitStack() as ctx:
        sb, ps, sem = alloc(nc, ctx)
        stats = sb(f"{tag}_stats", [P, NT, 6])
        moments = sb(f"{tag}_moments", [P, NT, 2])
        std = sb(f"{tag}_std", [P, NT])
        rstd = sb(f"{tag}_rstd", [P, NT])
        eps = sb(f"{tag}_eps", [P, 2])
        xn = sb(f"{tag}_xn", [P, UT, D])
        if rms is not None:
            mean_sq = sb(f"{tag}_mean_sq", [P, NT])
            root = sb(f"{tag}_root", [P, NT])
            scale = sb(f"{tag}_scale", [P, NT])
            gain = sb(f"{tag}_gain", [P, NT])
            offset = sb(f"{tag}_offset", [P, NT])
        xT = ps(f"{tag}_xT", [P, UT, NB])
        stats_done = sem(f"{tag}_stats_done")
        moments_done = sem(f"{tag}_moments_done")
        std_done = sem(f"{tag}_std_done")
        chain = sem(f"{tag}_chain")
        eps_done = sem(f"{tag}_eps_done")
        xn_done = sem(f"{tag}_xn_done")
        transposed = sem(f"{tag}_transposed")
        copied = sem(f"{tag}_copied")
        block = open_block(nc, ctx, sem)

        def tile(t):
            return x_sb[:, ds(t, 1), :].rearrange("p a d -> p (a d)")

        def add_norm(dve, t):
            dve.wait_ge(xn_done, t + 1)
            nc.vector.tensor_scalar(tile(t), tile(t), gain[:, ds(t, 1)], offset[:, ds(t, 1)], ALU.mult, ALU.add)

        @block.sync
        def _(sp):
            if loads is not None:
                loads(sp)

        @block.vector
        def _(dve):
            n = 0

            def link(ins):
                nonlocal n
                n += 1
                ins.then_inc(chain, 1)
                dve.wait_ge(chain, n)

            nc.vector.memset(xnT[:, :, TOK:], 0.0)
            nc.vector.memset(eps[:, 0:1], LN_EPS)
            nc.vector.memset(eps[:, 1:2], RMS_EPS).then_inc(eps_done, 1)
            with dve.Fori(0, NT // UT) as turn:
                for j in range(UT):
                    t = turn * UT + j
                    nc.vector.bn_stats(stats[:, ds(t, 1), :].rearrange("p a s -> p (a s)"), tile(t)
                                       ).then_inc(stats_done, 1)
            dve.wait_ge(stats_done, NT)
            for t in range(NT):
                ins = nc.vector.bn_aggr(moments[:, t, :], stats[:, t, :])
            ins.then_inc(moments_done, 1)
            dve.wait_ge(std_done, 1)
            link(nc.vector.reciprocal(rstd[:, :], std[:, :]))
            by = rstd
            if rms is not None:
                dve.wait_ge(moments_done, 1)
                link(nc.vector.tensor_tensor(mean_sq[:, :], moments[:, :, 1], rstd[:, :], ALU.mult))
                nc.vector.tensor_tensor(mean_sq[:, :], mean_sq[:, :], rstd[:, :], ALU.mult).then_inc(moments_done, 1)
                link(nc.vector.tensor_scalar(gain[:, :], rstd[:, :], 1.0, None, ALU.add))
                link(nc.vector.scalar_tensor_tensor(offset[:, :], moments[:, :, 0], -1.0, rstd[:, :],
                                                    ALU.mult, ALU.mult))
                dve.wait_ge(std_done, 2)
                link(nc.vector.reciprocal(scale[:, :], root[:, :]))
                link(nc.vector.tensor_tensor(scale[:, :], scale[:, :], rstd[:, :], ALU.mult))
                by = scale
            with dve.Fori(0, NT // UT) as turn:
                for j in range(UT):
                    t = turn * UT + j
                    dve.wait_ge(transposed, t + 1)
                    if rms is not None:
                        dve.wait_ge(copied, t + 1)
                    nc.vector.tensor_scalar(xn[:, j, :], tile(t), moments[:, ds(t, 1), 0:1].rearrange("p a s -> p (a s)"),
                                            by[:, ds(t, 1)], ALU.subtract, ALU.mult).then_inc(xn_done, 1)
                    if rms is not None and j > 0:
                        add_norm(dve, t - 1)
                if rms is not None:
                    add_norm(dve, turn * UT + UT - 1)

        @block.scalar
        def _(act):
            act.wait_ge(eps_done, 1)
            act.wait_ge(moments_done, 1)
            nc.scalar.activation(std[:, :], moments[:, :, 1], ACT.Sqrt, bias=eps[:, 0:1]).then_inc(std_done, 1)
            if rms is not None:
                act.wait_ge(moments_done, 2)
                nc.scalar.activation(root[:, :], mean_sq[:, :], ACT.Sqrt, bias=eps[:, 1:2]).then_inc(std_done, 1)
            with act.Fori(0, NT // UT) as turn:
                for j in range(UT):
                    t = turn * UT + j
                    if rms is not None:
                        act.wait_ge(xn_done, t + 1)
                        nc.scalar.activation(rows[:, ds(t, 1), :].rearrange("p a d -> p (a d)"), xn[:, j, :], ACT.Copy)
                    act.wait_ge(transposed, t + UT + 1)
                    if rms is not None:
                        for c in range(KD):
                            ins = nc.scalar.activation(xnT[:, c, ds(t * P, P)], xT[:, j, c * P:(c + 1) * P],
                                                       ACT.Copy, scale=rms[:, c:c + 1])
                    else:
                        ins = nc.scalar.activation(xnT[:, :, ds(t * P, P)],
                                                   xT[:, j, 0:KD * P].rearrange("p (c n) -> p c n", c=KD), ACT.Copy)
                    ins.then_inc(copied, 1)

        @block.tensor
        def _(pe):
            pe.sem_inc(transposed, UT)
            pe.sem_inc(copied, UT)
            with pe.Fori(0, NT // UT) as turn:
                for j in range(UT):
                    t = turn * UT + j
                    pe.wait_ge(xn_done, t + 1)
                    pe.wait_ge(copied, t + 1)
                    for c in range(KD):
                        ins = nc.tensor.transpose(xT[:, j, c * P:(c + 1) * P], xn[:, j, c * P:(c + 1) * P], ident[:, :])
                    ins.then_inc(transposed, 1)


def project_queries(nc, ctx, tag, x_sb, ident, qT, wq, bq, loads):
    sb, ps, sem = alloc(nc, ctx)
    xnT = normed(nc, ctx, tag)
    wq_sb = sb(f"{tag}_wq", [P, KD, D])
    bq_sb = sb(f"{tag}_bq", [P, KD])
    w_in = sem(f"{tag}_q_w_in")

    def all_loads(sp):
        sp.dma_start(wq_sb[:, :, :], wq).then_inc(w_in, 16)
        sp.dma_start(bq_sb[:, :], bq).then_inc(w_in, 16)
        loads(sp)

    layer_norm(nc, f"ln_{tag}", x_sb, xnT, ident, loads=all_loads)
    q_ps = ps(f"{tag}_q_ps", [P, 2, NB])
    q_made = sem(f"{tag}_q_made")
    q_done = sem(f"{tag}_q_done")
    block = open_block(nc, ctx, sem)
    parts = [(c, blk) for c in range(KD) for blk in range(NBLK)]

    @block.tensor
    def _(pe):
        pe.wait_ge(w_in, 32)
        for n, (c, blk) in enumerate(parts):
            if n >= 2:
                pe.wait_ge(q_done, n - 1)
            for k in range(KD):
                ins = nc.tensor.matmul(q_ps[:, n % 2, :], wq_sb[:, k, c * P:(c + 1) * P],
                                       xnT[:, k, blk * NB:(blk + 1) * NB], start=k == 0, stop=k == KD - 1)
            ins.then_inc(q_made, 1)

    @block.vector
    def _(dve):
        nc.vector.memset(qT[:, :, TOK:], 0.0)
        dve.wait_ge(w_in, 32)
        for n, (c, blk) in enumerate(parts):
            dve.wait_ge(q_made, n + 1)
            nc.vector.tensor_scalar(qT[:, c, blk * NB:(blk + 1) * NB], q_ps[:, n % 2, :], bq_sb[:, c:c + 1],
                                    DH ** -0.5, ALU.add, ALU.mult).then_inc(q_done, 1)


def cross_attention(nc, tag, x_all, ident, pair_mask, ctxT, wq, wk, wv, wo, bq, bv, bo):
    x_sb = x_all[:, 1:, :]
    UN = 4
    NU, UH = 2, H // 2
    UC = UH * LQ
    GH = 4
    NGR = H // GH
    GV, GC = GH * DH, GH * LQ
    LAG = 2
    NSB, NMB = 3, 3
    NPB = 4
    assert KT * UN % NPB == 0 and B % UN == 0
    MAXES = [("M", p, w) for p in range(PAIRS) for w in range(len(WINDOWS))]
    PLACES = 4 + NGR
    PLAN, AT = {}, {}
    for u in range(UN):
        rows = [{2: [("V", i)]} for i in range(KT)]
        for m, op in enumerate(MAXES):
            rows[1 + m // 3].setdefault((0, 4, 7)[m % 3], []).append(op)
        for i, place, op in ((3, 5, ("S", 0)), (4, 5, ("S", 1)), (5, 5, ("X", 0)), (6, 5, ("X", 1)), (8, 5, ("Y",)),
                             (9, 5, ("Z",)), (12, 0, ("T",))):
            rows[i].setdefault(place, []).append(op)
        if u % 2 == 0:
            for k, (i, place) in enumerate(((0, 4), (0, 6), (12, 4), (12, 6))):
                rows[i].setdefault(place, []).append(("Q", k))
        PLAN[u] = [[op for place in range(PLACES) for op in row.get(place, [])] for row in rows]
        AT[u] = [[sum(len(row.get(q, [])) for q in range(place + 1)) for place in range(PLACES)] for row in rows]
    FINISH = [("S", 0), ("S", 1), ("X", 0), ("X", 1), ("Y",), ("Z",)]
    PROLOGUE = ([("Q", k) for k in range(4)]
                + MAXES + [("T",)])
    FIRST = {}
    n = len(PROLOGUE)
    for u in range(UN):
        FIRST[u] = n
        n += sum(len(r) for r in PLAN[u])
    ROUND = n - len(PROLOGUE)
    assert ROUND % NMB == 0

    def last_unit(j):
        return max(k for k in range(-KT * NU, j) if k % (KT * NU) % NSB == j % NSB)

    def row_first(u, i):
        return FIRST[u] + sum(len(r) for r in PLAN[u][:i])

    def number(u, i, op):
        return row_first(u, i) + PLAN[u][i].index(op)

    with ExitStack() as ctx:
        sb, ps, sem = alloc(nc, ctx)
        qT = sb(f"{tag}_qT", [P, KD, TOK + 2 * LQ])
        wk_sb = sb(f"{tag}_wk", [P, H, DC])
        wv_sb = sb(f"{tag}_wv", [P, D])
        bv_sb = sb(f"{tag}_bv", [P, 2])
        wo_sb = sb(f"{tag}_wo", [P, 2, D])
        bo_sb = sb(f"{tag}_bo", [P, D])
        raw = sb(f"{tag}_raw", [P, 2, LKV])
        w_in = sem(f"{tag}_w_in")
        ctx_in = [sem(f"{tag}_ctx_in{j}") for j in range(2)]
        NW = 5 if bo is not None else 4

        def loads(sp):
            sp.dma_start(wk_sb[:, :, :], wk).then_inc(w_in, 16)
            sp.dma_start(wv_sb[:, :], wv).then_inc(w_in, 16)
            sp.dma_start(bv_sb[:, :], bv).then_inc(w_in, 16)
            sp.dma_start(wo_sb[:, :, :], wo).then_inc(w_in, 16)
            if bo is not None:
                sp.dma_start(bo_sb[:, :], bo.partition_broadcast(P)).then_inc(w_in, 16)
            for j in range(2):
                sp.dma_start(raw[:, j, :], ctxT[j, :, :]).then_inc(ctx_in[j], 16)

        with ExitStack() as inner:
            project_queries(nc, inner, tag, x_sb, ident, qT, wq, bq, loads)
        wv_hi = sb(f"{tag}_wv_hi", [P, D], F32R)
        wv_lo = sb(f"{tag}_wv_lo", [P, D], F32R)
        ones = sb(f"{tag}_ones", [PAIRS, P], F32R)
        all_ones = sb(f"{tag}_all_ones", [P, P])
        q_hi = sb(f"{tag}_q_hi", [P, 2, 2, H, LQ], F32R)
        q_lo = sb(f"{tag}_q_lo", [P, 2, 2, H, LQ], F32R)
        c_hi = sb(f"{tag}_c_hi", [P, 2, LKV], F32R)
        c_lo = sb(f"{tag}_c_lo", [P, 2, LKV], F32R)
        maxes = sb(f"{tag}_maxes", [P, PAIRS, len(WINDOWS)])
        neg_max = sb(f"{tag}_neg_max", [P, PAIRS])
        shift = sb(f"{tag}_shift", [PAIRS, 2, PAIRS, P], F32R)
        v_sb = sb(f"{tag}_v", [P, NPB, NGR, 2, GV], F32R)
        probs = sb(f"{tag}_probs", [P, NPB, H * LQ])
        p_hi = sb(f"{tag}_p_hi", [P, NPB, H * LQ], F32R)
        p_lo = sb(f"{tag}_p_lo", [P, NPB, H * LQ], F32R)
        sums = sb(f"{tag}_sums", [P, 2, H * LQ])
        u_sb = sb(f"{tag}_u", [P, H * LQ])
        recip = sb(f"{tag}_recip", [P, PAIRS])
        o_sb = sb(f"{tag}_o", [P, PAIRS, DH])
        oT = sb(f"{tag}_oT", [P, P])
        score_ps = ps(f"{tag}_score_ps", [P, NSB, NB])
        pv_ps = ps(f"{tag}_pv_ps", [P, NU, NB])
        misc_ps = ps(f"{tag}_misc_ps", [P, NMB, NB])

        const_done = sem(f"{tag}_const_done")
        wv_hi_done = sem(f"{tag}_wv_hi_done")
        wv_done = sem(f"{tag}_wv_done")
        x_biased = sem(f"{tag}_x_biased")
        c_hi_done = sem(f"{tag}_c_hi_done")
        c_lo_done = sem(f"{tag}_c_lo_done")
        q_hi_done = sem(f"{tag}_q_hi_done")
        v_hi_done = sem(f"{tag}_v_hi_done")
        misc_ready = sem(f"{tag}_misc_ready")
        misc_free = sem(f"{tag}_misc_free")
        max_done = sem(f"{tag}_max_done")
        score_ready = sem(f"{tag}_score_ready")
        score_free = sem(f"{tag}_score_free")
        p_hi_done = sem(f"{tag}_p_hi_done")
        p_lo_done = sem(f"{tag}_p_lo_done")
        sums_done = sem(f"{tag}_sums_done")
        pv_done = sem(f"{tag}_pv_done")
        u_done = sem(f"{tag}_u_done")
        o_normed = sem(f"{tag}_o_normed")
        block = open_block(nc, ctx, sem)

        def keys(i):
            return KLAST if i == KT - 1 else P

        def unit(w):
            return slice(w * UC, (w + 1) * UC)

        @block.sync
        def _(sp):
            with sp.Fori(0, B // UN) as t:
                for u in range(UN):
                    sp.wait_ge(c_lo_done, t * UN + u + 1)
                    sp.dma_start(raw[:, u % 2, :],
                                 ctxT[ds(t * UN + u + 2, 1), :, :].rearrange("b p k -> p (b k)")
                                 ).then_inc(ctx_in[u % 2], 16)
            for j in range(2):
                sp.wait_ge(ctx_in[j], 16 * (B // 2 + 1))

        @block.tensor
        def _(pe):
            def small(op, u, t, n):
                bank = misc_ps[:, n % NMB, :]
                nxt = (u + 1) % UN
                b = t * UN + u
                pe.wait_ge(misc_free, t * ROUND + n + 1)
                if op[0] == "Q":
                    first = 0 if u < 0 else (b + 2) * LQ
                    for j in range(4):
                        h = 4 * op[1] + j
                        ins = nc.tensor.matmul(bank[:, j * P:(j + 1) * P], wk_sb[:, h, :],
                                               qT[:, h // 8, ds(first, P)], start=True, stop=True)
                elif op[0] == "V":
                    i = op[1]
                    for m, (a, w) in enumerate(((c_hi, wv_hi), (c_hi, wv_lo), (c_lo, wv_hi))):
                        ins = nc.tensor.matmul(bank[0:keys(i), 0:D], a[:, u % 2, i * P:i * P + keys(i)],
                                               w[:, :], start=m == 0, stop=m == 2)
                elif op[0] == "M":
                    _, p, w = op
                    k0, kn = WINDOWS[w]
                    pe.wait_ge(c_hi_done, b + 2)
                    q = q_hi[:, nxt // 2, nxt % 2, 2 * p:2 * p + 2, :].rearrange("p h q -> p (h q)")
                    ins = nc.tensor.matmul(bank[:, 0:kn], q, c_hi[:, nxt % 2, k0:k0 + kn], start=True, stop=True)
                elif op[0] == "T":
                    pe.wait_ge(max_done, b + 2)
                    ins = nc.tensor.transpose(bank[0:PAIRS, 0:P], neg_max[:, :], ident[:, :])
                elif op[0] == "S":
                    pe.wait_ge(sums_done, b * KT + NPB)
                    for k in range(UH // 2):
                        col = op[1] * UC + k * P
                        ins = nc.tensor.matmul(bank[:, k * P:(k + 1) * P], sums[:, (u - 1) % 2, col:col + P],
                                               all_ones[:, :], start=True, stop=True)
                elif op[0] == "X":
                    pe.wait_ge(u_done, b * NU + op[1] + 1)
                    for k in range(UH // 2):
                        col = op[1] * UC + k * P
                        ins = nc.tensor.transpose(bank[:, k * P:(k + 1) * P], u_sb[:, col:col + P], ident[:, :])
                elif op[0] == "Y":
                    pe.wait_ge(o_normed, b * NU + NU)
                    ins = nc.tensor.transpose(bank[:, 0:P], o_sb[:, :, :].rearrange("p a d -> p (a d)"), ident[:, :])
                elif op[0] == "Z":
                    half = (u - 1) % 2
                    pe.wait_ge(misc_free, t * ROUND + n + NMB)
                    for j in range(2):
                        ins = nc.tensor.matmul(bank[half * LQ:(half + 1) * LQ, 0:D], oT[:, j * LQ:(j + 1) * LQ],
                                               wo_sb[:, j, :], start=j == 0, stop=j == 1)
                ins.then_inc(misc_ready, 1)

            def pv(u, t, i, then):
                tile = KT * u + i
                N = t * (UN * KT) + tile
                pe.wait_ge(p_lo_done, N + NPB + 1)
                value = number(u % UN, i, ("V", i)) - (ROUND if u < 0 else 0)
                pe.wait_ge(misc_free, t * ROUND + value + NMB + 1)
                if i == 0:
                    pe.wait_ge(u_done, (t * UN + u) * NU + NU)
                for g in range(NGR):
                    w, col = g // 2, g % 2 * GC
                    cols = slice(g * GC, (g + 1) * GC)
                    nc.tensor.matmul(pv_ps[:, w, col:col + GC],
                                     v_sb[0:keys(i), tile % NPB, g, :, :].rearrange("p a d -> p (a d)"),
                                     p_hi[0:keys(i), tile % NPB, cols], start=i == 0 and col == 0, stop=False,
                                     skip_group_check=True)
                    ins = nc.tensor.matmul(pv_ps[0:GV, w, col:col + GC], v_sb[0:keys(i), tile % NPB, g, 0, :],
                                           p_lo[0:keys(i), tile % NPB, cols], start=False, stop=i == KT - 1,
                                           skip_group_check=True)
                    if g == NGR - 1:
                        ins.then_inc(pv_done, 1)
                    then(4 + g)

            pe.sem_inc(score_ready, 1)
            pe.sem_inc(pv_done, 2)
            pe.wait_ge(w_in, 16 * NW)
            pe.wait_ge(const_done, 1)
            for n, op in enumerate(PROLOGUE):
                if op == ("M", 0, 0):
                    pe.wait_ge(misc_free, n + NMB)
                small(op, -1, 0, n)
            pe.wait_ge(wv_done, 1)
            for g in range(NGR):
                nc.tensor.matmul(pv_ps[:, g // 2, g % 2 * GC:g % 2 * GC + GC],
                                 v_sb[:, NPB - 1, g, :, :].rearrange("p a d -> p (a d)"),
                                 p_hi[:, NPB - 1, g * GC:(g + 1) * GC], start=True, stop=True)
            with pe.Fori(0, B // UN) as t:
                for u in range(UN):
                    b = t * UN + u
                    for i in range(KT):
                        tile = KT * u + i
                        N = t * (UN * KT) + tile
                        n = row_first(u, i)
                        work = list(enumerate(PLAN[u][i], n))

                        def then(place):
                            while AT[u][i][place] > len(PLAN[u][i]) - len(work):
                                k, op = work.pop(0)
                                small(op, u, t, k)

                        cols = slice(i * P, i * P + keys(i))
                        for w in range(NU):
                            if i == 0 and w == 0:
                                pe.wait_ge(c_lo_done, b + 1)
                                maxima = number(u - 1, KT - 1, ("T",)) if u > 0 else FIRST[0] - 1
                                pe.wait_ge(misc_free, t * ROUND + maxima + NMB + 1)
                            pe.wait_ge(score_free, b * (KT * NU) + last_unit(i * NU + w) + NSB + 1)
                            out = score_ps[0:keys(i), (i * NU + w) % NSB, :]
                            heads = slice(w * UH, (w + 1) * UH)
                            for m, (a, q) in enumerate(((c_hi, q_hi), (c_hi, q_lo), (c_lo, q_hi))):
                                nc.tensor.matmul(out, a[:, u % 2, cols],
                                                 q[:, u // 2, u % 2, heads, :].rearrange("p h q -> p (h q)"),
                                                 start=m == 0, stop=False)
                                if m == 1:
                                    then(2 * w)
                            nc.tensor.matmul(out, ones[:, 0:keys(i)],
                                             shift[:, u % 2, :, :].rearrange("r a c -> r (a c)")[:, unit(w)],
                                             start=False, stop=True).then_inc(score_ready, 1)
                            then(2 * w + 1)
                        if i < LAG:
                            pv(u - 1, t, KT + i - LAG, then)
                        else:
                            pv(u, t, i - LAG, then)
                        assert not work
            end = B // UN
            for i in range(KT - LAG, KT):
                pv(-1, end, i, lambda place: None)
            for n, op in enumerate(FINISH, FIRST[0]):
                small(op, 0, end, n)

        @block.scalar
        def _(act):
            act.sem_inc(score_free, NSB)
            act.sem_inc(p_hi_done, NPB)
            act.wait_ge(w_in, 16 * NW)
            nc.scalar.activation(wv_hi[:, :], wv_sb[:, :], ACT.Copy).then_inc(wv_hi_done, 1)

            def split(j, arrived):
                act.wait_ge(ctx_in[j], arrived)
                nc.scalar.activation(c_hi[:, j, :], raw[:, j, :], ACT.Copy).then_inc(c_hi_done, 1)

            def queries(k, s, t, n):
                act.wait_ge(misc_ready, t * ROUND + n + 1)
                nc.scalar.activation(
                    q_hi[:, s, :, 4 * k:4 * k + 4, :],
                    misc_ps[:, n % NMB, :].rearrange("p (h s q) -> p s h q", h=4, s=2), ACT.Copy).then_inc(q_hi_done, 1)

            def out(b):
                for w in range(NU):
                    if w == 0:
                        act.wait_ge(pv_done, b * KT + LAG + 2)
                    nc.scalar.activation(u_sb[:, unit(w)], pv_ps[:, w, :], ACT.Copy).then_inc(u_done, 1)

            split(0, 16)
            for n, op in enumerate(PROLOGUE):
                if op[0] == "Q":
                    queries(op[1], 0, 0, n)
            act.wait_ge(const_done, 1)
            with act.Fori(0, B // UN) as t:
                for u in range(UN):
                    b = t * UN + u
                    act.wait_ge(score_ready, b * (KT * NU) + 1)
                    split((u + 1) % 2, (t * 2 + (u + 1) // 2) * 16 + 16)
                    for i in range(KT):
                        tile = KT * u + i
                        N = t * (UN * KT) + tile
                        n = row_first(u, i)
                        rows = slice(0, keys(i))
                        for w in range(NU):
                            if w == 0:
                                act.wait_ge(p_hi_done, N + 1)
                                act.wait_ge(p_lo_done, N + 1)
                                act.wait_ge(sums_done, N + 1)
                            act.wait_ge(score_ready, N * NU + w + 2)
                            nc.scalar.activation(probs[rows, tile % NPB, unit(w)], score_ps[rows, (i * NU + w) % NSB, :], ACT.Exp
                                                 ).then_inc(score_free, 1)
                            if w == 0:
                                k = number(u, i, ("V", i))
                                act.wait_ge(misc_ready, t * ROUND + k + 1)
                                act.wait_ge(pv_done, N + 1)
                                nc.scalar.activation(v_sb[rows, tile % NPB, :, 0, :],
                                                     misc_ps[rows, k % NMB, 0:D].rearrange("p (g n) -> p g n", g=NGR),
                                                     ACT.Copy).then_inc(v_hi_done, 1)
                        act.wait_ge(score_free, N * NU + NU + NSB)
                        nc.scalar.activation(p_hi[rows, tile % NPB, :], probs[rows, tile % NPB, :], ACT.Copy
                                             ).then_inc(p_hi_done, 1)
                        if i == LAG - 1:
                            out(b)
                        for k, op in enumerate(PLAN[u][i], n):
                            if op[0] == "Q":
                                queries(op[1], (u // 2 + 1) % 2, t, k)
            out(B)

        @block.gpsimd
        def _(pool):
            pool.sem_inc(sums_done, NPB)
            nc.gpsimd.memset(sums[:, 1, :], 1.0)

            def lo(j, need):
                pool.wait_ge(c_hi_done, need)
                nc.gpsimd.tensor_tensor(c_lo[:, j, :], raw[:, j, :], c_hi[:, j, :].bitcast(F32), ALU.subtract
                                        ).then_inc(c_lo_done, 1)

            lo(0, 1)
            with pool.Fori(0, B // UN) as t:
                for u in range(UN):
                    lo((u + 1) % 2, t * UN + u + 2)
                    for i in range(1, KT):
                        tile = KT * u + i
                        N = t * (UN * KT) + tile
                        rows = slice(0, keys(i))
                        pool.wait_ge(score_free, N * NU + NU + NSB)
                        if i > 1:
                            pool.wait_ge(sums_done, N + NPB)
                        before = probs[rows, (tile - 1) % NPB, :] if i == 1 else sums[rows, u % 2, :]
                        nc.gpsimd.tensor_tensor(sums[rows, u % 2, :], before, probs[rows, tile % NPB, :], ALU.add
                                                ).then_inc(sums_done, 2 if i == 1 else 1)

        @block.vector
        def _(dve):
            dve.sem_inc(misc_free, NMB)
            dve.sem_inc(p_lo_done, NPB - 1)
            nc.vector.memset(ones[:, :].bitcast(F32), 1.0)
            nc.vector.memset(all_ones[:, :], 1.0)
            nc.vector.memset(probs[:, NPB - 1, :], 0.0)
            nc.vector.memset(v_sb[:, NPB - LAG:, :, :, :].bitcast(F32), 0.0)
            nc.vector.memset(p_lo[:, NPB - LAG:, :].bitcast(F32), 0.0)
            nc.vector.memset(p_hi[:, NPB - LAG:, :].bitcast(F32), 0.0).then_inc(const_done, 1)
            dve.wait_ge(const_done, 1)
            dve.wait_ge(w_in, 16 * NW)
            dve.wait_ge(wv_hi_done, 1)
            nc.vector.tensor_tensor(wv_lo[:, :], wv_sb[:, :], wv_hi[:, :].bitcast(F32), ALU.subtract
                                    ).then_inc(wv_done, 1)
            if bo is not None:
                nc.vector.tensor_tensor(x_sb, x_sb, bo_sb[:, :].rearrange("p (a d) -> p a d", a=1).broadcast_to([P, NT, D]),
                                        ALU.add).then_inc(x_biased, 1)
                dve.wait_ge(x_biased, 1)

            def lo(u, t, i):
                tile = KT * u + i
                N = t * (UN * KT) + tile
                rows = slice(0, keys(i))
                dve.wait_ge(p_hi_done, N + NPB + 1)
                nc.vector.tensor_tensor(p_lo[rows, tile % NPB, :], probs[rows, tile % NPB, :],
                                        p_hi[rows, tile % NPB, :].bitcast(F32), ALU.subtract).then_inc(p_lo_done, 1)

            def use(op, u, t, n):
                bank = misc_ps[:, n % NMB, :]
                b = t * UN + u
                dve.wait_ge(misc_ready, t * ROUND + n + 1)
                if op[0] == "Q":
                    s = 0 if u < 0 else (u // 2 + 1) % 2
                    k = op[1]
                    if u < 0:
                        dve.wait_ge(q_hi_done, k + 1)
                    else:
                        dve.wait_ge(q_hi_done, t * (UN // 2 * 4) + 4 + (u // 2) * 4 + k + 1)
                    ins = nc.vector.tensor_tensor(q_lo[:, s, :, 4 * k:4 * k + 4, :],
                                                  bank.rearrange("p (h s q) -> p s h q", h=4, s=2),
                                                  q_hi[:, s, :, 4 * k:4 * k + 4, :].bitcast(F32), ALU.subtract)
                elif op[0] == "V":
                    i = op[1]
                    tile = KT * u + i
                    rows = slice(0, keys(i))
                    dve.wait_ge(v_hi_done, t * (UN * KT) + tile + 1)
                    ins = nc.vector.tensor_tensor(v_sb[rows, tile % NPB, :, 1, :],
                                                  bank[rows, 0:D].rearrange("p (g n) -> p g n", g=NGR),
                                                  v_sb[rows, tile % NPB, :, 0, :].bitcast(F32), ALU.subtract)
                elif op[0] == "M":
                    _, p, w = op
                    ins = nc.vector.tensor_reduce(maxes[:, p, w:w + 1], bank[:, 0:WINDOWS[w][1]], AX.X, ALU.max)
                elif op[0] == "T":
                    ins = nc.vector.tensor_tensor(
                        shift[:, (u + 1) % 2, :, :],
                        bank[0:PAIRS, 0:P].rearrange("r (a c) -> r a c", a=1).broadcast_to([PAIRS, PAIRS, P]),
                        pair_mask[:, :].rearrange("r (a c) -> r a c", c=1).broadcast_to([PAIRS, PAIRS, P]), ALU.mult)
                elif op[0] == "S":
                    ins = nc.vector.reciprocal(recip[:, op[1] * 4:op[1] * 4 + 4],
                                               bank.rearrange("p (a n) -> p a n", n=P)[:, :, 0])
                elif op[0] == "X":
                    for j in range(2):
                        rows = slice(j * LQ, (j + 1) * LQ)
                        for pp in range(2):
                            view = bank.rearrange("p (g n) -> p g n", n=2 * P)[rows, :, pp * P:(pp + 1) * P]
                            col = pp * 2 * DH + j * DH
                            ins = nc.vector.tensor_reduce(
                                o_sb[rows, op[1] * 4 + pp:op[1] * 4 + pp + 3:2, :],
                                view.rearrange("p g (a n) -> p g n a", a=2)[:, :, col:col + DH, :], AX.X, ALU.add)
                elif op[0] == "Y":
                    for j in range(2):
                        ins = nc.vector.tensor_scalar(oT[:, j * LQ:(j + 1) * LQ], bank[:, j * LQ:(j + 1) * LQ],
                                                      bv_sb[:, j:j + 1], None, ALU.add)
                elif op[0] == "Z":
                    half = (u - 1) % 2
                    rows = slice(half * LQ, (half + 1) * LQ)
                    x_t = x_all[rows, ds(t * (UN // 2) + (u + 1) // 2, 1), :].rearrange("p a d -> p (a d)")
                    ins = nc.vector.tensor_tensor(x_t, bank[rows, 0:D], x_t, ALU.add)
                ins.then_inc(misc_free, 1)
                if op[0] == "X":
                    dve.wait_ge(misc_free, t * ROUND + n + NMB + 1)
                    o = o_sb[:, op[1] * 4:op[1] * 4 + 4, :]
                    nc.vector.tensor_tensor(
                        o, o, recip[:, op[1] * 4:op[1] * 4 + 4].rearrange("p (a d) -> p a d", d=1).broadcast_to([P, 4, DH]),
                        ALU.mult).then_inc(o_normed, 1)
                if op[0] == "M" and (op[1], op[2]) == (PAIRS - 1, len(WINDOWS) - 1):
                    dve.wait_ge(misc_free, t * ROUND + n + NMB + 1)
                    nc.vector.tensor_reduce(neg_max[:, :], maxes[:, :, :], AX.X, ALU.max, negate=True
                                            ).then_inc(max_done, 1)

            for n, op in enumerate(PROLOGUE):
                use(op, -1, 0, n)
            with dve.Fori(0, B // UN) as t:
                for u in range(UN):
                    for i in range(KT):
                        for k, op in enumerate(PLAN[u][i]):
                            if k == min(1, len(PLAN[u][i]) - 1):
                                if i == 0:
                                    lo(u - 1, t, KT - 1)
                                else:
                                    lo(u, t, i - 1)
                            use(op, u, t, row_first(u, i) + k)
            end = B // UN
            lo(-1, end, KT - 1)
            for n, op in enumerate(FINISH, FIRST[0]):
                use(op, 0, end, n)


def self_attention(nc, x_sb, ident, a):
    with ExitStack() as ctx:
        sb, ps, sem = alloc(nc, ctx)
        xnT = normed(nc, ctx, "s")
        w_sb = sb("s_w", [P, KD, 3 * D])
        mask = sb("s_mask", [P, 8])
        w_in = sem("s_w_in")

        def loads(sp):
            sp.dma_start(w_sb[:, :, :], a["s_w"]).then_inc(w_in, 16)
            sp.dma_start(mask[:, :], a["s_mask"]).then_inc(w_in, 16)

        layer_norm(nc, "ln_s", x_sb, xnT, ident, loads=loads)
        xt = sb("s_xt", [P, 2, KD, P])
        qz = sb("s_qz", [P, 2, 2, 8, LQ])
        kT = sb("s_kT", [P, 2, KD, P])
        v_sb = sb("s_v", [P, 2, D + P - 2 * DH])
        neg_max = sb("s_neg_max", [P, PAIRS])
        shifted = sb("s_shifted", [P, PAIRS, LQ])
        probs = sb("s_probs", [P, 2, PAIRS, P])
        pT = sb("s_pT", [P, PAIRS, P])
        total = sb("s_total", [P, 2, PAIRS])
        recip = sb("s_recip", [P, PAIRS])
        o_sb = sb("s_o", [P, H, DH])
        proj_ps = ps("s_proj_ps", [P, 2, NB])
        score_ps = ps("s_score_ps", [P, PAIRS, P])
        pT_ps = ps("s_pT_ps", [P, PAIRS, P])
        pv_ps = ps("s_pv_ps", [P, 2, 4 * P])
        zeroed = sem("s_zeroed")
        xt_done = sem("s_xt_done")
        proj_done = sem("s_proj_done")
        kv_done = sem("s_kv_done")
        q_done = sem("s_q_done")
        score_done = sem("s_score_done")
        max_done = sem("s_max_done")
        shift_done = sem("s_shift_done")
        probs_done = sem("s_probs_done")
        sum_done = sem("s_sum_done")
        trans_done = sem("s_trans_done")
        pT_done = sem("s_pT_done")
        pv_done = sem("s_pv_done")
        recip_done = sem("s_recip_done")
        o_done = sem("s_o_done")
        x_done = sem("s_x_done")
        block = open_block(nc, ctx, sem)

        @block.gpsimd
        def _(pool):
            nc.gpsimd.memset(v_sb[:, :, D:], 0.0)
            nc.gpsimd.memset(probs[:, :, :, :], 0.0).then_inc(zeroed, 1)

            def stage(tile, j, n):
                if n is not None:
                    pool.wait_ge(proj_done, n + 1)
                nc.gpsimd.tensor_copy(xt[:, j, :, :], xnT[:, :, tile]).then_inc(xt_done, 1)

            stage(slice(0, P), 0, None)
            with pool.Fori(0, NT // 2) as t:
                for j in range(2):
                    stage(ds((t * 2 + j + 1) * P, P), (j + 1) % 2, t * 2 + j)

        @block.tensor
        def _(pe):
            def project(j, n):
                pe.wait_ge(xt_done, n)
                pe.wait_ge(q_done, (n - 1) * 2)
                pe.wait_ge(kv_done, n - 1)
                for c in range(2 * KD):
                    for k in range(KD):
                        nc.tensor.matmul(proj_ps[:, 0, c * P:(c + 1) * P], w_sb[:, k, c * P:(c + 1) * P],
                                         xt[:, j, k, :], start=k == 0, stop=k == KD - 1)
                for k in range(KD):
                    ins = nc.tensor.matmul(proj_ps[:, 1, 0:D], xt[:, j, k, :], w_sb[:, k, 2 * D:3 * D],
                                           start=k == 0, stop=k == KD - 1)
                ins.then_inc(proj_done, 1)

            def scores(s, j, n):
                pe.wait_ge(q_done, n)
                pe.wait_ge(shift_done, n - 1)
                for p in range(PAIRS):
                    c, r = p // 4, 2 * (p % 4)
                    ins = nc.tensor.matmul(score_ps[:, p, :],
                                           qz[:, s, c, r:r + 2, :].rearrange("p h q -> p (h q)"),
                                           kT[:, j, c, :], start=True, stop=True)
                ins.then_inc(score_done, 1)

            pe.sem_inc(proj_done, 1)
            pe.sem_inc(pv_done, 1)
            pe.sem_inc(pT_done, 1)
            pe.sem_inc(o_done, 2)
            pe.wait_ge(w_in, 32)
            project(0, 1)
            pe.wait_ge(kv_done, 1)
            scores(0, 0, 1)
            with pe.Fori(0, NT // 2) as t:
                for j in range(2):
                    for s in range(2):
                        b = t * 4 + j * 2 + s
                        pe.wait_ge(probs_done, b + 1)
                        pe.wait_ge(pT_done, b + 1)
                        for p in range(PAIRS):
                            ins = nc.tensor.transpose(pT_ps[:, p, :], probs[:, s, p, :], ident[:, :])
                        ins.then_inc(trans_done, 1)
                        if s == 0:
                            scores(1, j, b + 2)
                            project((j + 1) % 2, t * 2 + j + 2)
                        else:
                            pe.wait_ge(kv_done, t * 2 + j + 2)
                            scores(0, (j + 1) % 2, b + 2)
                        pe.wait_ge(pT_done, b + 2)
                        pe.wait_ge(o_done, b * 2 + 2)
                        for p in range(PAIRS):
                            c = p // 4
                            ins = nc.tensor.matmul(pv_ps[:, c, (p % 4) * P:(p % 4 + 1) * P], pT[:, p, :],
                                                   v_sb[:, j, p * 2 * DH:p * 2 * DH + P], start=True, stop=True)
                        ins.then_inc(pv_done, 1)

        @block.scalar
        def _(act):
            def keys_values(j, n):
                act.wait_ge(proj_done, n + 1)
                nc.scalar.activation(kT[:, j, :, :].rearrange("p c n -> p (c n)"), proj_ps[:, 0, D:2 * D], ACT.Copy)
                nc.scalar.activation(v_sb[:, j, 0:D], proj_ps[:, 1, 0:D], ACT.Copy).then_inc(kv_done, 1)

            def exps(s, n):
                act.wait_ge(shift_done, n)
                act.wait_ge(trans_done, n - 1)
                act.wait_ge(sum_done, n - 1)
                nc.scalar.activation(probs[:, s, :, s * LQ:(s + 1) * LQ], shifted[:, :, :], ACT.Exp
                                     ).then_inc(probs_done, 1)

            act.wait_ge(zeroed, 1)
            keys_values(0, 1)
            exps(0, 1)
            with act.Fori(0, NT // 2) as t:
                for j in range(2):
                    for s in range(2):
                        b = t * 4 + j * 2 + s
                        act.wait_ge(trans_done, b + 1)
                        act.wait_ge(pv_done, b + 1)
                        nc.scalar.activation(pT[:, :, :], pT_ps[:, :, :], ACT.Copy).then_inc(pT_done, 1)
                        if s == 0:
                            exps(1, b + 2)
                            keys_values((j + 1) % 2, t * 2 + j + 2)
                        else:
                            exps(0, b + 2)

        @block.vector
        def _(dve):
            def queries(s, n):
                for c in range(KD):
                    ins = nc.vector.tensor_tensor(
                        qz[:, s, c, :, :],
                        proj_ps[:, 0, c * P + s * LQ:c * P + (s + 1) * LQ].rearrange("p (h q) -> p h q", h=1)
                        .broadcast_to([P, 8, LQ]),
                        mask[:, :].rearrange("p (h q) -> p h q", q=1).broadcast_to([P, 8, LQ]), ALU.mult)
                ins.then_inc(q_done, 1)

            def shift(s, n):
                dve.wait_ge(score_done, n)
                own = score_ps[:, :, s * LQ:(s + 1) * LQ]
                nc.vector.tensor_reduce(neg_max[:, :], own, AX.X, ALU.max).then_inc(max_done, 1)
                dve.wait_ge(max_done, n)
                dve.wait_ge(probs_done, n - 1)
                nc.vector.tensor_tensor(shifted[:, :, :], own,
                                        neg_max[:, :].rearrange("p (a q) -> p a q", q=1).broadcast_to([P, PAIRS, LQ]),
                                        ALU.subtract).then_inc(shift_done, 1)

            def sums(s, n):
                dve.wait_ge(probs_done, n)
                nc.vector.tensor_reduce(total[:, s, :], probs[:, s, :, s * LQ:(s + 1) * LQ], AX.X, ALU.add
                                        ).then_inc(sum_done, 1)

            dve.sem_inc(x_done, 1)
            dve.wait_ge(w_in, 32)
            dve.wait_ge(kv_done, 1)
            queries(0, 1)
            queries(1, 2)
            shift(0, 1)
            with dve.Fori(0, NT // 2) as t:
                for j in range(2):
                    for s in range(2):
                        b = t * 4 + j * 2 + s
                        sums(s, b + 1)
                        shift((s + 1) % 2, b + 2)
                        if s == 0:
                            dve.wait_ge(kv_done, t * 2 + j + 2)
                            queries(0, b + 3)
                            queries(1, b + 4)
                        dve.wait_ge(sum_done, b + 1)
                        nc.vector.reciprocal(recip[:, :], total[:, s, :]).then_inc(recip_done, 1)
                        dve.wait_ge(recip_done, b + 1)
                        dve.wait_ge(pv_done, b + 2)
                        dve.wait_ge(x_done, b + 1)
                        for half in range(2):
                            rows = slice(half * LQ, (half + 1) * LQ)
                            out = pv_ps[rows, :, :].rearrange("p c (a n) -> p (c a) n", n=P)
                            nc.vector.tensor_tensor(
                                o_sb[s * LQ:(s + 1) * LQ, half::2, :], out[:, :, half * DH:(half + 1) * DH],
                                recip[rows, :].rearrange("p (a d) -> p a d", d=1).broadcast_to([LQ, PAIRS, DH]),
                                ALU.mult).then_inc(o_done, 1)
                        dve.wait_ge(o_done, b * 2 + 4)
                        rows = slice(s * LQ, (s + 1) * LQ)
                        x_t = x_sb[rows, ds(t * 2 + j, 1), :].rearrange("p a d -> p (a d)")
                        nc.vector.tensor_tensor(x_t, x_t, o_sb[rows, :, :].rearrange("p h d -> p (h d)"), ALU.add
                                                ).then_inc(x_done, 1)


def experts(nc, x_sb, ident, a):
    with ExitStack() as ctx:
        sb, ps, sem = alloc(nc, ctx)
        w1 = sb("m_w1", [P, NE, KD, DE])
        w2 = sb("m_w2", [P, NE, KD, DE])
        w3 = sb("m_w3", [P, NE, EC, D])
        rms_w = sb("m_rms_w", [P, KD])
        prob = sb("m_prob", [P, 2, NT])
        slot = sb("m_slot", [P, 2, NT], U32)
        block_expert = sb("m_block_expert", [P, SLOT_BLOCKS], I32)
        slot_rows = nc.dram_tensor("m_slot_rows", (SLOT_BLOCKS * P, D), F32, kind="Internal").ap()
        slot_out = nc.dram_tensor("m_slot_out", (SLOT_BLOCKS * P, D), F32, kind="Internal").ap()
        rms_in = sem("m_rms_in")
        w_in = sem("m_w_in")
        zeroed = sem("m_zeroed")
        zero_out = sem("m_zero_out")
        scattered = sem("m_scattered")
        stored = [sem(f"m_stored{j}") for j in range(2)]
        with ExitStack() as inner:
            route(nc, inner, x_sb, ident, a, w1, w2, w3, rms_w, prob, slot, block_expert, slot_rows,
                  rms_in, w_in, zeroed, zero_out, scattered)
        with ExitStack() as inner:
            expert_blocks(nc, inner, ident, w1, w2, w3, rms_w, block_expert, slot_rows, slot_out,
                          w_in, scattered, stored)
        sb, ps, inner_sem = alloc(nc, ctx)
        back = sb("m_back", [P, NT, 2, D])
        GROUP = 4
        gathered = [sem(f"m_gathered{g}") for g in range(NT // GROUP)]
        first_added = sem("m_first_added")
        block = open_block(nc, ctx, sem)

        @block.gpsimd
        def _(pool):
            for j in range(2):
                pool.wait_ge(stored[j], 16 * ((SLOT_BLOCKS + 1 - j) // 2))
            for t in range(NT):
                for i in range(2):
                    nc.gpsimd.indirect_dma_start(back[:, t, i, :], None, slot_out,
                                                 bass.IndirectOffsetOnAxis(ap=slot[:, i, t:t + 1], axis=0)
                                                 ).then_inc(gathered[t // GROUP], 16)

        @block.vector
        def _(dve):
            for t in range(NT):
                if t % GROUP == 0:
                    dve.wait_ge(gathered[t // GROUP], 16 * 2 * GROUP)
                nc.vector.scalar_tensor_tensor(x_sb[:, t, :], back[:, t, 0, :], prob[:, 0, t:t + 1], x_sb[:, t, :],
                                               ALU.mult, ALU.add).then_inc(first_added, 1)
                if t > 0:
                    dve.wait_ge(first_added, t)
                    nc.vector.scalar_tensor_tensor(x_sb[:, t - 1, :], back[:, t - 1, 1, :], prob[:, 1, t - 1:t],
                                                   x_sb[:, t - 1, :], ALU.mult, ALU.add)
            dve.wait_ge(first_added, NT)
            nc.vector.scalar_tensor_tensor(x_sb[:, NT - 1, :], back[:, NT - 1, 1, :], prob[:, 1, NT - 1:NT],
                                           x_sb[:, NT - 1, :], ALU.mult, ALU.add)


def route(nc, ctx, x_sb, ident, a, w1, w2, w3, rms_w, prob, slot, block_expert, slot_rows,
          rms_in, w_in, zeroed, zero_out, scattered):
    sb, ps, sem = alloc(nc, ctx)
    xnT = normed(nc, ctx, "m")
    rows = sb("m_rows", [P, NT, D])
    zero = sb("m_zero", [P, D])
    gate_w = sb("m_gate_w", [P, KD, NE])
    const = sb("m_const", [P, M_CONST])
    cols = {}
    at = 0
    for name, n in M_CONST_PARTS:
        cols[name] = const[:, at:at + n]
        at += n
    c_in = sem("m_c_in")
    with nc.Block() as block:
        @block.vector
        def _(dve):
            nc.vector.memset(zero[:, :], 0.0).then_inc(zeroed, 1)

        @block.sync
        def _(sp):
            sp.dma_start(rms_w[:, :], a["m_rms_w"]).then_inc(rms_in, 16)
            sp.dma_start(gate_w[:, :, :], a["m_gate_w"]).then_inc(c_in, 16)
            sp.dma_start(const[:, :], a["m_const"]).then_inc(c_in, 16)
            sp.wait_ge(rms_in, 16)
            sp.wait_ge(c_in, 32)
    def loads(sp):
        sp.wait_ge(zeroed, 1)
        sp.dma_start(slot_rows.rearrange("(b p) d -> p b d", p=P),
                     zero[:, :].rearrange("p (b d) -> p b d", b=1).broadcast_to([P, SLOT_BLOCKS, D])
                     ).then_inc(zero_out, 16)
        for e in range(NE):
            for dst, src in ((w1, a["m_w1"]), (w2, a["m_w2"]), (w3, a["m_w3"])):
                sp.dma_start(dst[:, e, :, :], src[e, :, :, :]).then_inc(w_in, 16)

    layer_norm(nc, "ln_m", x_sb, xnT, ident, rms=rms_w, rows=rows, loads=loads)

    logits = sb("m_logits", [P, NT, NE])
    top = sb("m_top", [P, 2, NT])
    best_at = sb("m_best_at", [P, 2, NT])
    first = sb("m_first", [P, NT, NE])
    second = sb("m_second", [P, NT, NE])
    cand = sb("m_cand", [P, NT, NE])
    gap = sb("m_gap", [P, NT])
    expo = sb("m_expo", [P, NT])
    denom = sb("m_denom", [P, NT])
    both = sb("m_both", [P, NE, NT])
    upto = sb("m_upto", [P, NE, NT])
    before = sb("m_before", [P, NE, NT])
    count = sb("m_count", [P, NE])
    over = sb("m_over", [P, NE, NT])
    blocks = sb("m_blocks", [P, NE])
    block_end = sb("m_block_end", [P, NE])
    base = sb("m_base", [P, NE])
    place = sb("m_place", [P, NE, NT])
    mine = sb("m_mine", [P, 2, NE, NT])
    slot_f = sb("m_slot_f", [P, 2, NT])
    ended = sb("m_ended", [P, SLOT_BLOCKS, NE])
    expert_f = sb("m_expert_f", [P, SLOT_BLOCKS])
    gate_ps = ps("m_gate_ps", [P, NB])
    prefix_ps = ps("m_prefix_ps", [P, NB])
    count_ps = ps("m_count_ps", [P, NB])
    logits_done = sem("m_logits_done")
    gap_done = sem("m_gap_done")
    e_done = sem("m_e_done")
    before_done = sem("m_before_done")
    prefix_done = sem("m_prefix_done")
    slot_done = sem("m_slot_done")
    seq = sem("m_seq")
    block = open_block(nc, ctx, sem)

    @block.tensor
    def _(pe):
        for t in range(NT):
            for k in range(KD):
                ins = nc.tensor.matmul(gate_ps[:, t * NE:(t + 1) * NE], xnT[:, k, t * P:(t + 1) * P],
                                       gate_w[:, k, :], start=k == 0, stop=k == KD - 1)
        ins.then_inc(logits_done, 1)
        pe.wait_ge(before_done, 1)
        nc.tensor.matmul(prefix_ps[:, 0:NE * NT], cols["rows_before"], both[:, :, :].rearrange("p e t -> p (e t)"),
                         start=True, stop=False)
        nc.tensor.matmul(prefix_ps[:, 0:NE * NT], cols["ones"], before[:, :, :].rearrange("p e t -> p (e t)"),
                         start=False, stop=True)
        nc.tensor.matmul(count_ps[:, 0:NE], cols["ones"], upto[:, :, NT - 1], start=True, stop=True
                         ).then_inc(prefix_done, 1)

    @block.scalar
    def _(act):
        act.wait_ge(gap_done, 1)
        nc.scalar.activation(expo[:, :], gap[:, :], ACT.Exp).then_inc(e_done, 1)

    @block.vector
    def _(dve):
        n = 0

        def link(ins):
            nonlocal n
            n += 1
            ins.then_inc(seq, 1)
            dve.wait_ge(seq, n)

        def over_experts(v):
            return v.rearrange("p (t e) -> p t e", e=1).broadcast_to([P, NT, NE])

        def over_tiles(v):
            return v.rearrange("p (e t) -> p e t", t=1).broadcast_to([P, NE, NT])

        def best(values, i, hot):
            link(nc.vector.tensor_reduce(top[:, i, :], values[:, :, :], AX.X, ALU.max))
            link(nc.vector.tensor_tensor(cand[:, :, :], values[:, :, :], over_experts(top[:, i, :]), ALU.is_equal))
            link(nc.vector.tensor_tensor(cand[:, :, :], cand[:, :, :], experts_all, ALU.mult))
            link(nc.vector.tensor_reduce(best_at[:, i, :], cand[:, :, :], AX.X, ALU.min))
            link(nc.vector.tensor_tensor(hot[:, :, :], experts_all, over_experts(best_at[:, i, :]), ALU.is_equal))

        experts_all = cols["experts"].rearrange("p (t e) -> p t e", t=1).broadcast_to([P, NT, NE])
        dve.wait_ge(logits_done, 1)
        link(nc.vector.tensor_copy(logits[:, :, :].rearrange("p t e -> p (t e)"), gate_ps[:, 0:NT * NE]))
        best(logits, 0, first)
        link(nc.vector.scalar_tensor_tensor(logits[:, :, :], first[:, :, :], -FLT_MAX, logits[:, :, :],
                                            ALU.mult, ALU.add))
        best(logits, 1, second)
        nc.vector.tensor_tensor(gap[:, :], top[:, 1, :], top[:, 0, :], ALU.subtract).then_inc(gap_done, 1)
        link(nc.vector.tensor_tensor(both[:, :, :].rearrange("p e t -> p t e"), first[:, :, :], second[:, :, :], ALU.add))
        link(nc.vector.tensor_tensor_scan(upto[:, :, :].rearrange("p e t -> p (e t)"), cols["tile_chain"],
                                          both[:, :, :].rearrange("p e t -> p (e t)"), 0.0, ALU.mult, ALU.add))
        nc.vector.tensor_tensor(before[:, :, :], upto[:, :, :], both[:, :, :], ALU.subtract).then_inc(before_done, 1)
        dve.wait_ge(e_done, 1)
        link(nc.vector.tensor_scalar(denom[:, :], expo[:, :], 1.0, None, ALU.add))
        link(nc.vector.reciprocal(prob[:, 0, :], denom[:, :]))
        link(nc.vector.tensor_tensor(prob[:, 1, :], expo[:, :], prob[:, 0, :], ALU.mult))
        dve.wait_ge(prefix_done, 1)
        link(nc.vector.tensor_copy(count[:, :], count_ps[:, 0:NE]))
        link(nc.vector.tensor_tensor(over[:, :, :], over_tiles(count[:, :]),
                                     cols["whole_blocks"].rearrange("p (e t) -> p e t", e=1).broadcast_to([P, NE, NT]),
                                     ALU.is_gt))
        link(nc.vector.tensor_reduce(blocks[:, :], over[:, :, :], AX.X, ALU.add))
        link(nc.vector.tensor_tensor_scan(block_end[:, :], cols["ones"][:, 0:NE], blocks[:, :], 0.0, ALU.mult, ALU.add))
        link(nc.vector.tensor_tensor(base[:, :], block_end[:, :], blocks[:, :], ALU.subtract))
        link(nc.vector.tensor_scalar(base[:, :], base[:, :], float(P), None, ALU.mult))
        link(nc.vector.tensor_tensor(place[:, :, :], prefix_ps[:, 0:NE * NT].rearrange("p (e t) -> p e t", e=NE),
                                     over_tiles(base[:, :]), ALU.add))
        for i, hot in enumerate((first, second)):
            link(nc.vector.tensor_tensor(mine[:, i, :, :], place[:, :, :], hot[:, :, :].rearrange("p t e -> p e t"),
                                         ALU.mult))
            link(nc.vector.tensor_reduce(slot_f[:, i, :], mine[:, i, :, :].rearrange("p e t -> p t e"), AX.X, ALU.add))
        nc.vector.tensor_copy(slot[:, :, :], slot_f[:, :, :]).then_inc(slot_done, 1)
        link(nc.vector.tensor_tensor(
            ended[:, :, :], block_end[:, :].rearrange("p (b e) -> p b e", b=1).broadcast_to([P, SLOT_BLOCKS, NE]),
            cols["blocks"].rearrange("p (b e) -> p b e", e=1).broadcast_to([P, SLOT_BLOCKS, NE]), ALU.is_le))
        link(nc.vector.tensor_reduce(expert_f[:, :], ended[:, :, :], AX.X, ALU.add))
        link(nc.vector.tensor_scalar(expert_f[:, :], expert_f[:, :], float(NE - 1), None, ALU.min))
        nc.vector.tensor_copy(block_expert[:, :], expert_f[:, :])

    @block.gpsimd
    def _(pool):
        pool.wait_ge(zero_out, 16)
        pool.wait_ge(slot_done, 1)
        for t in range(NT):
            for i in range(2):
                nc.gpsimd.indirect_dma_start(slot_rows, bass.IndirectOffsetOnAxis(ap=slot[:, i, t:t + 1], axis=0),
                                             rows[:, t, :], None).then_inc(scattered, 16)
        pool.wait_ge(scattered, 16 * 2 * NT)


def expert_blocks(nc, ctx, ident, w1, w2, w3, rms_w, block_expert, slot_rows, slot_out, w_in, scattered, stored):
    sb, ps, sem = alloc(nc, ctx)
    HN = DE // 2
    rows = sb("m_block_rows", [P, 2, D])
    yT = sb("m_yT", [P, 2, KD, P])
    gate = sb("m_gate", [P, 2, HN])
    h = sb("m_h", [P, 2, HN])
    hT = sb("m_hT", [P, EC, P])
    out = sb("m_out", [P, 2, D])
    yT_ps = ps("m_yT_ps", [P, NB])
    up_ps = ps("m_up_ps", [P, 2, NB])
    mul_ps = ps("m_mul_ps", [P, 2, NB])
    hT_ps = ps("m_hT_ps", [P, 2, NB])
    out_ps = ps("m_out_ps", [P, NB])
    rows_in = [sem(f"m_rows_in{j}") for j in range(2)]
    rows_turned = sem("m_rows_turned")
    yT_done = sem("m_yT_done")
    up_done = sem("m_up_done")
    gate_done = sem("m_gate_done")
    h_done = sem("m_h_done")
    h_turned = sem("m_h_turned")
    hT_done = sem("m_hT_done")
    out_made = sem("m_out_made")
    out_done = sem("m_out_done")
    block = open_block(nc, ctx, sem)
    LAST = SLOT_BLOCKS - 1
    LOOPED = (SLOT_BLOCKS - 2) // 2
    CB = NB // P

    def steps(engine, step):
        for b in range(2):
            step(0, b, b)
        with engine.Fori(1, LOOPED) as pair:
            for j in range(2):
                step(pair, j, None)
        for b in range(2 * LOOPED, SLOT_BLOCKS):
            step(b // 2, b % 2, b)

    def exists(b, ahead):
        return b is None or b + ahead <= LAST

    @block.sync
    def _(sp):
        def load(first, j):
            sp.dma_start(rows[:, j, :], slot_rows.rearrange("(b p) d -> b p d", p=P)[ds(first + j, 1), :, :]
                         .rearrange("b p d -> p (b d)")).then_inc(rows_in[j], 16)

        def step(pair, j, b):
            n = pair * 2 + j
            if exists(b, 2):
                sp.wait_ge(rows_turned, n + 1)
                load(pair * 2 + 2, j)
            sp.wait_ge(out_done, n + 1)
            sp.dma_start(slot_out.rearrange("(b p) d -> b p d", p=P)[ds(n, 1), :, :].rearrange("b p d -> p (b d)"),
                         out[:, j, :]).then_inc(stored[j], 16)

        for j in range(2):
            load(0, j)
        steps(sp, step)

    @block.tensor
    def _(pe):
        def turn_rows(pair, j):
            n = pair * 2 + j
            pe.wait_ge(rows_in[j], pair * 16 + 16)
            pe.wait_ge(yT_done, n)
            for c in range(KD):
                ins = nc.tensor.transpose(yT_ps[:, c * P:(c + 1) * P], rows[:, j, c * P:(c + 1) * P], ident[:, :])
            ins.then_inc(rows_turned, 1)

        def products(pair, j):
            n = pair * 2 + j
            e = pe.value_load(block_expert[0:1, ds(n, 1)], min_val=0, max_val=NE - 1)
            pe.wait_ge(yT_done, n + 1)
            pe.wait_ge(h_done, n)
            for dst, w in ((up_ps, w1), (mul_ps, w2)):
                for half in range(2):
                    for k in range(KD):
                        ins = nc.tensor.matmul(
                            dst[:, half, 0:HN], yT[:, j, k, :],
                            w[:, ds(e, 1), k, half * HN:(half + 1) * HN].rearrange("p e n -> p (e n)"),
                            start=k == 0, stop=k == KD - 1)
            ins.then_inc(up_done, 1)

        def step(pair, j, b):
            n = pair * 2 + j
            pe.wait_ge(h_done, n + 1)
            pe.wait_ge(hT_done, n * 2)
            for c in range(EC):
                m = ELAST if c == EC - 1 else P
                ins = nc.tensor.transpose(hT_ps[0:m, c // CB, c % CB * P:(c % CB + 1) * P],
                                          h[:, :, :].rearrange("p a n -> p (a n)")[:, c * P:c * P + m], ident[:, :])
                if c in (CB - 1, EC - 1):
                    ins.then_inc(h_turned, 1)
            if exists(b, 1):
                products(pair + (1 if j else 0), 1 - j)
            if exists(b, 2):
                turn_rows(pair + 1, j)
            e = pe.value_load(block_expert[0:1, ds(n, 1)], min_val=0, max_val=NE - 1)
            pe.wait_ge(hT_done, n * 2 + 2)
            pe.wait_ge(out_done, n)
            for c in range(EC):
                m = ELAST if c == EC - 1 else P
                ins = nc.tensor.matmul(out_ps[:, 0:D], hT[0:m, c, :],
                                       w3[0:m, ds(e, 1), c, :].rearrange("p e n -> p (e n)"),
                                       start=c == 0, stop=c == EC - 1)
            ins.then_inc(out_made, 1)

        turn_rows(0, 0)
        turn_rows(0, 1)
        pe.wait_ge(w_in, 16 * 3 * NE)
        products(0, 0)
        steps(pe, step)

    @block.scalar
    def _(act):
        def take_rows(n, j):
            act.wait_ge(rows_turned, n + 1)
            for c in range(KD):
                ins = nc.scalar.activation(yT[:, j, c, :], yT_ps[:, c * P:(c + 1) * P], ACT.Copy, scale=rms_w[:, c:c + 1])
            ins.then_inc(yT_done, 1)

        def silu(n):
            act.wait_ge(up_done, n + 1)
            act.wait_ge(h_done, n)
            nc.scalar.activation(gate[:, :, :], up_ps[:, :, 0:HN], ACT.Silu).then_inc(gate_done, 1)

        def step(pair, j, b):
            n = pair * 2 + j
            act.wait_ge(h_turned, n * 2 + 1)
            act.wait_ge(out_made, n)
            nc.scalar.activation(hT[:, 0:CB, :].rearrange("p c n -> p (c n)"), hT_ps[:, 0, :], ACT.Copy
                                 ).then_inc(hT_done, 1)
            if exists(b, 1):
                silu(n + 1)
            if exists(b, 2):
                take_rows(n + 2, j)

        take_rows(0, 0)
        take_rows(1, 1)
        silu(0)
        steps(act, step)

    @block.vector
    def _(dve):
        def hidden(n):
            dve.wait_ge(gate_done, n + 1)
            dve.wait_ge(h_turned, n * 2)
            nc.vector.tensor_tensor(h[:, :, :], mul_ps[:, :, 0:HN], gate[:, :, :], ALU.mult).then_inc(h_done, 1)

        def step(pair, j, b):
            n = pair * 2 + j
            dve.wait_ge(h_turned, n * 2 + 2)
            dve.wait_ge(out_made, n)
            nc.vector.tensor_copy(hT[:, CB, :], hT_ps[:, 1, 0:P])
            nc.vector.tensor_copy(hT[0:ELAST, CB + 1, :], hT_ps[0:ELAST, 1, P:2 * P]).then_inc(hT_done, 1)
            if exists(b, 1):
                hidden(n + 1)
            dve.wait_ge(out_made, n + 1)
            if b is None or b > 1:
                dve.wait_ge(stored[j], pair * 16)
            nc.vector.tensor_copy(out[:, j, :], out_ps[:, 0:D]).then_inc(out_done, 1)

        hidden(0)
        steps(dve, step)


def mamba(nc, x_sb, ident, a):
    SEQ = B // 2
    HB = HALF // NB
    with ExitStack() as ctx:
        sb, ps, sem = alloc(nc, ctx)
        xpad = sb("b_xpad", [P, CI, B, PADL])
        zs = sb("b_zs", [P, CI, TOK])
        with ExitStack() as inner:
            sb, ps, sem = alloc(nc, inner)
            xnT = normed(nc, inner, "b")
            win = sb("b_win", [P, KD, 2 * DI])
            w_in = sem("b_win_in")

            def loads(sp):
                sp.dma_start(win[:, :, :], a["b_win"]).then_inc(w_in, 16)

            layer_norm(nc, "ln_b", x_sb, xnT, ident, loads=loads)
            xz_ps = ps("b_xz_ps", [P, 2, 2, NB])
            zeroed = sem("b_zeroed")
            x_done = sem("b_x_done")
            z_done = sem("b_z_done")
            x_free = sem("b_x_free")
            z_free = sem("b_z_free")
            block = open_block(nc, inner, sem)
            seq_blk = NB // LQ

            @block.vector
            def _(dve):
                nc.vector.memset(xpad[:, :, :, 0:KC - 1], 0.0)
                nc.vector.memset(xpad[:, :, :, KC - 1 + LQ:], 0.0).then_inc(zeroed, 1)
                for c in range(CI):
                    with dve.Fori(0, NBLK // 2) as pair:
                        for j in range(2):
                            blk = pair * 2 + j
                            dve.wait_ge(x_done, pair * 2 + c * NBLK + j + 1)
                            nc.vector.tensor_copy(xpad[:, c, ds(blk * seq_blk, seq_blk), KC - 1:KC - 1 + LQ],
                                                  xz_ps[:, j, 0, :].rearrange("p (s l) -> p s l", l=LQ)
                                                  ).then_inc(x_free, 1)

            @block.scalar
            def _(act):
                for c in range(CI):
                    with act.Fori(0, NBLK // 2) as pair:
                        for j in range(2):
                            act.wait_ge(z_done, pair * 2 + c * NBLK + j + 1)
                            nc.scalar.activation(zs[:, c, ds((pair * 2 + j) * NB, NB)], xz_ps[:, j, 1, :], ACT.Silu
                                                 ).then_inc(z_free, 1)

            @block.tensor
            def _(pe):
                pe.wait_ge(w_in, 16)
                pe.sem_inc(x_free, 2)
                pe.sem_inc(z_free, 2)
                for c in range(CI):
                    with pe.Fori(0, NBLK // 2) as pair:
                        for j in range(2):
                            for i, (free, done) in enumerate(((x_free, x_done), (z_free, z_done))):
                                pe.wait_ge(free, pair * 2 + c * NBLK + j + 1)
                                for k in range(KD):
                                    ins = nc.tensor.matmul(
                                        xz_ps[:, j, i, :], win[:, k, i * DI + c * P:i * DI + (c + 1) * P],
                                        xnT[:, k, ds((pair * 2 + j) * NB, NB)], start=k == 0, stop=k == KD - 1)
                                ins.then_inc(done, 1)

        for d, tag in enumerate(("f", "r")):
            with ExitStack() as inner:
                sb, ps, sem = alloc(nc, inner)
                wx = sb(f"b{tag}_wx", [P, CI, R + 2 * NS])
                wdt = sb(f"b{tag}_wdt", [R, DI])
                wout = sb(f"b{tag}_wout", [P, CI, D])
                vecs = sb(f"b{tag}_vecs", [P, CI, KC + 3])
                a_log = sb(f"b{tag}_a_log", [P, CI, NS])
                a_neg = sb(f"b{tag}_a_neg", [P, CI, NS])
                xc = sb(f"b{tag}_xc", [P, CI, HALF])
                dt = sb(f"b{tag}_dt", [P, CI, HALF])
                dtx = sb(f"b{tag}_dtx", [P, CI, HALF])
                xdbl = sb(f"b{tag}_xdbl", [R + 2 * NS, HALF])
                b_all = sb(f"b{tag}_b_all", [P, 2, HALF])
                c_all = sb(f"b{tag}_c_all", [P, 2, HALF])
                decay = sb(f"b{tag}_decay", [P, 2, HALF])
                drive = sb(f"b{tag}_drive", [P, 2, HALF])
                state = sb(f"b{tag}_state", [P, 2, HALF])
                read = sb(f"b{tag}_read", [P, 2, HALF])
                zero = sb(f"b{tag}_zero", [P, NB])
                scratch = nc.dram_tensor(f"b{tag}_scratch", (2, 2 * NS, HALF), F32, kind="Internal").ap()
                acc_ps = ps(f"b{tag}_acc_ps", [P, CI * HB, NB])
                w_in = sem(f"b{tag}_w_in")
                rows_out = sem(f"b{tag}_rows_out")
                bc_in = [sem(f"b{tag}_bc_in{j}") for j in range(2)]
                seq = sem(f"b{tag}_seq")
                conv_done = sem(f"b{tag}_conv_done")
                xc_done = sem(f"b{tag}_xc_done")
                dbl_done = sem(f"b{tag}_dbl_done")
                xdbl_done = sem(f"b{tag}_xdbl_done")
                step_done = sem(f"b{tag}_step_done")
                abs_done = sem(f"b{tag}_abs_done")
                exp_done = sem(f"b{tag}_exp_done")
                soft_done = sem(f"b{tag}_soft_done")
                relu_done = sem(f"b{tag}_relu_done")
                dt_done = sem(f"b{tag}_dt_done")
                decay_done = sem(f"b{tag}_decay_done")
                drive_done = sem(f"b{tag}_drive_done")
                state_done = sem(f"b{tag}_state_done")
                read_done = sem(f"b{tag}_read_done")
                acc_done = sem(f"b{tag}_acc_done")
                y_done = sem(f"b{tag}_y_done")
                out_done = sem(f"b{tag}_out_done")
                x_done = sem(f"b{tag}_x_done")
                a_done = sem(f"b{tag}_a_done")
                block = open_block(nc, inner, sem)
                NSTEP = CI * HB
                NCH = NS * CI
                taps = range(KC)
                rev = tag == "r"
                inside = slice(0, LQ - 1) if rev else slice(1, LQ)
                edge = slice(LQ - 1, LQ) if rev else slice(0, 1)
                HT = HALF // P

                def order(ap):
                    return ap[:, ::-1] if rev else ap

                @block.sync
                def _(sp):
                    for dst, name in ((wx, "wx"), (wdt, "wdt"), (wout, "wout"), (vecs, "vecs"), (a_log, "a_log")):
                        src = a["b_wout"] if name == "wout" else a[f"b{tag}_{name}"]
                        sp.dma_start(dst[:], src).then_inc(w_in, 16)
                    with sp.Fori(0, 2) as hf:
                        sp.wait_ge(xdbl_done, hf * HB + HB)
                        sp.dma_start(scratch[ds(hf, 1), :, :].rearrange("h r n -> r (h n)"),
                                     xdbl[R:R + 2 * NS, :]).then_inc(rows_out, 16)
                        with sp.Fori(0, NS // 2) as n2:
                            for j in range(2):
                                if j == 0:
                                    sp.wait_ge(rows_out, hf * 16 + 16)
                                sp.wait_ge(read_done, hf * NCH + n2 * (2 * CI) + j * CI + CI)
                                for dst, row in ((b_all, n2 * 2 + j), (c_all, n2 * 2 + j + NS)):
                                    sp.dma_start(dst[:, j, :],
                                                 scratch[ds(hf, 1), ds(row, 1), :].rearrange("h r n -> (h r n)")
                                                 .partition_broadcast(P)).then_inc(bc_in[j], 16)

                @block.tensor
                def _(pe):
                    pe.wait_ge(w_in, 80)
                    pe.wait_ge(conv_done, 1)
                    pe.sem_inc(out_done, 1)
                    pe.sem_inc(acc_done, 2)
                    with pe.Fori(0, 2) as hf:
                        pe.wait_ge(x_done, hf * HT + 2)
                        pe.wait_ge(xc_done, hf * CI + CI)
                        for blk in range(HB):
                            for c in range(CI):
                                ins = nc.tensor.matmul(acc_ps[0:R + 2 * NS, blk, :], wx[:, c, :],
                                                       xc[:, c, blk * NB:(blk + 1) * NB], start=c == 0, stop=c == CI - 1)
                            ins.then_inc(dbl_done, 1)
                        pe.wait_ge(xdbl_done, hf * HB + HB)
                        for s in range(NSTEP):
                            c, blk = s // HB, s % HB
                            ins = nc.tensor.matmul(acc_ps[:, s, :], wdt[:, c * P:(c + 1) * P],
                                                   xdbl[0:R, blk * NB:(blk + 1) * NB], start=True, stop=True)
                            if blk == HB - 1:
                                ins.then_inc(step_done, 1)
                        pe.wait_ge(dt_done, hf * CI + CI)
                        for s in range(NSTEP):
                            nc.tensor.matmul(acc_ps[:, s, :], ident[:, :], zero[:, :], start=True, stop=True)
                        with pe.Fori(0, NS // 2) as n2:
                            for j in range(2):
                                for c in range(CI):
                                    k = hf * NCH + n2 * (2 * CI) + j * CI + c
                                    pe.wait_ge(read_done, k + 2 * CI + 1)
                                    for blk in range(HB):
                                        ins = nc.tensor.matmul(acc_ps[:, c * HB + blk, :], ident[:, :],
                                                               read[:, c % 2, blk * NB:(blk + 1) * NB],
                                                               start=False, stop=True, skip_group_check=True)
                                    ins.then_inc(acc_done, 1)
                        pe.wait_ge(y_done, hf * CI + CI)
                        for i in range(HT):
                            pe.wait_ge(x_done, hf * HT + i + 1)
                            for c in range(CI):
                                ins = nc.tensor.matmul(acc_ps[:, i % 2, 0:D], dtx[:, c, i * P:(i + 1) * P], wout[:, c, :],
                                                       start=c == 0, stop=c == CI - 1)
                            ins.then_inc(out_done, 1)

                @block.scalar
                def _(act):
                    act.wait_ge(w_in, 80)
                    nc.scalar.activation(a_neg[:, :, :], a_log[:, :, :], ACT.Exp).then_inc(a_done, 1)
                    with act.Fori(0, 2) as hf:
                        for c in range(CI):
                            act.wait_ge(conv_done, hf * CI + 1 + c + 1)
                            nc.scalar.activation(xc[:, c, :], dt[:, c, :], ACT.Silu).then_inc(xc_done, 1)
                        for blk in range(HB):
                            act.wait_ge(dbl_done, hf * HB + blk + 1)
                            nc.scalar.activation(xdbl[:, blk * NB:(blk + 1) * NB], acc_ps[0:R + 2 * NS, blk, :],
                                                 ACT.Copy).then_inc(xdbl_done, 1)
                        act.wait_ge(out_done, hf * HT + 1)
                        for c in range(CI):
                            act.wait_ge(step_done, hf * CI + c + 1)
                            nc.scalar.activation(dtx[:, c, :], acc_ps[:, c * HB:(c + 1) * HB, :].rearrange("p b n -> p (b n)"),
                                                 ACT.Abs, bias=vecs[:, c, KC + 1:KC + 2]).then_inc(abs_done, 1)
                        for c in range(CI):
                            act.wait_ge(abs_done, hf * CI + c + 1)
                            nc.scalar.activation(dtx[:, c, :], dtx[:, c, :], ACT.Exp, scale=-1.0).then_inc(exp_done, 1)
                        for c in range(CI):
                            act.wait_ge(exp_done, hf * CI + c + 1)
                            nc.scalar.activation(dtx[:, c, :], dtx[:, c, :], ACT.Ln, bias=1.0).then_inc(soft_done, 1)
                        act.wait_ge(a_done, 3)
                        act.wait_ge(dt_done, hf * CI + CI)
                        with act.Fori(0, NS // 2) as n2:
                            for j in range(2):
                                for c in range(CI):
                                    k = hf * NCH + n2 * (2 * CI) + j * CI + c
                                    act.wait_ge(state_done, k + 1)
                                    nc.scalar.activation(
                                        decay[:, c % 2, :].rearrange("p (s l) -> p s l", l=LQ)[:, :, inside],
                                        dt[:, c, :].rearrange("p (s l) -> p s l", l=LQ)[:, :, inside], ACT.Exp,
                                        scale=a_neg[:, c, ds(n2 * 2 + j, 1)]).then_inc(decay_done, 1)

                @block.vector
                def _(dve):
                    dve.wait_ge(w_in, 80)
                    for j in range(2):
                        nc.vector.memset(decay[:, j, :].rearrange("p (s l) -> p s l", l=LQ)[:, :, edge], 0.0)
                    nc.vector.memset(zero[:, :], 0.0).then_inc(conv_done, 1)
                    dve.sem_inc(read_done, 2 * CI)
                    dve.sem_inc(state_done, 2)
                    dve.sem_inc(x_done, 2)
                    dve.wait_ge(a_done, 1)
                    nc.vector.tensor_scalar(a_neg[:, :, :], a_neg[:, :, :], -1.0, None, ALU.mult).then_inc(a_done, 2)
                    with dve.Fori(0, 2) as hf:
                        k = [0]
                        CHAIN = CI * (KC - 1) + 2 * CI

                        def link(ins):
                            k[0] += 1
                            ins.then_inc(seq, 1)
                            dve.wait_ge(seq, hf * CHAIN + k[0])

                        for c in range(CI):
                            if c == 0:
                                dve.wait_ge(out_done, hf * HT + 1)
                            acc = dt[:, c, :].rearrange("p (s l) -> p s l", l=LQ)

                            def window(tap):
                                off = KC - 1 + (KC - 1 - tap if rev else tap - (KC - 1))
                                return xpad[:, c, ds(hf * SEQ, SEQ), off:off + LQ]

                            link(nc.vector.tensor_scalar(acc, window(0), vecs[:, c, 0:1], vecs[:, c, KC:KC + 1],
                                                         ALU.mult, ALU.add))
                            for tap in range(1, KC):
                                ins = nc.vector.scalar_tensor_tensor(acc, window(tap), vecs[:, c, tap:tap + 1], acc,
                                                                     ALU.mult, ALU.add)
                                if tap < KC - 1:
                                    link(ins)
                                else:
                                    ins.then_inc(conv_done, 1)
                        dve.wait_ge(xc_done, hf * CI + CI)
                        for c in range(CI):
                            dve.wait_ge(abs_done, hf * CI + c + 1)
                            nc.vector.tensor_scalar(dt[:, c, :],
                                                    acc_ps[:, c * HB:(c + 1) * HB, :].rearrange("p b n -> p (b n)"),
                                                    vecs[:, c, KC + 1:KC + 2], 0.0, ALU.add, ALU.max
                                                    ).then_inc(relu_done, 1)
                        for c in range(CI):
                            dve.wait_ge(relu_done, hf * CI + c + 1)
                            dve.wait_ge(soft_done, hf * CI + c + 1)
                            nc.vector.tensor_tensor(dt[:, c, :], dt[:, c, :], dtx[:, c, :], ALU.add
                                                    ).then_inc(dt_done, 1)
                        for c in range(CI):
                            dve.wait_ge(dt_done, hf * CI + c + 1)
                            k[0] += 1
                            nc.vector.tensor_tensor(dtx[:, c, :], dt[:, c, :], xc[:, c, :], ALU.mult).then_inc(seq, 1)
                        DTX = k[0]

                        def make_drive(n2, j, c):
                            if c == 0:
                                if j == 0:
                                    dve.wait_ge(seq, hf * CHAIN + DTX)
                                dve.wait_ge(bc_in[j], n2 * 32 + hf * (NS // 2 * 32) + 32)
                            nc.vector.tensor_tensor(drive[:, c % 2, :], dtx[:, c, :], b_all[:, j, :], ALU.mult
                                                    ).then_inc(drive_done, 1)

                        def turn(n2, last):
                            for j in range(2):
                                for c in range(CI):
                                    kk = n2 * (2 * CI) + hf * NCH + j * CI + c
                                    dve.wait_ge(drive_done, kk + 1)
                                    dve.wait_ge(decay_done, kk + 1)
                                    nc.vector.tensor_tensor_scan(order(state[:, c % 2, :]), order(decay[:, c % 2, :]),
                                                                 order(drive[:, c % 2, :]), 0.0, ALU.mult, ALU.add
                                                                 ).then_inc(state_done, 1)
                                    if c < CI - 1:
                                        make_drive(n2, j, c + 1)
                                    elif j == 0:
                                        make_drive(n2, 1, 0)
                                    elif not last:
                                        make_drive(n2 + 1, 0, 0)
                                    dve.wait_ge(state_done, kk + 3)
                                    dve.wait_ge(acc_done, kk + 1)
                                    nc.vector.tensor_tensor(read[:, c % 2, :], state[:, c % 2, :], c_all[:, j, :],
                                                            ALU.mult).then_inc(read_done, 1)

                        make_drive(0, 0, 0)
                        with dve.Fori(0, NS // 2 - 1) as n2:
                            turn(n2, False)
                        turn(NS // 2 - 1, True)
                        dve.wait_ge(acc_done, hf * NCH + NCH + 2)
                        for c in range(CI):
                            link(nc.vector.scalar_tensor_tensor(
                                dtx[:, c, :], xc[:, c, :], vecs[:, c, KC + 2:KC + 3],
                                acc_ps[:, c * HB:(c + 1) * HB, :].rearrange("p b n -> p (b n)"), ALU.mult, ALU.add))
                            nc.vector.tensor_tensor(dtx[:, c, :], dtx[:, c, :], zs[:, c, ds(hf * HALF, HALF)], ALU.mult
                                                    ).then_inc(y_done, 1)
                        assert k[0] == CHAIN, (k[0], CHAIN)
                        for i in range(HT):
                            x_t = x_sb[:, ds(hf * HT + i, 1), :].rearrange("p a d -> p (a d)")
                            dve.wait_ge(out_done, hf * HT + i + 2)
                            nc.vector.tensor_tensor(x_t, acc_ps[:, i % 2, 0:D], x_t, ALU.add).then_inc(x_done, 1)


def feed_forward(nc, x_sb, ident, a):
    TOPK = 2
    with ExitStack() as ctx:
        sb, ps, sem = alloc(nc, ctx)
        xnT = normed(nc, ctx, "f")
        wi = sb("f_wi", [P, KD, FF])
        wo = sb("f_wo", [P, CF, D])
        wk = sb("f_wk", [P, TOPK, KD, FF])
        lora_a = sb("f_lora_a", [RANK, TOPK, D])
        lora_b = sb("f_lora_b", [RANK, TOPK, FF])
        index = sb("f_index", [1, TOPK], I32)
        value = sb("f_value", [P, TOPK])
        i_in = sem("f_i_in")
        w_in = sem("f_w_in")
        lora_in = sem("f_lora_in")

        def loads(sp):
            sp.dma_start(index[:, :], a["f_index"]).then_inc(i_in, 16)
            sp.dma_start(wi[:, :, :], a["f_wi"]).then_inc(w_in, 16)
            sp.dma_start(wo[:, :, :], a["f_wo"]).then_inc(w_in, 16)
            sp.dma_start(value[:, :], a["f_value"].partition_broadcast(P)).then_inc(w_in, 16)
            sp.wait_ge(i_in, 16)
            for k in range(TOPK):
                e = sp.value_load(index[0:1, k:k + 1], min_val=0, max_val=NE - 1)
                sp.dma_start(lora_a[:, k, :], a["f_lora_a"][ds(e, 1), :, :].rearrange("e r d -> r (e d)")
                             ).then_inc(lora_in, 16)
                sp.dma_start(lora_b[:, k, :], a["f_lora_b"][ds(e, 1), :, :].rearrange("e r f -> r (e f)")
                             ).then_inc(lora_in, 16)

        layer_norm(nc, "ln_f", x_sb, xnT, ident, loads=loads)
        h0 = sb("f_h0", [P, 2, NB])
        h1 = sb("f_h1", [P, 2, NB])
        h = sb("f_h", [P, CF, NB])
        first_ps = ps("f_first_ps", [P, 2, NB])
        second_ps = ps("f_second_ps", [P, 2, NB])
        out_ps = ps("f_out_ps", [P, 2, NB])
        lora_done = sem("f_lora_done")
        wk_done = sem("f_wk_done")
        up_done = sem("f_up_done")
        h0_done = sem("f_h0_done")
        h1_done = sem("f_h1_done")
        h_done = sem("f_h_done")
        out_done = sem("f_out_done")
        x_done = sem("f_x_done")
        block = open_block(nc, ctx, sem)
        FB = FF // NB

        @block.tensor
        def _(pe):
            for free, n in ((h0_done, 2), (h1_done, 2), (h_done, 2), (x_done, 2), (out_done, 1)):
                pe.sem_inc(free, n)
            pe.wait_ge(lora_in, 16 * 2 * TOPK)
            n = 0
            for k in range(TOPK):
                for c in range(KD):
                    for j in range(FB):
                        pe.wait_ge(wk_done, max(n - 1, 0))
                        nc.tensor.matmul(first_ps[:, n % 2, :], lora_a[:, k, c * P:(c + 1) * P],
                                         lora_b[:, k, j * NB:(j + 1) * NB], start=True, stop=True
                                         ).then_inc(lora_done, 1)
                        n += 1
            pe.wait_ge(wk_done, n)
            with pe.Fori(0, NBLK) as blk:
                for c in range(CF):
                    for k, dst in enumerate((first_ps, second_ps)):
                        pe.wait_ge(h0_done if k == 0 else h1_done, blk * CF + c + 1)
                        for i in range(KD):
                            ins = nc.tensor.matmul(dst[:, c % 2, :], wk[:, k, i, c * P:(c + 1) * P],
                                                   xnT[:, i, ds(blk * NB, NB)], start=i == 0, stop=i == KD - 1)
                        ins.then_inc(up_done, 1)
                pe.wait_ge(h_done, blk * CF + CF + 2)
                for i in range(TPB):
                    pe.wait_ge(x_done, blk * TPB + i + 1)
                    for c in range(CF):
                        ins = nc.tensor.matmul(out_ps[:, i % 2, 0:D], h[:, c, i * P:(i + 1) * P], wo[:, c, :],
                                               start=c == 0, stop=c == CF - 1)
                    ins.then_inc(out_done, 1)

        @block.scalar
        def _(act):
            with act.Fori(0, NBLK) as blk:
                for c in range(CF):
                    act.wait_ge(up_done, blk * (2 * CF) + 2 * c + 2)
                    act.wait_ge(h_done, blk * CF + c + 1)
                    nc.scalar.activation(h1[:, c % 2, :], second_ps[:, c % 2, :], ACT.Relu).then_inc(h1_done, 1)

        @block.vector
        def _(dve):
            dve.wait_ge(w_in, 48)
            n = 0
            for k in range(TOPK):
                for c in range(KD):
                    for j in range(FB):
                        cols = slice(j * NB, (j + 1) * NB)
                        dve.wait_ge(lora_done, n + 1)
                        nc.vector.tensor_tensor(wk[:, k, c, cols], first_ps[:, n % 2, :], wi[:, c, cols], ALU.add
                                                ).then_inc(wk_done, 1)
                        n += 1
            with dve.Fori(0, NBLK) as blk:
                dve.wait_ge(out_done, blk * TPB + 1)
                for c in range(CF):
                    dve.wait_ge(up_done, blk * (2 * CF) + 2 * c + 1)
                    nc.vector.tensor_scalar(h0[:, c % 2, :], first_ps[:, c % 2, :], 0.0, value[:, 0:1],
                                            ALU.max, ALU.mult).then_inc(h0_done, 1)
                    dve.wait_ge(h0_done, blk * CF + c + 3)
                    dve.wait_ge(h1_done, blk * CF + c + 3)
                    nc.vector.scalar_tensor_tensor(h[:, c, :], h1[:, c % 2, :], value[:, 1:2], h0[:, c % 2, :],
                                                   ALU.mult, ALU.add).then_inc(h_done, 1)
                for i in range(TPB):
                    x_t = x_sb[:, ds(blk * TPB + i, 1), :].rearrange("p a d -> p (a d)")
                    dve.wait_ge(out_done, blk * TPB + i + 2)
                    nc.vector.tensor_tensor(x_t, out_ps[:, i % 2, 0:D], x_t, ALU.add).then_inc(x_done, 1)


def program(nc, a, out, phases=6):
    with ExitStack() as ctx:
        sb, ps, sem = alloc(nc, ctx)
        x_all = sb("x_all", [P, NT + 1, D])
        x_sb = x_all[:, 1:, :]
        ident = sb("ident", [P, P])
        pair_mask = sb("pair_mask", [PAIRS, PAIRS])
        x_in = sem("x_in")
        x_out = sem("x_out")
        with nc.Block() as block:
            @block.vector
            def _(dve):
                nc.vector.memset(x_all[:, 0, :], 0.0)

            @block.sync
            def _(sp):
                sp.dma_start(x_sb[:, :, :], a["x"].rearrange("(t p) d -> p t d", p=P)).then_inc(x_in, 16)
                sp.dma_start(ident[:, :], a["ident"]).then_inc(x_in, 16)
                sp.dma_start(pair_mask[:, :], a["ident"][0:PAIRS, 0:PAIRS]).then_inc(x_in, 16)
                sp.wait_ge(x_in, 48)

        def xattn(i):
            w = {k: a[f"x{i}_{k}"] for k in ("wq", "wk", "wv", "wo", "bq", "bv")}
            cross_attention(nc, f"x{i}", x_all, ident, pair_mask, a["ctxT"], bo=a["x0_bo"] if i == 0 else None, **w)

        steps = [lambda: xattn(0),
                 lambda: self_attention(nc, x_sb, ident, a),
                 lambda: experts(nc, x_sb, ident, a),
                 lambda: xattn(1),
                 lambda: mamba(nc, x_sb, ident, a),
                 lambda: feed_forward(nc, x_sb, ident, a)]
        for i in (phases if isinstance(phases, (list, tuple)) else range(phases)):
            steps[i]()
        with nc.Block() as block:
            @block.sync
            def _(sp):
                sp.dma_start(out.rearrange("(t p) d -> p t d", p=P), x_sb[:, :, :]).then_inc(x_out, 16)
                sp.wait_ge(x_out, 16)



def more_layouts(i, arr):
    import numpy as np
    f = np.float32
    arr["s_w"] = i["L0_attn_w_qkv"].reshape(KD, P, 3 * D).transpose(1, 0, 2)
    mask = np.zeros((P, 8), f)
    for r in range(P):
        mask[r, r // DH] = D ** -0.5
    arr["s_mask"] = mask
    arr["m_rms_w"] = i["L0_ffn_rms_w"].reshape(KD, P).T
    arr["m_gate_w"] = i["L0_ffn_gate_w"].T.reshape(KD, P, NE).transpose(1, 0, 2)
    const = {"rows_before": np.triu(np.ones((P, P), f), 1), "ones": np.ones(P, f), "experts": np.arange(NE, dtype=f) - NE,
             "tile_chain": np.tile(np.arange(NT) > 0, NE), "whole_blocks": P * np.arange(NT),
             "blocks": np.arange(SLOT_BLOCKS)}
    arr["m_const"] = np.concatenate([np.broadcast_to(const[k], (P, n)).astype(f) for k, n in M_CONST_PARTS], axis=1)
    for n in (1, 2):
        arr[f"m_w{n}"] = i[f"L0_ffn_W{n}"].transpose(0, 2, 1).reshape(NE, KD, P, DE).transpose(0, 2, 1, 3)
    w3 = np.zeros((NE, EC * P, D), f)
    w3[:, :DE] = i["L0_ffn_W3"].transpose(0, 2, 1)
    arr["m_w3"] = w3.reshape(NE, EC, P, D).transpose(0, 2, 1, 3)
    arr["b_win"] = i["L1_attn_W_in"].T.reshape(KD, P, 2 * DI).transpose(1, 0, 2)
    arr["b_wout"] = i["L1_attn_W_out"].T.reshape(CI, P, D).transpose(1, 0, 2)
    for tag, n in (("f", "fwd"), ("r", "rev")):
        def chunks(v):
            return v.reshape(CI, P, -1).transpose(1, 0, 2)
        arr[f"b{tag}_wx"] = chunks(i[f"L1_attn_Wx_{n}"].T)
        arr[f"b{tag}_wdt"] = i[f"L1_attn_Wdt_{n}"].T
        arr[f"b{tag}_a_log"] = chunks(i[f"L1_attn_A_log_{n}"])
        arr[f"b{tag}_vecs"] = np.concatenate(
            [chunks(i[f"L1_attn_{v}_{n}"]) for v in ("conv_w", "conv_b", "bdt", "D")], axis=2)
    arr["f_wi"] = i["L1_ffn_wi_w"].T.reshape(KD, P, FF).transpose(1, 0, 2)
    arr["f_wo"] = i["L1_ffn_wo_w"].T.reshape(CF, P, D).transpose(1, 0, 2)
    arr["f_lora_a"] = i["L1_ffn_lora_As"]
    arr["f_lora_b"] = i["L1_ffn_lora_Bs"].transpose(0, 2, 1)
    arr["f_index"] = i["L1_ffn_top_k_indices"].reshape(1, 2)
    arr["f_value"] = i["L1_ffn_top_k_values"]


def layouts(inputs):
    import numpy as np
    i = {k: np.asarray(v) for k, v in inputs.items()}
    f = np.float32
    arr = {"x": i["x"].reshape(TOK, D), "ident": np.eye(P, dtype=f)}
    ctxT = np.zeros((B + 2, DC, LKV), f)
    ctxT[:B] = i["ctx_512"].transpose(0, 2, 1)
    arr["ctxT"] = ctxT

    def xattn(n, wq, wk, wv, wo, bq, bv):
        arr[f"x{n}_wq"] = wq.reshape(KD, P, D).transpose(1, 0, 2)
        z = np.zeros((P, H, DC), f)
        for h in range(H):
            r = h % 8 * DH
            z[r:r + DH, h, :] = wk[:, h * DH:(h + 1) * DH].T
        arr[f"x{n}_wk"] = z
        arr[f"x{n}_wv"] = wv
        arr[f"x{n}_bv"] = (bv if bv is not None else np.zeros(D, f)).reshape(PAIRS, 2, DH).transpose(0, 2, 1).reshape(P, 2)
        arr[f"x{n}_wo"] = wo.reshape(PAIRS, 2, DH, D).transpose(0, 2, 1, 3).reshape(P, 2, D)
        arr[f"x{n}_bq"] = (bq if bq is not None else np.zeros(D, f)).reshape(KD, P).T

    xattn(0, i["L0_xattn_Wq"], i["L0_xattn_Wk"], i["L0_xattn_Wv"], i["L0_xattn_Wo"], i["L0_xattn_bq"], i["L0_xattn_bv"])
    arr["x0_bo"] = i["L0_xattn_bo"]
    kv = i["L1_xattn_Wkv"]
    xattn(1, i["L1_xattn_Wq"].T, kv[:D].T, kv[D:].T, i["L1_xattn_Wo"].T, None, None)
    more_layouts(i, arr)
    return {k: np.ascontiguousarray(v) for k, v in arr.items()}


def kernel(**inputs):
    import concourse.bacc as bacc
    from concourse.bass_utils import run_bass_kernel_spmd

    arrays = layouts(inputs)
    nc = bacc.Bacc("TRN2", target_bir_lowering=False, num_devices=1)
    a = {k: nc.dram_tensor(f"in_{k}", v.shape, mybir.dt.from_np(v.dtype), kind="ExternalInput").ap()
         for k, v in arrays.items()}
    out = nc.dram_tensor("out_x", (TOK, D), F32, kind="ExternalOutput").ap()
    program(nc, a, out)
    r = run_bass_kernel_spmd(nc, [{f"in_{k}": v for k, v in arrays.items()}], core_ids=[0])
    return r.results[0]["out_x"].reshape(B, LQ, D)
```

```python
import concourse.bass as bass
from concourse import mybir
from concourse.alu_op_type import AluOpType as ALU
from contextlib import ExitStack

F32 = mybir.dt.float32
F32R = mybir.dt.float32r
U32 = mybir.dt.uint32
I32 = mybir.dt.int32
ACT = mybir.ActivationFunctionType
AX = mybir.AxisListType
ds = bass.ds

P = 128
B, LQ, D = 32, 64, 256
LKV, DC = 1601, 128
H, DH = 16, 16
TOK = B * LQ
NT = TOK // P
KD = D // P
NB = 512
NBLK = TOK // NB
TPB = NB // P
LN_EPS, RMS_EPS = 1e-5, 1e-6

KT = -(-LKV // P)
KLAST = LKV - (KT - 1) * P
PAIRS = H // 2
WINDOWS = [(0, 402), (402, 402), (804, 402), (LKV - 402, 402)]
NE, DE = 8, 704
FLT_MAX = 3.4028234663852886e38
SLOT_BLOCKS = (2 * TOK + NE * (P - 1)) // P
M_CONST_PARTS = [("rows_before", P), ("ones", P), ("experts", NE), ("tile_chain", NE * NT), ("whole_blocks", NT),
                 ("blocks", SLOT_BLOCKS)]
M_CONST = sum(n for _, n in M_CONST_PARTS)
EC = -(-DE // P)
ELAST = DE - (EC - 1) * P
DI, NS, KC, R = 512, 16, 4, 64
CI = DI // P
PADL = LQ + 2 * (KC - 1)
FF, RANK = 1024, 16
CF = FF // P


def alloc(nc, ctx):
    def sb(name, shape, dt=F32):
        return ctx.enter_context(nc.sbuf_tensor(name, shape, dt))

    def ps(name, shape, dt=F32):
        return ctx.enter_context(nc.psum_tensor(name, shape, dt))

    def sem(name):
        s = ctx.enter_context(nc.semaphore(name))
        sem.taken.append(s)
        return s

    sem.taken = []
    return sb, ps, sem


def open_block(nc, ctx, sem):
    def clear(error, *_):
        if error is None:
            with nc.Block() as block:
                @block.sync
                def _(sp):
                    for s in sem.taken:
                        sp.sem_clear(s)

    ctx.push(clear)
    return ctx.enter_context(nc.Block())


def normed(nc, ctx, tag):
    return ctx.enter_context(nc.sbuf_tensor(f"{tag}_xnT", [P, KD, TOK + P], F32))


def layer_norm(nc, tag, x_sb, xnT, ident, rms=None, rows=None, loads=None):
    UT = 4
    with ExitStack() as ctx:
        sb, ps, sem = alloc(nc, ctx)
        stats = sb(f"{tag}_stats", [P, NT, 6])
        moments = sb(f"{tag}_moments", [P, NT, 2])
        std = sb(f"{tag}_std", [P, NT])
        rstd = sb(f"{tag}_rstd", [P, NT])
        eps = sb(f"{tag}_eps", [P, 2])
        xn = sb(f"{tag}_xn", [P, UT, D])
        if rms is not None:
            mean_sq = sb(f"{tag}_mean_sq", [P, NT])
            root = sb(f"{tag}_root", [P, NT])
            scale = sb(f"{tag}_scale", [P, NT])
            gain = sb(f"{tag}_gain", [P, NT])
            offset = sb(f"{tag}_offset", [P, NT])
        xT = ps(f"{tag}_xT", [P, UT, NB])
        stats_done = sem(f"{tag}_stats_done")
        moments_done = sem(f"{tag}_moments_done")
        std_done = sem(f"{tag}_std_done")
        chain = sem(f"{tag}_chain")
        eps_done = sem(f"{tag}_eps_done")
        xn_done = sem(f"{tag}_xn_done")
        transposed = sem(f"{tag}_transposed")
        copied = sem(f"{tag}_copied")
        block = open_block(nc, ctx, sem)

        def tile(t):
            return x_sb[:, ds(t, 1), :].rearrange("p a d -> p (a d)")

        def add_norm(dve, t):
            dve.wait_ge(xn_done, t + 1)
            nc.vector.tensor_scalar(tile(t), tile(t), gain[:, ds(t, 1)], offset[:, ds(t, 1)], ALU.mult, ALU.add)

        @block.sync
        def _(sp):
            if loads is not None:
                loads(sp)

        @block.vector
        def _(dve):
            n = 0

            def link(ins):
                nonlocal n
                n += 1
                ins.then_inc(chain, 1)
                dve.wait_ge(chain, n)

            nc.vector.memset(xnT[:, :, TOK:], 0.0)
            nc.vector.memset(eps[:, 0:1], LN_EPS)
            nc.vector.memset(eps[:, 1:2], RMS_EPS).then_inc(eps_done, 1)
            with dve.Fori(0, NT // UT) as turn:
                for j in range(UT):
                    t = turn * UT + j
                    nc.vector.bn_stats(stats[:, ds(t, 1), :].rearrange("p a s -> p (a s)"), tile(t)
                                       ).then_inc(stats_done, 1)
            dve.wait_ge(stats_done, NT)
            for t in range(NT):
                ins = nc.vector.bn_aggr(moments[:, t, :], stats[:, t, :])
            ins.then_inc(moments_done, 1)
            dve.wait_ge(std_done, 1)
            link(nc.vector.reciprocal(rstd[:, :], std[:, :]))
            by = rstd
            if rms is not None:
                dve.wait_ge(moments_done, 1)
                link(nc.vector.tensor_tensor(mean_sq[:, :], moments[:, :, 1], rstd[:, :], ALU.mult))
                nc.vector.tensor_tensor(mean_sq[:, :], mean_sq[:, :], rstd[:, :], ALU.mult).then_inc(moments_done, 1)
                link(nc.vector.tensor_scalar(gain[:, :], rstd[:, :], 1.0, None, ALU.add))
                link(nc.vector.scalar_tensor_tensor(offset[:, :], moments[:, :, 0], -1.0, rstd[:, :],
                                                    ALU.mult, ALU.mult))
                dve.wait_ge(std_done, 2)
                link(nc.vector.reciprocal(scale[:, :], root[:, :]))
                link(nc.vector.tensor_tensor(scale[:, :], scale[:, :], rstd[:, :], ALU.mult))
                by = scale
            with dve.Fori(0, NT // UT) as turn:
                for j in range(UT):
                    t = turn * UT + j
                    dve.wait_ge(transposed, t + 1)
                    if rms is not None:
                        dve.wait_ge(copied, t + 1)
                    nc.vector.tensor_scalar(xn[:, j, :], tile(t), moments[:, ds(t, 1), 0:1].rearrange("p a s -> p (a s)"),
                                            by[:, ds(t, 1)], ALU.subtract, ALU.mult).then_inc(xn_done, 1)
                    if rms is not None and j > 0:
                        add_norm(dve, t - 1)
                if rms is not None:
                    add_norm(dve, turn * UT + UT - 1)

        @block.scalar
        def _(act):
            act.wait_ge(eps_done, 1)
            act.wait_ge(moments_done, 1)
            nc.scalar.activation(std[:, :], moments[:, :, 1], ACT.Sqrt, bias=eps[:, 0:1]).then_inc(std_done, 1)
            if rms is not None:
                act.wait_ge(moments_done, 2)
                nc.scalar.activation(root[:, :], mean_sq[:, :], ACT.Sqrt, bias=eps[:, 1:2]).then_inc(std_done, 1)
            with act.Fori(0, NT // UT) as turn:
                for j in range(UT):
                    t = turn * UT + j
                    if rms is not None:
                        act.wait_ge(xn_done, t + 1)
                        nc.scalar.activation(rows[:, ds(t, 1), :].rearrange("p a d -> p (a d)"), xn[:, j, :], ACT.Copy)
                    act.wait_ge(transposed, t + UT + 1)
                    if rms is not None:
                        for c in range(KD):
                            ins = nc.scalar.activation(xnT[:, c, ds(t * P, P)], xT[:, j, c * P:(c + 1) * P],
                                                       ACT.Copy, scale=rms[:, c:c + 1])
                    else:
                        ins = nc.scalar.activation(xnT[:, :, ds(t * P, P)],
                                                   xT[:, j, 0:KD * P].rearrange("p (c n) -> p c n", c=KD), ACT.Copy)
                    ins.then_inc(copied, 1)

        @block.tensor
        def _(pe):
            pe.sem_inc(transposed, UT)
            pe.sem_inc(copied, UT)
            with pe.Fori(0, NT // UT) as turn:
                for j in range(UT):
                    t = turn * UT + j
                    pe.wait_ge(xn_done, t + 1)
                    pe.wait_ge(copied, t + 1)
                    for c in range(KD):
                        ins = nc.tensor.transpose(xT[:, j, c * P:(c + 1) * P], xn[:, j, c * P:(c + 1) * P], ident[:, :])
                    ins.then_inc(transposed, 1)


def project_queries(nc, ctx, tag, x_sb, ident, qT, wq, bq, loads):
    sb, ps, sem = alloc(nc, ctx)
    xnT = normed(nc, ctx, tag)
    wq_sb = sb(f"{tag}_wq", [P, KD, D])
    bq_sb = sb(f"{tag}_bq", [P, KD])
    w_in = sem(f"{tag}_q_w_in")

    def all_loads(sp):
        sp.dma_start(wq_sb[:, :, :], wq).then_inc(w_in, 16)
        sp.dma_start(bq_sb[:, :], bq).then_inc(w_in, 16)
        loads(sp)

    layer_norm(nc, f"ln_{tag}", x_sb, xnT, ident, loads=all_loads)
    q_ps = ps(f"{tag}_q_ps", [P, 2, NB])
    q_made = sem(f"{tag}_q_made")
    q_done = sem(f"{tag}_q_done")
    block = open_block(nc, ctx, sem)
    parts = [(c, blk) for c in range(KD) for blk in range(NBLK)]

    @block.tensor
    def _(pe):
        pe.wait_ge(w_in, 32)
        for n, (c, blk) in enumerate(parts):
            if n >= 2:
                pe.wait_ge(q_done, n - 1)
            for k in range(KD):
                ins = nc.tensor.matmul(q_ps[:, n % 2, :], wq_sb[:, k, c * P:(c + 1) * P],
                                       xnT[:, k, blk * NB:(blk + 1) * NB], start=k == 0, stop=k == KD - 1)
            ins.then_inc(q_made, 1)

    @block.vector
    def _(dve):
        nc.vector.memset(qT[:, :, TOK:], 0.0)
        dve.wait_ge(w_in, 32)
        for n, (c, blk) in enumerate(parts):
            dve.wait_ge(q_made, n + 1)
            nc.vector.tensor_scalar(qT[:, c, blk * NB:(blk + 1) * NB], q_ps[:, n % 2, :], bq_sb[:, c:c + 1],
                                    DH ** -0.5, ALU.add, ALU.mult).then_inc(q_done, 1)


def cross_attention(nc, tag, x_all, ident, pair_mask, ctxT, wq, wk, wv, wo, bq, bv, bo):
    x_sb = x_all[:, 1:, :]
    UN = 4
    NU, UH = 2, H // 2
    UC = UH * LQ
    GH = 4
    NGR = H // GH
    GC = GH * LQ
    LAG = 2
    NSB, NMB = 3, 3
    NPB = 4
    assert KT * UN % NPB == 0 and B % UN == 0
    MAXES = [("M", p, w) for p in range(PAIRS) for w in range(len(WINDOWS))]
    PLACES = 4 + NGR
    PLAN, AT = {}, {}
    for u in range(UN):
        rows = [{2: [("V", i)]} for i in range(KT)]
        for m, op in enumerate(MAXES):
            rows[1 + m // 3].setdefault((0, 4, 7)[m % 3], []).append(op)
        for i, place, op in ((3, 5, ("S", 0)), (4, 5, ("S", 1)), (5, 5, ("X", 0)), (6, 5, ("X", 1)), (8, 5, ("Y",)),
                             (11, 7, ("Z",)), (12, 0, ("T",))):
            rows[i].setdefault(place, []).append(op)
        if u % 2 == 0:
            for k, (i, place) in enumerate(((0, 4), (0, 6), (12, 4), (12, 6))):
                rows[i].setdefault(place, []).append(("Q", k))
        PLAN[u] = [[op for place in range(PLACES) for op in row.get(place, [])] for row in rows]
        AT[u] = [[sum(len(row.get(q, [])) for q in range(place + 1)) for place in range(PLACES)] for row in rows]
    FINISH = [("S", 0), ("S", 1), ("X", 0), ("X", 1), ("Y",), ("Z",)]
    PROLOGUE = ([("Q", k) for k in range(4)]
                + MAXES + [("T",)])
    FIRST = {}
    n = len(PROLOGUE)
    for u in range(UN):
        FIRST[u] = n
        n += sum(len(r) for r in PLAN[u])
    ROUND = n - len(PROLOGUE)
    assert ROUND % NMB == 0

    def last_unit(j):
        return max(k for k in range(-KT * NU, j) if k % (KT * NU) % NSB == j % NSB)

    def row_first(u, i):
        return FIRST[u] + sum(len(r) for r in PLAN[u][:i])

    def number(u, i, op):
        return row_first(u, i) + PLAN[u][i].index(op)

    with ExitStack() as ctx:
        sb, ps, sem = alloc(nc, ctx)
        qT = sb(f"{tag}_qT", [P, KD, TOK + 2 * LQ])
        wk_sb = sb(f"{tag}_wk", [P, H, DC])
        wv_sb = sb(f"{tag}_wv", [P, D])
        bv_sb = sb(f"{tag}_bv", [P, 2])
        wo_sb = sb(f"{tag}_wo", [P, 2, D])
        bo_sb = sb(f"{tag}_bo", [P, D])
        raw = sb(f"{tag}_raw", [P, 2, LKV])
        w_in = sem(f"{tag}_w_in")
        ctx_in = [sem(f"{tag}_ctx_in{j}") for j in range(2)]
        NW = 5 if bo is not None else 4

        def loads(sp):
            sp.dma_start(wk_sb[:, :, :], wk).then_inc(w_in, 16)
            sp.dma_start(wv_sb[:, :], wv).then_inc(w_in, 16)
            sp.dma_start(bv_sb[:, :], bv).then_inc(w_in, 16)
            sp.dma_start(wo_sb[:, :, :], wo).then_inc(w_in, 16)
            if bo is not None:
                sp.dma_start(bo_sb[:, :], bo.partition_broadcast(P)).then_inc(w_in, 16)
            for j in range(2):
                sp.dma_start(raw[:, j, :], ctxT[j, :, :]).then_inc(ctx_in[j], 16)

        with ExitStack() as inner:
            project_queries(nc, inner, tag, x_sb, ident, qT, wq, bq, loads)
        wv_hi = sb(f"{tag}_wv_hi", [P, D], F32R)
        wv_lo = sb(f"{tag}_wv_lo", [P, D], F32R)
        ones = sb(f"{tag}_ones", [PAIRS, P], F32R)
        all_ones = sb(f"{tag}_all_ones", [P, P])
        q_hi = sb(f"{tag}_q_hi", [P, 2, 2, H, LQ], F32R)
        q_lo = sb(f"{tag}_q_lo", [P, 2, 2, H, LQ], F32R)
        c_hi = sb(f"{tag}_c_hi", [P, 2, LKV], F32R)
        c_lo = sb(f"{tag}_c_lo", [P, 2, LKV], F32R)
        maxes = sb(f"{tag}_maxes", [P, PAIRS, len(WINDOWS)])
        neg_max = sb(f"{tag}_neg_max", [P, PAIRS])
        shift = sb(f"{tag}_shift", [PAIRS, 2, PAIRS, P], F32R)
        v_sb = sb(f"{tag}_v", [P, NPB, H, 2, DH], F32R)
        probs = sb(f"{tag}_probs", [P, NPB, H * LQ])
        p_hi = sb(f"{tag}_p_hi", [P, NPB, H * LQ], F32R)
        p_lo = sb(f"{tag}_p_lo", [P, NPB, H * LQ], F32R)
        sums = sb(f"{tag}_sums", [P, 2, H * LQ])
        u_sb = sb(f"{tag}_u", [P, NGR, LQ])
        recip = sb(f"{tag}_recip", [P, PAIRS])
        o_sb = sb(f"{tag}_o", [P, PAIRS, DH])
        oT = sb(f"{tag}_oT", [P, P])
        score_ps = ps(f"{tag}_score_ps", [P, NSB, NB])
        pv_ps = ps(f"{tag}_pv_ps", [P, NU, NB])
        misc_ps = ps(f"{tag}_misc_ps", [P, NMB, NB])

        const_done = sem(f"{tag}_const_done")
        wv_hi_done = sem(f"{tag}_wv_hi_done")
        wv_done = sem(f"{tag}_wv_done")
        x_biased = sem(f"{tag}_x_biased")
        c_hi_done = sem(f"{tag}_c_hi_done")
        c_lo_done = sem(f"{tag}_c_lo_done")
        q_hi_done = sem(f"{tag}_q_hi_done")
        v_hi_done = sem(f"{tag}_v_hi_done")
        misc_ready = sem(f"{tag}_misc_ready")
        misc_free = sem(f"{tag}_misc_free")
        max_done = sem(f"{tag}_max_done")
        score_ready = sem(f"{tag}_score_ready")
        score_free = sem(f"{tag}_score_free")
        p_hi_done = sem(f"{tag}_p_hi_done")
        p_lo_done = sem(f"{tag}_p_lo_done")
        sums_done = sem(f"{tag}_sums_done")
        pv_done = sem(f"{tag}_pv_done")
        u_done = sem(f"{tag}_u_done")
        o_normed = sem(f"{tag}_o_normed")
        block = open_block(nc, ctx, sem)

        def keys(i):
            return KLAST if i == KT - 1 else P

        def unit(w):
            return slice(w * UC, (w + 1) * UC)

        @block.sync
        def _(sp):
            with sp.Fori(0, B // UN) as t:
                for u in range(UN):
                    sp.wait_ge(c_lo_done, t * UN + u + 1)
                    sp.dma_start(raw[:, u % 2, :],
                                 ctxT[ds(t * UN + u + 2, 1), :, :].rearrange("b p k -> p (b k)")
                                 ).then_inc(ctx_in[u % 2], 16)
            for j in range(2):
                sp.wait_ge(ctx_in[j], 16 * (B // 2 + 1))

        @block.tensor
        def _(pe):
            def small(op, u, t, n):
                bank = misc_ps[:, n % NMB, :]
                nxt = (u + 1) % UN
                b = t * UN + u
                pe.wait_ge(misc_free, t * ROUND + n + 1)
                if op[0] == "Q":
                    first = 0 if u < 0 else (b + 2) * LQ
                    for j in range(4):
                        h = 4 * op[1] + j
                        ins = nc.tensor.matmul(bank[:, j * P:(j + 1) * P], wk_sb[:, h, :],
                                               qT[:, h // 8, ds(first, P)], start=True, stop=True)
                elif op[0] == "V":
                    i = op[1]
                    for m, (a, w) in enumerate(((c_hi, wv_hi), (c_hi, wv_lo), (c_lo, wv_hi))):
                        ins = nc.tensor.matmul(bank[0:keys(i), 0:D], a[:, u % 2, i * P:i * P + keys(i)],
                                               w[:, :], start=m == 0, stop=m == 2)
                elif op[0] == "M":
                    _, p, w = op
                    k0, kn = WINDOWS[w]
                    pe.wait_ge(c_hi_done, b + 2)
                    q = q_hi[:, nxt // 2, nxt % 2, 2 * p:2 * p + 2, :].rearrange("p h q -> p (h q)")
                    ins = nc.tensor.matmul(bank[:, 0:kn], q, c_hi[:, nxt % 2, k0:k0 + kn], start=True, stop=True)
                elif op[0] == "T":
                    pe.wait_ge(max_done, b + 2)
                    ins = nc.tensor.transpose(bank[0:PAIRS, 0:P], neg_max[:, :], ident[:, :])
                elif op[0] == "S":
                    pe.wait_ge(sums_done, b * KT + NPB)
                    for k in range(GH):
                        col = op[1] * UC + k * P
                        ins = nc.tensor.matmul(bank[:, k * P:(k + 1) * P], sums[:, (u - 1) % 2, col:col + P],
                                               all_ones[:, :], start=True, stop=True)
                elif op[0] == "X":
                    pe.wait_ge(u_done, b * GH + GH)
                    groups = slice(op[1] * 2, op[1] * 2 + 2)
                    ins = nc.tensor.transpose(bank[:, 0:P], u_sb[:, groups, :].rearrange("p g q -> p (g q)"), ident[:, :])
                elif op[0] == "Y":
                    pe.wait_ge(o_normed, b * NU + NU)
                    ins = nc.tensor.transpose(bank[:, 0:P], o_sb[:, :, :].rearrange("p a d -> p (a d)"), ident[:, :])
                elif op[0] == "Z":
                    half = (u - 1) % 2
                    pe.wait_ge(misc_free, t * ROUND + n + NMB)
                    for j in range(2):
                        ins = nc.tensor.matmul(bank[half * LQ:(half + 1) * LQ, 0:D], oT[:, j * LQ:(j + 1) * LQ],
                                               wo_sb[:, j, :], start=j == 0, stop=j == 1)
                ins.then_inc(misc_ready, 1)

            def pv(u, t, i, then):
                tile = KT * u + i
                N = t * (UN * KT) + tile
                pe.wait_ge(p_lo_done, N + NPB + 1)
                value = number(u % UN, i, ("V", i)) - (ROUND if u < 0 else 0)
                pe.wait_ge(misc_free, t * ROUND + value + NMB + 1)
                if i == 0:
                    pe.wait_ge(u_done, (t * UN + u) * GH + GH)
                for g in range(NGR):
                    w, col = g // 2, g % 2 * GC
                    values = v_sb[0:keys(i), tile % NPB, g * GH:(g + 1) * GH, :, :].rearrange("p a b d -> p (a b d)")

                    def own(p):
                        return p[0:keys(i), tile % NPB, unit(w)].rearrange("p (h g q) -> p h g q", g=2, q=LQ
                                                                           )[:, :, g % 2, :]

                    nc.tensor.matmul(pv_ps[:, w, col:col + GC], values, own(p_hi),
                                     start=i == 0 and col == 0, stop=False, skip_group_check=True)
                    ins = nc.tensor.matmul(pv_ps[:, w, col:col + GC], values, own(p_lo),
                                           start=False, stop=i == KT - 1, skip_group_check=True)
                    if g == NGR - 1:
                        ins.then_inc(pv_done, 1)
                    then(4 + g)

            pe.sem_inc(score_ready, 1)
            pe.sem_inc(pv_done, 2)
            pe.wait_ge(w_in, 16 * NW)
            pe.wait_ge(const_done, 1)
            for n, op in enumerate(PROLOGUE):
                if op == ("M", 0, 0):
                    pe.wait_ge(misc_free, n + NMB)
                small(op, -1, 0, n)
            pe.wait_ge(wv_done, 1)
            for g in range(NGR):
                nc.tensor.matmul(pv_ps[:, g // 2, g % 2 * GC:g % 2 * GC + GC],
                                 v_sb[:, NPB - 1, g * GH:(g + 1) * GH, :, :].rearrange("p a b d -> p (a b d)"),
                                 p_hi[:, NPB - 1, g * GC:(g + 1) * GC], start=True, stop=True)
            with pe.Fori(0, B // UN) as t:
                for u in range(UN):
                    b = t * UN + u
                    for i in range(KT):
                        tile = KT * u + i
                        N = t * (UN * KT) + tile
                        n = row_first(u, i)
                        work = list(enumerate(PLAN[u][i], n))

                        def then(place):
                            while AT[u][i][place] > len(PLAN[u][i]) - len(work):
                                k, op = work.pop(0)
                                small(op, u, t, k)

                        cols = slice(i * P, i * P + keys(i))
                        for w in range(NU):
                            if i == 0 and w == 0:
                                pe.wait_ge(c_lo_done, b + 1)
                                maxima = number(u - 1, KT - 1, ("T",)) if u > 0 else FIRST[0] - 1
                                pe.wait_ge(misc_free, t * ROUND + maxima + NMB + 1)
                            pe.wait_ge(score_free, b * (KT * NU) + last_unit(i * NU + w) + NSB + 1)
                            out = score_ps[0:keys(i), (i * NU + w) % NSB, :]
                            heads = slice(w * UH, (w + 1) * UH)
                            for m, (a, q) in enumerate(((c_hi, q_hi), (c_hi, q_lo), (c_lo, q_hi))):
                                nc.tensor.matmul(out, a[:, u % 2, cols],
                                                 q[:, u // 2, u % 2, heads, :].rearrange("p h q -> p (h q)"),
                                                 start=m == 0, stop=False)
                                if m == 1:
                                    then(2 * w)
                            nc.tensor.matmul(out, ones[:, 0:keys(i)],
                                             shift[:, u % 2, :, :].rearrange("r a c -> r (a c)")[:, unit(w)],
                                             start=False, stop=True).then_inc(score_ready, 1)
                            then(2 * w + 1)
                        if i < LAG:
                            pv(u - 1, t, KT + i - LAG, then)
                        else:
                            pv(u, t, i - LAG, then)
                        assert not work
            end = B // UN
            for i in range(KT - LAG, KT):
                pv(-1, end, i, lambda place: None)
            for n, op in enumerate(FINISH, FIRST[0]):
                small(op, 0, end, n)

        @block.scalar
        def _(act):
            act.sem_inc(score_free, NSB)
            act.sem_inc(p_hi_done, NPB)
            act.wait_ge(w_in, 16 * NW)
            nc.scalar.activation(wv_hi[:, :], wv_sb[:, :], ACT.Copy).then_inc(wv_hi_done, 1)

            def split(j, arrived):
                act.wait_ge(ctx_in[j], arrived)
                nc.scalar.activation(c_hi[:, j, :], raw[:, j, :], ACT.Copy).then_inc(c_hi_done, 1)

            def queries(k, s, t, n):
                act.wait_ge(misc_ready, t * ROUND + n + 1)
                nc.scalar.activation(
                    q_hi[:, s, :, 4 * k:4 * k + 4, :],
                    misc_ps[:, n % NMB, :].rearrange("p (h s q) -> p s h q", h=4, s=2), ACT.Copy).then_inc(q_hi_done, 1)

            def out(b):
                for k in range(GH):
                    if k == 0:
                        act.wait_ge(pv_done, b * KT + LAG + 2)
                    rows = slice(k * 2 * DH, (k + 1) * 2 * DH)
                    groups = pv_ps[rows, :, :].rearrange("p w n -> p (w n)").rearrange("p (g n) -> p g n", n=GC)
                    nc.scalar.activation(u_sb[rows, :, :], groups[:, :, k * LQ:(k + 1) * LQ], ACT.Copy
                                         ).then_inc(u_done, 1)

            split(0, 16)
            for n, op in enumerate(PROLOGUE):
                if op[0] == "Q":
                    queries(op[1], 0, 0, n)
            act.wait_ge(const_done, 1)
            with act.Fori(0, B // UN) as t:
                for u in range(UN):
                    b = t * UN + u
                    act.wait_ge(score_ready, b * (KT * NU) + 1)
                    split((u + 1) % 2, (t * 2 + (u + 1) // 2) * 16 + 16)
                    for i in range(KT):
                        tile = KT * u + i
                        N = t * (UN * KT) + tile
                        n = row_first(u, i)
                        rows = slice(0, keys(i))
                        for w in range(NU):
                            if w == 0:
                                act.wait_ge(p_hi_done, N + 1)
                                act.wait_ge(p_lo_done, N + 1)
                                act.wait_ge(sums_done, N + 1)
                            act.wait_ge(score_ready, N * NU + w + 2)
                            nc.scalar.activation(probs[rows, tile % NPB, unit(w)], score_ps[rows, (i * NU + w) % NSB, :], ACT.Exp
                                                 ).then_inc(score_free, 1)
                            if w == 0:
                                k = number(u, i, ("V", i))
                                act.wait_ge(misc_ready, t * ROUND + k + 1)
                                act.wait_ge(pv_done, N + 1)
                                nc.scalar.activation(v_sb[rows, tile % NPB, :, 0, :],
                                                     misc_ps[rows, k % NMB, 0:D].rearrange("p (h n) -> p h n", h=H),
                                                     ACT.Copy).then_inc(v_hi_done, 1)
                        act.wait_ge(score_free, N * NU + NU + NSB)
                        nc.scalar.activation(p_hi[rows, tile % NPB, :], probs[rows, tile % NPB, :], ACT.Copy
                                             ).then_inc(p_hi_done, 1)
                        if i == LAG - 1:
                            out(b)
                        for k, op in enumerate(PLAN[u][i], n):
                            if op[0] == "Q":
                                queries(op[1], (u // 2 + 1) % 2, t, k)
            out(B)

        @block.gpsimd
        def _(pool):
            pool.sem_inc(sums_done, NPB)
            nc.gpsimd.memset(sums[:, 1, :], 1.0)

            def lo(j, need):
                pool.wait_ge(c_hi_done, need)
                nc.gpsimd.tensor_tensor(c_lo[:, j, :], raw[:, j, :], c_hi[:, j, :].bitcast(F32), ALU.subtract
                                        ).then_inc(c_lo_done, 1)

            lo(0, 1)
            with pool.Fori(0, B // UN) as t:
                for u in range(UN):
                    lo((u + 1) % 2, t * UN + u + 2)
                    for i in range(1, KT):
                        tile = KT * u + i
                        N = t * (UN * KT) + tile
                        rows = slice(0, keys(i))
                        pool.wait_ge(score_free, N * NU + NU + NSB)
                        if i > 1:
                            pool.wait_ge(sums_done, N + NPB)
                        before = probs[rows, (tile - 1) % NPB, :] if i == 1 else sums[rows, u % 2, :]
                        nc.gpsimd.tensor_tensor(sums[rows, u % 2, :], before, probs[rows, tile % NPB, :], ALU.add
                                                ).then_inc(sums_done, 2 if i == 1 else 1)

        @block.vector
        def _(dve):
            dve.sem_inc(misc_free, NMB)
            dve.sem_inc(p_lo_done, NPB - 1)
            nc.vector.memset(ones[:, :].bitcast(F32), 1.0)
            nc.vector.memset(all_ones[:, :], 1.0)
            nc.vector.memset(probs[:, NPB - 1, :], 0.0)
            nc.vector.memset(v_sb[:, NPB - LAG:, :, :, :].bitcast(F32), 0.0)
            nc.vector.memset(p_lo[:, NPB - LAG:, :].bitcast(F32), 0.0)
            nc.vector.memset(p_hi[:, NPB - LAG:, :].bitcast(F32), 0.0).then_inc(const_done, 1)
            dve.wait_ge(const_done, 1)
            dve.wait_ge(w_in, 16 * NW)
            dve.wait_ge(wv_hi_done, 1)
            nc.vector.tensor_tensor(wv_lo[:, :], wv_sb[:, :], wv_hi[:, :].bitcast(F32), ALU.subtract
                                    ).then_inc(wv_done, 1)
            if bo is not None:
                nc.vector.tensor_tensor(x_sb, x_sb, bo_sb[:, :].rearrange("p (a d) -> p a d", a=1).broadcast_to([P, NT, D]),
                                        ALU.add).then_inc(x_biased, 1)
                dve.wait_ge(x_biased, 1)

            def lo(u, t, i):
                tile = KT * u + i
                N = t * (UN * KT) + tile
                rows = slice(0, keys(i))
                dve.wait_ge(p_hi_done, N + NPB + 1)
                nc.vector.tensor_tensor(p_lo[rows, tile % NPB, :], probs[rows, tile % NPB, :],
                                        p_hi[rows, tile % NPB, :].bitcast(F32), ALU.subtract).then_inc(p_lo_done, 1)

            def use(op, u, t, n):
                bank = misc_ps[:, n % NMB, :]
                b = t * UN + u
                dve.wait_ge(misc_ready, t * ROUND + n + 1)
                if op[0] == "Q":
                    s = 0 if u < 0 else (u // 2 + 1) % 2
                    k = op[1]
                    if u < 0:
                        dve.wait_ge(q_hi_done, k + 1)
                    else:
                        dve.wait_ge(q_hi_done, t * (UN // 2 * 4) + 4 + (u // 2) * 4 + k + 1)
                    ins = nc.vector.tensor_tensor(q_lo[:, s, :, 4 * k:4 * k + 4, :],
                                                  bank.rearrange("p (h s q) -> p s h q", h=4, s=2),
                                                  q_hi[:, s, :, 4 * k:4 * k + 4, :].bitcast(F32), ALU.subtract)
                elif op[0] == "V":
                    i = op[1]
                    tile = KT * u + i
                    rows = slice(0, keys(i))
                    dve.wait_ge(v_hi_done, t * (UN * KT) + tile + 1)
                    ins = nc.vector.tensor_tensor(v_sb[rows, tile % NPB, :, 1, :],
                                                  bank[rows, 0:D].rearrange("p (h n) -> p h n", h=H),
                                                  v_sb[rows, tile % NPB, :, 0, :].bitcast(F32), ALU.subtract)
                elif op[0] == "M":
                    _, p, w = op
                    ins = nc.vector.tensor_reduce(maxes[:, p, w:w + 1], bank[:, 0:WINDOWS[w][1]], AX.X, ALU.max)
                elif op[0] == "T":
                    ins = nc.vector.tensor_tensor(
                        shift[:, (u + 1) % 2, :, :],
                        bank[0:PAIRS, 0:P].rearrange("r (a c) -> r a c", a=1).broadcast_to([PAIRS, PAIRS, P]),
                        pair_mask[:, :].rearrange("r (a c) -> r a c", c=1).broadcast_to([PAIRS, PAIRS, P]), ALU.mult)
                elif op[0] == "S":
                    ins = nc.vector.reciprocal(recip[:, op[1] * 4:op[1] * 4 + 4],
                                               bank.rearrange("p (a n) -> p a n", n=P)[:, :, 0])
                elif op[0] == "X":
                    ins = nc.vector.tensor_reduce(o_sb[:, op[1] * GH:(op[1] + 1) * GH, :],
                                                  bank[:, 0:P].rearrange("p (h a n) -> p h n a", h=GH, a=2), AX.X, ALU.add)
                elif op[0] == "Y":
                    for j in range(2):
                        ins = nc.vector.tensor_scalar(oT[:, j * LQ:(j + 1) * LQ], bank[:, j * LQ:(j + 1) * LQ],
                                                      bv_sb[:, j:j + 1], None, ALU.add)
                elif op[0] == "Z":
                    half = (u - 1) % 2
                    rows = slice(half * LQ, (half + 1) * LQ)
                    x_t = x_all[rows, ds(t * (UN // 2) + (u + 1) // 2, 1), :].rearrange("p a d -> p (a d)")
                    ins = nc.vector.tensor_tensor(x_t, bank[rows, 0:D], x_t, ALU.add)
                ins.then_inc(misc_free, 1)
                if op[0] == "X":
                    dve.wait_ge(misc_free, t * ROUND + n + NMB + 1)
                    o = o_sb[:, op[1] * 4:op[1] * 4 + 4, :]
                    nc.vector.tensor_tensor(
                        o, o, recip[:, op[1] * 4:op[1] * 4 + 4].rearrange("p (a d) -> p a d", d=1).broadcast_to([P, 4, DH]),
                        ALU.mult).then_inc(o_normed, 1)
                if op[0] == "M" and (op[1], op[2]) == (PAIRS - 1, len(WINDOWS) - 1):
                    dve.wait_ge(misc_free, t * ROUND + n + NMB + 1)
                    nc.vector.tensor_reduce(neg_max[:, :], maxes[:, :, :], AX.X, ALU.max, negate=True
                                            ).then_inc(max_done, 1)

            for n, op in enumerate(PROLOGUE):
                use(op, -1, 0, n)
            with dve.Fori(0, B // UN) as t:
                for u in range(UN):
                    for i in range(KT):
                        for k, op in enumerate(PLAN[u][i]):
                            if k == min(1, len(PLAN[u][i]) - 1):
                                if i == 0:
                                    lo(u - 1, t, KT - 1)
                                else:
                                    lo(u, t, i - 1)
                            use(op, u, t, row_first(u, i) + k)
            end = B // UN
            lo(-1, end, KT - 1)
            for n, op in enumerate(FINISH, FIRST[0]):
                use(op, 0, end, n)


def self_attention(nc, x_sb, ident, a):
    with ExitStack() as ctx:
        sb, ps, sem = alloc(nc, ctx)
        xnT = normed(nc, ctx, "s")
        w_sb = sb("s_w", [P, KD, 3 * D])
        mask = sb("s_mask", [P, 8])
        w_in = sem("s_w_in")

        def loads(sp):
            sp.dma_start(w_sb[:, :, :], a["s_w"]).then_inc(w_in, 16)
            sp.dma_start(mask[:, :], a["s_mask"]).then_inc(w_in, 16)

        layer_norm(nc, "ln_s", x_sb, xnT, ident, loads=loads)
        xt = sb("s_xt", [P, 2, KD, P])
        qz = sb("s_qz", [P, 2, 2, 8, LQ])
        kT = sb("s_kT", [P, 2, KD, P])
        v_sb = sb("s_v", [P, 2, D + P - 2 * DH])
        neg_max = sb("s_neg_max", [P, PAIRS])
        shifted = sb("s_shifted", [P, PAIRS, LQ])
        probs = sb("s_probs", [P, 2, PAIRS, P])
        pT = sb("s_pT", [P, PAIRS, P])
        total = sb("s_total", [P, 2, PAIRS])
        recip = sb("s_recip", [P, PAIRS])
        o_sb = sb("s_o", [P, H, DH])
        proj_ps = ps("s_proj_ps", [P, 2, NB])
        score_ps = ps("s_score_ps", [P, PAIRS, P])
        pT_ps = ps("s_pT_ps", [P, PAIRS, P])
        pv_ps = ps("s_pv_ps", [P, 2, 4 * P])
        zeroed = sem("s_zeroed")
        xt_done = sem("s_xt_done")
        proj_done = sem("s_proj_done")
        kv_done = sem("s_kv_done")
        q_done = sem("s_q_done")
        score_done = sem("s_score_done")
        max_done = sem("s_max_done")
        shift_done = sem("s_shift_done")
        probs_done = sem("s_probs_done")
        sum_done = sem("s_sum_done")
        trans_done = sem("s_trans_done")
        pT_done = sem("s_pT_done")
        pv_done = sem("s_pv_done")
        recip_done = sem("s_recip_done")
        o_done = sem("s_o_done")
        x_done = sem("s_x_done")
        block = open_block(nc, ctx, sem)

        @block.gpsimd
        def _(pool):
            nc.gpsimd.memset(v_sb[:, :, D:], 0.0)
            nc.gpsimd.memset(probs[:, :, :, :], 0.0).then_inc(zeroed, 1)

            def stage(tile, j, n):
                if n is not None:
                    pool.wait_ge(proj_done, n + 1)
                nc.gpsimd.tensor_copy(xt[:, j, :, :], xnT[:, :, tile]).then_inc(xt_done, 1)

            stage(slice(0, P), 0, None)
            with pool.Fori(0, NT // 2) as t:
                for j in range(2):
                    stage(ds((t * 2 + j + 1) * P, P), (j + 1) % 2, t * 2 + j)

        @block.tensor
        def _(pe):
            def project(j, n):
                pe.wait_ge(xt_done, n)
                pe.wait_ge(q_done, (n - 1) * 2)
                pe.wait_ge(kv_done, n - 1)
                for c in range(2 * KD):
                    for k in range(KD):
                        nc.tensor.matmul(proj_ps[:, 0, c * P:(c + 1) * P], w_sb[:, k, c * P:(c + 1) * P],
                                         xt[:, j, k, :], start=k == 0, stop=k == KD - 1)
                for k in range(KD):
                    ins = nc.tensor.matmul(proj_ps[:, 1, 0:D], xt[:, j, k, :], w_sb[:, k, 2 * D:3 * D],
                                           start=k == 0, stop=k == KD - 1)
                ins.then_inc(proj_done, 1)

            def scores(s, j, n):
                pe.wait_ge(q_done, n)
                pe.wait_ge(shift_done, n - 1)
                for p in range(PAIRS):
                    c, r = p // 4, 2 * (p % 4)
                    ins = nc.tensor.matmul(score_ps[:, p, :],
                                           qz[:, s, c, r:r + 2, :].rearrange("p h q -> p (h q)"),
                                           kT[:, j, c, :], start=True, stop=True)
                ins.then_inc(score_done, 1)

            pe.sem_inc(proj_done, 1)
            pe.sem_inc(pv_done, 1)
            pe.sem_inc(pT_done, 1)
            pe.sem_inc(o_done, 2)
            pe.wait_ge(w_in, 32)
            project(0, 1)
            pe.wait_ge(kv_done, 1)
            scores(0, 0, 1)
            with pe.Fori(0, NT // 2) as t:
                for j in range(2):
                    for s in range(2):
                        b = t * 4 + j * 2 + s
                        pe.wait_ge(probs_done, b + 1)
                        pe.wait_ge(pT_done, b + 1)
                        for p in range(PAIRS):
                            ins = nc.tensor.transpose(pT_ps[:, p, :], probs[:, s, p, :], ident[:, :])
                        ins.then_inc(trans_done, 1)
                        if s == 0:
                            scores(1, j, b + 2)
                            project((j + 1) % 2, t * 2 + j + 2)
                        else:
                            pe.wait_ge(kv_done, t * 2 + j + 2)
                            scores(0, (j + 1) % 2, b + 2)
                        pe.wait_ge(pT_done, b + 2)
                        pe.wait_ge(o_done, b * 2 + 2)
                        for p in range(PAIRS):
                            c = p // 4
                            ins = nc.tensor.matmul(pv_ps[:, c, (p % 4) * P:(p % 4 + 1) * P], pT[:, p, :],
                                                   v_sb[:, j, p * 2 * DH:p * 2 * DH + P], start=True, stop=True)
                        ins.then_inc(pv_done, 1)

        @block.scalar
        def _(act):
            def keys_values(j, n):
                act.wait_ge(proj_done, n + 1)
                nc.scalar.activation(kT[:, j, :, :].rearrange("p c n -> p (c n)"), proj_ps[:, 0, D:2 * D], ACT.Copy)
                nc.scalar.activation(v_sb[:, j, 0:D], proj_ps[:, 1, 0:D], ACT.Copy).then_inc(kv_done, 1)

            def exps(s, n):
                act.wait_ge(shift_done, n)
                act.wait_ge(trans_done, n - 1)
                act.wait_ge(sum_done, n - 1)
                nc.scalar.activation(probs[:, s, :, s * LQ:(s + 1) * LQ], shifted[:, :, :], ACT.Exp
                                     ).then_inc(probs_done, 1)

            act.wait_ge(zeroed, 1)
            keys_values(0, 1)
            exps(0, 1)
            with act.Fori(0, NT // 2) as t:
                for j in range(2):
                    for s in range(2):
                        b = t * 4 + j * 2 + s
                        act.wait_ge(trans_done, b + 1)
                        act.wait_ge(pv_done, b + 1)
                        nc.scalar.activation(pT[:, :, :], pT_ps[:, :, :], ACT.Copy).then_inc(pT_done, 1)
                        if s == 0:
                            exps(1, b + 2)
                            keys_values((j + 1) % 2, t * 2 + j + 2)
                        else:
                            exps(0, b + 2)

        @block.vector
        def _(dve):
            def queries(s, n):
                for c in range(KD):
                    ins = nc.vector.tensor_tensor(
                        qz[:, s, c, :, :],
                        proj_ps[:, 0, c * P + s * LQ:c * P + (s + 1) * LQ].rearrange("p (h q) -> p h q", h=1)
                        .broadcast_to([P, 8, LQ]),
                        mask[:, :].rearrange("p (h q) -> p h q", q=1).broadcast_to([P, 8, LQ]), ALU.mult)
                ins.then_inc(q_done, 1)

            def shift(s, n):
                dve.wait_ge(score_done, n)
                own = score_ps[:, :, s * LQ:(s + 1) * LQ]
                nc.vector.tensor_reduce(neg_max[:, :], own, AX.X, ALU.max).then_inc(max_done, 1)
                dve.wait_ge(max_done, n)
                dve.wait_ge(probs_done, n - 1)
                nc.vector.tensor_tensor(shifted[:, :, :], own,
                                        neg_max[:, :].rearrange("p (a q) -> p a q", q=1).broadcast_to([P, PAIRS, LQ]),
                                        ALU.subtract).then_inc(shift_done, 1)

            def sums(s, n):
                dve.wait_ge(probs_done, n)
                nc.vector.tensor_reduce(total[:, s, :], probs[:, s, :, s * LQ:(s + 1) * LQ], AX.X, ALU.add
                                        ).then_inc(sum_done, 1)

            dve.sem_inc(x_done, 1)
            dve.wait_ge(w_in, 32)
            dve.wait_ge(kv_done, 1)
            queries(0, 1)
            queries(1, 2)
            shift(0, 1)
            with dve.Fori(0, NT // 2) as t:
                for j in range(2):
                    for s in range(2):
                        b = t * 4 + j * 2 + s
                        sums(s, b + 1)
                        shift((s + 1) % 2, b + 2)
                        if s == 0:
                            dve.wait_ge(kv_done, t * 2 + j + 2)
                            queries(0, b + 3)
                            queries(1, b + 4)
                        dve.wait_ge(sum_done, b + 1)
                        nc.vector.reciprocal(recip[:, :], total[:, s, :]).then_inc(recip_done, 1)
                        dve.wait_ge(recip_done, b + 1)
                        dve.wait_ge(pv_done, b + 2)
                        dve.wait_ge(x_done, b + 1)
                        for half in range(2):
                            rows = slice(half * LQ, (half + 1) * LQ)
                            out = pv_ps[rows, :, :].rearrange("p c (a n) -> p (c a) n", n=P)
                            nc.vector.tensor_tensor(
                                o_sb[s * LQ:(s + 1) * LQ, half::2, :], out[:, :, half * DH:(half + 1) * DH],
                                recip[rows, :].rearrange("p (a d) -> p a d", d=1).broadcast_to([LQ, PAIRS, DH]),
                                ALU.mult).then_inc(o_done, 1)
                        dve.wait_ge(o_done, b * 2 + 4)
                        rows = slice(s * LQ, (s + 1) * LQ)
                        x_t = x_sb[rows, ds(t * 2 + j, 1), :].rearrange("p a d -> p (a d)")
                        nc.vector.tensor_tensor(x_t, x_t, o_sb[rows, :, :].rearrange("p h d -> p (h d)"), ALU.add
                                                ).then_inc(x_done, 1)


def experts(nc, x_sb, ident, a):
    with ExitStack() as ctx:
        sb, ps, sem = alloc(nc, ctx)
        w1 = sb("m_w1", [P, NE, KD, DE])
        w2 = sb("m_w2", [P, NE, KD, DE])
        w3 = sb("m_w3", [P, NE, EC, D])
        rms_w = sb("m_rms_w", [P, KD])
        prob = sb("m_prob", [P, 2, NT])
        slot = sb("m_slot", [P, 2, NT], U32)
        block_expert = sb("m_block_expert", [P, SLOT_BLOCKS], I32)
        slot_rows = nc.dram_tensor("m_slot_rows", (SLOT_BLOCKS * P, D), F32, kind="Internal").ap()
        slot_out = nc.dram_tensor("m_slot_out", (SLOT_BLOCKS * P, D), F32, kind="Internal").ap()
        rms_in = sem("m_rms_in")
        w_in = sem("m_w_in")
        zeroed = sem("m_zeroed")
        zero_out = sem("m_zero_out")
        scattered = sem("m_scattered")
        stored = [sem(f"m_stored{j}") for j in range(2)]
        with ExitStack() as inner:
            route(nc, inner, x_sb, ident, a, w1, w2, w3, rms_w, prob, slot, block_expert, slot_rows,
                  rms_in, w_in, zeroed, zero_out, scattered)
        with ExitStack() as inner:
            expert_blocks(nc, inner, ident, w1, w2, w3, rms_w, block_expert, slot_rows, slot_out,
                          w_in, scattered, stored)
        sb, ps, inner_sem = alloc(nc, ctx)
        back = sb("m_back", [P, NT, 2, D])
        GROUP = 4
        gathered = [sem(f"m_gathered{g}") for g in range(NT // GROUP)]
        first_added = sem("m_first_added")
        block = open_block(nc, ctx, sem)

        @block.gpsimd
        def _(pool):
            for j in range(2):
                pool.wait_ge(stored[j], 16 * ((SLOT_BLOCKS + 1 - j) // 2))
            for t in range(NT):
                for i in range(2):
                    nc.gpsimd.indirect_dma_start(back[:, t, i, :], None, slot_out,
                                                 bass.IndirectOffsetOnAxis(ap=slot[:, i, t:t + 1], axis=0)
                                                 ).then_inc(gathered[t // GROUP], 16)

        @block.vector
        def _(dve):
            for t in range(NT):
                if t % GROUP == 0:
                    dve.wait_ge(gathered[t // GROUP], 16 * 2 * GROUP)
                nc.vector.scalar_tensor_tensor(x_sb[:, t, :], back[:, t, 0, :], prob[:, 0, t:t + 1], x_sb[:, t, :],
                                               ALU.mult, ALU.add).then_inc(first_added, 1)
                if t > 0:
                    dve.wait_ge(first_added, t)
                    nc.vector.scalar_tensor_tensor(x_sb[:, t - 1, :], back[:, t - 1, 1, :], prob[:, 1, t - 1:t],
                                                   x_sb[:, t - 1, :], ALU.mult, ALU.add)
            dve.wait_ge(first_added, NT)
            nc.vector.scalar_tensor_tensor(x_sb[:, NT - 1, :], back[:, NT - 1, 1, :], prob[:, 1, NT - 1:NT],
                                           x_sb[:, NT - 1, :], ALU.mult, ALU.add)


def route(nc, ctx, x_sb, ident, a, w1, w2, w3, rms_w, prob, slot, block_expert, slot_rows,
          rms_in, w_in, zeroed, zero_out, scattered):
    sb, ps, sem = alloc(nc, ctx)
    xnT = normed(nc, ctx, "m")
    rows = sb("m_rows", [P, NT, D])
    zero = sb("m_zero", [P, D])
    gate_w = sb("m_gate_w", [P, KD, NE])
    const = sb("m_const", [P, M_CONST])
    cols = {}
    at = 0
    for name, n in M_CONST_PARTS:
        cols[name] = const[:, at:at + n]
        at += n
    c_in = sem("m_c_in")
    with nc.Block() as block:
        @block.vector
        def _(dve):
            nc.vector.memset(zero[:, :], 0.0).then_inc(zeroed, 1)

        @block.sync
        def _(sp):
            sp.dma_start(rms_w[:, :], a["m_rms_w"]).then_inc(rms_in, 16)
            sp.dma_start(gate_w[:, :, :], a["m_gate_w"]).then_inc(c_in, 16)
            sp.dma_start(const[:, :], a["m_const"]).then_inc(c_in, 16)
            sp.wait_ge(rms_in, 16)
            sp.wait_ge(c_in, 32)
    def loads(sp):
        sp.wait_ge(zeroed, 1)
        sp.dma_start(slot_rows.rearrange("(b p) d -> p b d", p=P),
                     zero[:, :].rearrange("p (b d) -> p b d", b=1).broadcast_to([P, SLOT_BLOCKS, D])
                     ).then_inc(zero_out, 16)
        for e in range(NE):
            for dst, src in ((w1, a["m_w1"]), (w2, a["m_w2"]), (w3, a["m_w3"])):
                sp.dma_start(dst[:, e, :, :], src[e, :, :, :]).then_inc(w_in, 16)

    layer_norm(nc, "ln_m", x_sb, xnT, ident, rms=rms_w, rows=rows, loads=loads)

    logits = sb("m_logits", [P, NT, NE])
    top = sb("m_top", [P, 2, NT])
    best_at = sb("m_best_at", [P, 2, NT])
    first = sb("m_first", [P, NT, NE])
    second = sb("m_second", [P, NT, NE])
    cand = sb("m_cand", [P, NT, NE])
    gap = sb("m_gap", [P, NT])
    expo = sb("m_expo", [P, NT])
    denom = sb("m_denom", [P, NT])
    both = sb("m_both", [P, NE, NT])
    upto = sb("m_upto", [P, NE, NT])
    before = sb("m_before", [P, NE, NT])
    count = sb("m_count", [P, NE])
    over = sb("m_over", [P, NE, NT])
    blocks = sb("m_blocks", [P, NE])
    block_end = sb("m_block_end", [P, NE])
    base = sb("m_base", [P, NE])
    place = sb("m_place", [P, NE, NT])
    mine = sb("m_mine", [P, 2, NE, NT])
    slot_f = sb("m_slot_f", [P, 2, NT])
    ended = sb("m_ended", [P, SLOT_BLOCKS, NE])
    expert_f = sb("m_expert_f", [P, SLOT_BLOCKS])
    gate_ps = ps("m_gate_ps", [P, NB])
    prefix_ps = ps("m_prefix_ps", [P, NB])
    count_ps = ps("m_count_ps", [P, NB])
    logits_done = sem("m_logits_done")
    gap_done = sem("m_gap_done")
    e_done = sem("m_e_done")
    before_done = sem("m_before_done")
    prefix_done = sem("m_prefix_done")
    slot_done = sem("m_slot_done")
    seq = sem("m_seq")
    block = open_block(nc, ctx, sem)

    @block.tensor
    def _(pe):
        for t in range(NT):
            for k in range(KD):
                ins = nc.tensor.matmul(gate_ps[:, t * NE:(t + 1) * NE], xnT[:, k, t * P:(t + 1) * P],
                                       gate_w[:, k, :], start=k == 0, stop=k == KD - 1)
        ins.then_inc(logits_done, 1)
        pe.wait_ge(before_done, 1)
        nc.tensor.matmul(prefix_ps[:, 0:NE * NT], cols["rows_before"], both[:, :, :].rearrange("p e t -> p (e t)"),
                         start=True, stop=False)
        nc.tensor.matmul(prefix_ps[:, 0:NE * NT], cols["ones"], before[:, :, :].rearrange("p e t -> p (e t)"),
                         start=False, stop=True)
        nc.tensor.matmul(count_ps[:, 0:NE], cols["ones"], upto[:, :, NT - 1], start=True, stop=True
                         ).then_inc(prefix_done, 1)

    @block.scalar
    def _(act):
        act.wait_ge(gap_done, 1)
        nc.scalar.activation(expo[:, :], gap[:, :], ACT.Exp).then_inc(e_done, 1)

    @block.vector
    def _(dve):
        n = 0

        def link(ins):
            nonlocal n
            n += 1
            ins.then_inc(seq, 1)
            dve.wait_ge(seq, n)

        def over_experts(v):
            return v.rearrange("p (t e) -> p t e", e=1).broadcast_to([P, NT, NE])

        def over_tiles(v):
            return v.rearrange("p (e t) -> p e t", t=1).broadcast_to([P, NE, NT])

        def best(values, i, hot):
            link(nc.vector.tensor_reduce(top[:, i, :], values[:, :, :], AX.X, ALU.max))
            link(nc.vector.tensor_tensor(cand[:, :, :], values[:, :, :], over_experts(top[:, i, :]), ALU.is_equal))
            link(nc.vector.tensor_tensor(cand[:, :, :], cand[:, :, :], experts_all, ALU.mult))
            link(nc.vector.tensor_reduce(best_at[:, i, :], cand[:, :, :], AX.X, ALU.min))
            link(nc.vector.tensor_tensor(hot[:, :, :], experts_all, over_experts(best_at[:, i, :]), ALU.is_equal))

        experts_all = cols["experts"].rearrange("p (t e) -> p t e", t=1).broadcast_to([P, NT, NE])
        dve.wait_ge(logits_done, 1)
        link(nc.vector.tensor_copy(logits[:, :, :].rearrange("p t e -> p (t e)"), gate_ps[:, 0:NT * NE]))
        best(logits, 0, first)
        link(nc.vector.scalar_tensor_tensor(logits[:, :, :], first[:, :, :], -FLT_MAX, logits[:, :, :],
                                            ALU.mult, ALU.add))
        best(logits, 1, second)
        nc.vector.tensor_tensor(gap[:, :], top[:, 1, :], top[:, 0, :], ALU.subtract).then_inc(gap_done, 1)
        link(nc.vector.tensor_tensor(both[:, :, :].rearrange("p e t -> p t e"), first[:, :, :], second[:, :, :], ALU.add))
        link(nc.vector.tensor_tensor_scan(upto[:, :, :].rearrange("p e t -> p (e t)"), cols["tile_chain"],
                                          both[:, :, :].rearrange("p e t -> p (e t)"), 0.0, ALU.mult, ALU.add))
        nc.vector.tensor_tensor(before[:, :, :], upto[:, :, :], both[:, :, :], ALU.subtract).then_inc(before_done, 1)
        dve.wait_ge(e_done, 1)
        link(nc.vector.tensor_scalar(denom[:, :], expo[:, :], 1.0, None, ALU.add))
        link(nc.vector.reciprocal(prob[:, 0, :], denom[:, :]))
        link(nc.vector.tensor_tensor(prob[:, 1, :], expo[:, :], prob[:, 0, :], ALU.mult))
        dve.wait_ge(prefix_done, 1)
        link(nc.vector.tensor_copy(count[:, :], count_ps[:, 0:NE]))
        link(nc.vector.tensor_tensor(over[:, :, :], over_tiles(count[:, :]),
                                     cols["whole_blocks"].rearrange("p (e t) -> p e t", e=1).broadcast_to([P, NE, NT]),
                                     ALU.is_gt))
        link(nc.vector.tensor_reduce(blocks[:, :], over[:, :, :], AX.X, ALU.add))
        link(nc.vector.tensor_tensor_scan(block_end[:, :], cols["ones"][:, 0:NE], blocks[:, :], 0.0, ALU.mult, ALU.add))
        link(nc.vector.tensor_tensor(base[:, :], block_end[:, :], blocks[:, :], ALU.subtract))
        link(nc.vector.tensor_scalar(base[:, :], base[:, :], float(P), None, ALU.mult))
        link(nc.vector.tensor_tensor(place[:, :, :], prefix_ps[:, 0:NE * NT].rearrange("p (e t) -> p e t", e=NE),
                                     over_tiles(base[:, :]), ALU.add))
        for i, hot in enumerate((first, second)):
            link(nc.vector.tensor_tensor(mine[:, i, :, :], place[:, :, :], hot[:, :, :].rearrange("p t e -> p e t"),
                                         ALU.mult))
            link(nc.vector.tensor_reduce(slot_f[:, i, :], mine[:, i, :, :].rearrange("p e t -> p t e"), AX.X, ALU.add))
        nc.vector.tensor_copy(slot[:, :, :], slot_f[:, :, :]).then_inc(slot_done, 1)
        link(nc.vector.tensor_tensor(
            ended[:, :, :], block_end[:, :].rearrange("p (b e) -> p b e", b=1).broadcast_to([P, SLOT_BLOCKS, NE]),
            cols["blocks"].rearrange("p (b e) -> p b e", e=1).broadcast_to([P, SLOT_BLOCKS, NE]), ALU.is_le))
        link(nc.vector.tensor_reduce(expert_f[:, :], ended[:, :, :], AX.X, ALU.add))
        link(nc.vector.tensor_scalar(expert_f[:, :], expert_f[:, :], float(NE - 1), None, ALU.min))
        nc.vector.tensor_copy(block_expert[:, :], expert_f[:, :])

    @block.gpsimd
    def _(pool):
        pool.wait_ge(zero_out, 16)
        pool.wait_ge(slot_done, 1)
        for t in range(NT):
            for i in range(2):
                nc.gpsimd.indirect_dma_start(slot_rows, bass.IndirectOffsetOnAxis(ap=slot[:, i, t:t + 1], axis=0),
                                             rows[:, t, :], None).then_inc(scattered, 16)
        pool.wait_ge(scattered, 16 * 2 * NT)


def expert_blocks(nc, ctx, ident, w1, w2, w3, rms_w, block_expert, slot_rows, slot_out, w_in, scattered, stored):
    sb, ps, sem = alloc(nc, ctx)
    HN = DE // 2
    rows = sb("m_block_rows", [P, 2, D])
    yT = sb("m_yT", [P, 2, KD, P])
    gate = sb("m_gate", [P, 2, HN])
    h = sb("m_h", [P, 2, HN])
    hT = sb("m_hT", [P, EC, P])
    out = sb("m_out", [P, 2, D])
    yT_ps = ps("m_yT_ps", [P, NB])
    up_ps = ps("m_up_ps", [P, 2, NB])
    mul_ps = ps("m_mul_ps", [P, 2, NB])
    hT_ps = ps("m_hT_ps", [P, 2, NB])
    out_ps = ps("m_out_ps", [P, NB])
    rows_in = [sem(f"m_rows_in{j}") for j in range(2)]
    rows_turned = sem("m_rows_turned")
    yT_done = sem("m_yT_done")
    up_done = sem("m_up_done")
    gate_done = sem("m_gate_done")
    h_done = sem("m_h_done")
    h_turned = sem("m_h_turned")
    hT_done = sem("m_hT_done")
    out_made = sem("m_out_made")
    out_done = sem("m_out_done")
    block = open_block(nc, ctx, sem)
    LAST = SLOT_BLOCKS - 1
    LOOPED = (SLOT_BLOCKS - 2) // 2
    CB = NB // P

    def steps(engine, step):
        for b in range(2):
            step(0, b, b)
        with engine.Fori(1, LOOPED) as pair:
            for j in range(2):
                step(pair, j, None)
        for b in range(2 * LOOPED, SLOT_BLOCKS):
            step(b // 2, b % 2, b)

    def exists(b, ahead):
        return b is None or b + ahead <= LAST

    @block.sync
    def _(sp):
        def load(first, j):
            sp.dma_start(rows[:, j, :], slot_rows.rearrange("(b p) d -> b p d", p=P)[ds(first + j, 1), :, :]
                         .rearrange("b p d -> p (b d)")).then_inc(rows_in[j], 16)

        def step(pair, j, b):
            n = pair * 2 + j
            if exists(b, 2):
                sp.wait_ge(rows_turned, n + 1)
                load(pair * 2 + 2, j)
            sp.wait_ge(out_done, n + 1)
            sp.dma_start(slot_out.rearrange("(b p) d -> b p d", p=P)[ds(n, 1), :, :].rearrange("b p d -> p (b d)"),
                         out[:, j, :]).then_inc(stored[j], 16)

        for j in range(2):
            load(0, j)
        steps(sp, step)

    @block.tensor
    def _(pe):
        def turn_rows(pair, j):
            n = pair * 2 + j
            pe.wait_ge(rows_in[j], pair * 16 + 16)
            pe.wait_ge(yT_done, n)
            for c in range(KD):
                ins = nc.tensor.transpose(yT_ps[:, c * P:(c + 1) * P], rows[:, j, c * P:(c + 1) * P], ident[:, :])
            ins.then_inc(rows_turned, 1)

        def products(pair, j):
            n = pair * 2 + j
            e = pe.value_load(block_expert[0:1, ds(n, 1)], min_val=0, max_val=NE - 1)
            pe.wait_ge(yT_done, n + 1)
            pe.wait_ge(h_done, n)
            for dst, w in ((up_ps, w1), (mul_ps, w2)):
                for half in range(2):
                    for k in range(KD):
                        ins = nc.tensor.matmul(
                            dst[:, half, 0:HN], yT[:, j, k, :],
                            w[:, ds(e, 1), k, half * HN:(half + 1) * HN].rearrange("p e n -> p (e n)"),
                            start=k == 0, stop=k == KD - 1)
            ins.then_inc(up_done, 1)

        def step(pair, j, b):
            n = pair * 2 + j
            pe.wait_ge(h_done, n + 1)
            pe.wait_ge(hT_done, n * 2)
            for c in range(EC):
                m = ELAST if c == EC - 1 else P
                ins = nc.tensor.transpose(hT_ps[0:m, c // CB, c % CB * P:(c % CB + 1) * P],
                                          h[:, :, :].rearrange("p a n -> p (a n)")[:, c * P:c * P + m], ident[:, :])
                if c in (CB - 1, EC - 1):
                    ins.then_inc(h_turned, 1)
            if exists(b, 1):
                products(pair + (1 if j else 0), 1 - j)
            if exists(b, 2):
                turn_rows(pair + 1, j)
            e = pe.value_load(block_expert[0:1, ds(n, 1)], min_val=0, max_val=NE - 1)
            pe.wait_ge(hT_done, n * 2 + 2)
            pe.wait_ge(out_done, n)
            for c in range(EC):
                m = ELAST if c == EC - 1 else P
                ins = nc.tensor.matmul(out_ps[:, 0:D], hT[0:m, c, :],
                                       w3[0:m, ds(e, 1), c, :].rearrange("p e n -> p (e n)"),
                                       start=c == 0, stop=c == EC - 1)
            ins.then_inc(out_made, 1)

        turn_rows(0, 0)
        turn_rows(0, 1)
        pe.wait_ge(w_in, 16 * 3 * NE)
        products(0, 0)
        steps(pe, step)

    @block.scalar
    def _(act):
        def take_rows(n, j):
            act.wait_ge(rows_turned, n + 1)
            for c in range(KD):
                ins = nc.scalar.activation(yT[:, j, c, :], yT_ps[:, c * P:(c + 1) * P], ACT.Copy, scale=rms_w[:, c:c + 1])
            ins.then_inc(yT_done, 1)

        def silu(n):
            act.wait_ge(up_done, n + 1)
            act.wait_ge(h_done, n)
            nc.scalar.activation(gate[:, :, :], up_ps[:, :, 0:HN], ACT.Silu).then_inc(gate_done, 1)

        def step(pair, j, b):
            n = pair * 2 + j
            act.wait_ge(h_turned, n * 2 + 1)
            act.wait_ge(out_made, n)
            nc.scalar.activation(hT[:, 0:CB, :].rearrange("p c n -> p (c n)"), hT_ps[:, 0, :], ACT.Copy
                                 ).then_inc(hT_done, 1)
            if exists(b, 1):
                silu(n + 1)
            if exists(b, 2):
                take_rows(n + 2, j)

        take_rows(0, 0)
        take_rows(1, 1)
        silu(0)
        steps(act, step)

    @block.vector
    def _(dve):
        def hidden(n):
            dve.wait_ge(gate_done, n + 1)
            dve.wait_ge(h_turned, n * 2)
            nc.vector.tensor_tensor(h[:, :, :], mul_ps[:, :, 0:HN], gate[:, :, :], ALU.mult).then_inc(h_done, 1)

        def step(pair, j, b):
            n = pair * 2 + j
            dve.wait_ge(h_turned, n * 2 + 2)
            dve.wait_ge(out_made, n)
            nc.vector.tensor_copy(hT[:, CB, :], hT_ps[:, 1, 0:P])
            nc.vector.tensor_copy(hT[0:ELAST, CB + 1, :], hT_ps[0:ELAST, 1, P:2 * P]).then_inc(hT_done, 1)
            if exists(b, 1):
                hidden(n + 1)
            dve.wait_ge(out_made, n + 1)
            if b is None or b > 1:
                dve.wait_ge(stored[j], pair * 16)
            nc.vector.tensor_copy(out[:, j, :], out_ps[:, 0:D]).then_inc(out_done, 1)

        hidden(0)
        steps(dve, step)


def mamba(nc, x_sb, ident, a):
    with ExitStack() as ctx:
        sb, _, outer_sem = alloc(nc, ctx)
        zs = sb("b_zs", [P, CI, TOK])
        xc = sb("b_xc", [P, 2, CI, TOK])
        xdbl = sb("b_xdbl", [R + 2 * NS, 2, TOK])
        wx = sb("b_wx", [P, 2, CI, R + 2 * NS])
        wdt = sb("b_wdt", [R, 2, DI])
        wout = sb("b_wout", [P, CI, D])
        vecs = sb("b_vecs", [P, 2, CI, KC + 3])
        a_log = sb("b_a_log", [P, 2, CI, NS])
        b_rows = nc.dram_tensor("b_b_rows", (2, NS, TOK), F32, kind="Internal").ap()
        c_rows = nc.dram_tensor("b_c_rows", (2, 2, NS, TOK), F32, kind="Internal").ap()
        dir_in = outer_sem("b_dir_in")
        project(nc, x_sb, ident, a, zs, xc, xdbl, wx, wdt, wout, vecs, a_log, b_rows, c_rows, dir_in)
        recur(nc, ctx, outer_sem, x_sb, ident, zs, xc, xdbl, wdt, wout, vecs, a_log, b_rows, c_rows)


def by_sequence(ap):
    return ap.rearrange("p (s l) -> p s l", l=LQ)


def project(nc, x_sb, ident, a, zs, xc, xdbl, wx, wdt, wout, vecs, a_log, b_rows, c_rows, dir_in):
    SEQ = NB // LQ
    DIR_LOADS = 9
    ROWS = R + 2 * NS
    with ExitStack() as ctx:
        sb, ps, sem = alloc(nc, ctx)
        xnT = normed(nc, ctx, "b")
        win = sb("b_win", [P, KD, 2 * DI])
        xpad = sb("b_xpad", [P, 2, SEQ, PADL])
        hi = sb("b_hi", [ROWS, 2, NB], F32R)
        lo = sb("b_lo", [ROWS, 2, NB], F32R)
        w_in = sem("b_win_in")

        def loads(sp):
            sp.dma_start(win[:, :, :], a["b_win"]).then_inc(w_in, 16)
            sp.dma_start(wout[:, :, :], a["b_wout"]).then_inc(dir_in, 16)
            for d, tag in enumerate("fr"):
                sp.dma_start(wx[:, d, :, :], a[f"b{tag}_wx"]).then_inc(dir_in, 16)
                sp.dma_start(wdt[:, d, :], a[f"b{tag}_wdt"]).then_inc(dir_in, 16)
                sp.dma_start(vecs[:, d, :, :], a[f"b{tag}_vecs"]).then_inc(dir_in, 16)
                sp.dma_start(a_log[:, d, :, :], a[f"b{tag}_a_log"]).then_inc(dir_in, 16)

        layer_norm(nc, "ln_b", x_sb, xnT, ident, loads=loads)
        x_ps = ps("b_x_ps", [P, 2, NB])
        z_ps = ps("b_z_ps", [P, 2, NB])
        dbl_ps = ps("b_dbl_ps", [ROWS, 2, NB])
        zeroed = sem("b_zeroed")
        x_done = sem("b_x_done")
        z_done = sem("b_z_done")
        x_moved = sem("b_x_moved")
        z_moved = sem("b_z_moved")
        conv_step = sem("b_conv_step")
        xc_done = sem("b_xc_done")
        dbl_done = sem("b_dbl_done")
        hi_done = sem("b_hi_done")
        lo_done = sem("b_lo_done")
        rows_out = sem("b_rows_out")
        rows_free = sem("b_rows_free")
        block = open_block(nc, ctx, sem)

        @block.sync
        def _(sp):
            with sp.Fori(0, NBLK) as blk:
                for d in range(2):
                    tokens = ds(blk * NB, NB)
                    sp.wait_ge(lo_done, blk * 2 + d + 3)
                    sp.dma_start(b_rows[d, :, tokens], xdbl[R:R + NS, d, tokens]).then_inc(rows_out, 16)
                    for i, part in enumerate((hi, lo)):
                        sp.dma_start(c_rows[d, i, :, tokens], part[R + NS:, d, :].bitcast(F32)).then_inc(rows_out, 16)
                    sp.wait_ge(rows_out, blk * (2 * 48) + (d + 1) * 48)
                    sp.sem_inc(rows_free, 1)

        @block.tensor
        def _(pe):
            pe.wait_ge(w_in, 16)
            pe.wait_ge(dir_in, 16 * DIR_LOADS)
            pe.sem_inc(x_moved, 2)
            pe.sem_inc(z_moved, 2)

            def to_rows(blk):
                for d in range(2):
                    pe.wait_ge(xc_done, blk * (2 * CI) + 2 * CI)
                    pe.wait_ge(lo_done, blk * 2 + d + 1)
                    for c in range(CI):
                        ins = nc.tensor.matmul(dbl_ps[:, d, :], wx[:, d, c, :], xc[:, d, c, ds(blk * NB, NB)],
                                               start=c == 0, stop=c == CI - 1)
                    ins.then_inc(dbl_done, 1)

            def input_block(blk, first=False):
                for c in range(CI):
                    for i, (dst, moved, done) in enumerate(((x_ps, x_moved, x_done), (z_ps, z_moved, z_done))):
                        pe.wait_ge(moved, blk * CI + (c + 1))
                        for k in range(KD):
                            ins = nc.tensor.matmul(dst[:, c % 2, :], win[:, k, i * DI + c * P:i * DI + (c + 1) * P],
                                                   xnT[:, k, ds(blk * NB, NB)], start=k == 0, stop=k == KD - 1)
                        ins.then_inc(done, 1)
                    if c == 2 and not first:
                        to_rows(blk - 1)

            input_block(0, first=True)
            with pe.Fori(1, NBLK) as blk:
                input_block(blk)
            to_rows(NBLK - 1)

        @block.scalar
        def _(act):
            act.wait_ge(zeroed, 1)

            def silu(blk, c):
                for d in range(2):
                    act.wait_ge(conv_step, blk * (CI * 2 * KC) + (c * 2 * KC + 2 * (KC - 1) + d + 1))
                    t = xc[:, d, c, ds(blk * NB, NB)]
                    nc.scalar.activation(t, t, ACT.Silu).then_inc(xc_done, 1)

            def take_rows(blk):
                for d in range(2):
                    act.wait_ge(dbl_done, blk * 2 + d + 1)
                    nc.scalar.activation(xdbl[:, d, ds(blk * NB, NB)], dbl_ps[:, d, :], ACT.Copy)
                    act.wait_ge(rows_free, blk * 2 + d + 1)
                    nc.scalar.activation(hi[R:, d, :], dbl_ps[R:, d, :], ACT.Copy).then_inc(hi_done, 1)

            def input_block(blk, first=False):
                for c in range(CI):
                    act.wait_ge(x_done, blk * CI + (c + 1))
                    if not first or c > 1:
                        act.wait_ge(conv_step, blk * (CI * 2 * KC) + (c - 1) * 2 * KC)
                    nc.scalar.activation(xpad[:, c % 2, :, KC - 1:KC - 1 + LQ], by_sequence(x_ps[:, c % 2, :]), ACT.Copy
                                         ).then_inc(x_moved, 1)
                    act.wait_ge(z_done, blk * CI + (c + 1))
                    nc.scalar.activation(zs[:, c, ds(blk * NB, NB)], z_ps[:, c % 2, :], ACT.Silu).then_inc(z_moved, 1)
                    if c > 0:
                        silu(blk, c - 1)
                    elif not first:
                        silu(blk - 1, CI - 1)
                    if c == CI - 1 and not first:
                        take_rows(blk - 1)

            input_block(0, first=True)
            with act.Fori(1, NBLK) as blk:
                input_block(blk)
            silu(NBLK - 1, CI - 1)
            take_rows(NBLK - 1)

        @block.vector
        def _(dve):
            nc.vector.memset(xpad[:, :, :, 0:KC - 1], 0.0)
            nc.vector.memset(xpad[:, :, :, KC - 1 + LQ:], 0.0).then_inc(zeroed, 1)
            dve.sem_inc(lo_done, 2)
            dve.sem_inc(rows_free, 2)

            def low_parts(blk):
                for d in range(2):
                    dve.wait_ge(hi_done, blk * 2 + d + 1)
                    nc.vector.tensor_tensor(lo[R:, d, :], dbl_ps[R:, d, :], hi[R:, d, :].bitcast(F32), ALU.subtract
                                            ).then_inc(lo_done, 1)

            def convolve(blk, c):
                dve.wait_ge(x_moved, blk * CI + (c + 3))
                for tap in range(KC):
                    for d in range(2):
                        out = by_sequence(xc[:, d, c, ds(blk * NB, NB)])
                        off = KC - 1 - tap + KC - 1 if d else tap
                        window = xpad[:, c % 2, :, off:off + LQ]
                        if tap == 0:
                            ins = nc.vector.tensor_scalar(out, window, vecs[:, d, c, 0:1], vecs[:, d, c, KC:KC + 1],
                                                          ALU.mult, ALU.add)
                        else:
                            dve.wait_ge(conv_step, blk * (CI * 2 * KC) + (c * 2 * KC + 2 * (tap - 1) + d + 1))
                            ins = nc.vector.scalar_tensor_tensor(out, window, vecs[:, d, c, tap:tap + 1], out,
                                                                 ALU.mult, ALU.add)
                        ins.then_inc(conv_step, 1)

            dve.wait_ge(dir_in, 16 * DIR_LOADS)
            for c in range(CI):
                convolve(0, c)
            with dve.Fori(1, NBLK) as blk:
                for c in range(CI):
                    convolve(blk, c)
                low_parts(blk - 1)
            low_parts(NBLK - 1)


def recur(nc, ctx, outer_sem, x_sb, ident, zs, xc, xdbl, wdt, wout, vecs, a_log, b_rows, c_rows):
    sb, ps, sem = alloc(nc, ctx)
    PASSES = 2 * NBLK
    TPH = TPB // 2
    NCH = NS * CI
    a_neg = sb("b_a_neg", [P, 2, CI, NS])
    diag = sb("b_diag", [P, 2, CI, P])
    ones = sb("b_ones", [1, P], F32R)
    table = sb("b_table", [P, 1])
    dt = sb("b_dt", [P, CI, NB])
    dtx = sb("b_dtx", [P, CI, NB])
    b_all = sb("b_b_all", [P, 2, NB])
    c_row = sb("b_c_row", [1, 2, 2, NB], F32R)
    drive = sb("b_drive", [P, CI, NB])
    state = sb("b_state", [P, CI, NB])
    read = sb("b_read", [P, CI, NB])
    acc_ps = ps("b_acc_ps", [P, CI, NB])
    c_ps = ps("b_c_ps", [P, 2, NB])
    decay_ps = ps("b_decay_ps", [P, 2, NB])
    a_done = sem("b_a_done")
    const_done = sem("b_const_done")
    b_in = [sem(f"b_b_in{j}") for j in range(2)]
    c_in = [sem(f"b_c_in{j}") for j in range(2)]
    step_done = sem("b_step_done")
    abs_done = sem("b_abs_done")
    exp_done = sem("b_exp_done")
    soft_done = sem("b_soft_done")
    relu_done = sem("b_relu_done")
    dt_done = sem("b_dt_done")
    dtx_done = sem("b_dtx_done")
    c_ready = sem("b_c_ready")
    edge_done = sem("b_edge_done")
    decay_done = sem("b_decay_done")
    drive_done = sem("b_drive_done")
    state_done = sem("b_state_done")
    read_done = sem("b_read_done")
    acc_done = sem("b_acc_done")
    y_done = sem("b_y_done")
    out_done = sem("b_out_done")
    x_done = sem("b_x_done")
    sem.taken.extend(outer_sem.taken)
    block = open_block(nc, ctx, sem)

    def direction(p):
        return p // NBLK, p % NBLK

    def step(p, n2, j, c):
        return n2 * (2 * CI) + (p * NCH + j * CI + c)

    def inside(p):
        return slice(0, LQ - 1) if direction(p)[0] else slice(1, LQ)

    def tokens(p):
        return slice(direction(p)[1] * NB, (direction(p)[1] + 1) * NB)

    @block.sync
    def _(sp):
        for p in range(PASSES):
            d, blk = direction(p)
            with sp.Fori(0, NS // 2) as n2:
                for j in range(2):
                    state_rows = ds(n2 * 2 + j, 1)
                    sp.wait_ge(drive_done, step(p, n2, j, 0) + CI)
                    sp.dma_start(b_all[:, j, :], b_rows[d, state_rows, tokens(p)].rearrange("n t -> (n t)")
                                 .partition_broadcast(P)).then_inc(b_in[j], 16)
                    sp.wait_ge(c_ready, n2 * 2 + (p * NS + j + 1))
                    sp.dma_start(c_row[:, j, :, :].bitcast(F32),
                                 c_rows[d, :, state_rows, tokens(p)].rearrange("i n t -> n i t")
                                 ).then_inc(c_in[j], 16)

    @block.tensor
    def _(pe):
        pe.sem_inc(c_ready, 2)
        pe.wait_ge(const_done, 1)

        def make_c(p, n2, j):
            pe.wait_ge(c_in[j], n2 * 16 + (p * (NS // 2) * 16 + 16))
            pe.wait_ge(read_done, step(p, n2, j, 0) + CI)
            nc.tensor.matmul(c_ps[:, j, :], ones[:, :], c_row[:, j, 0, :], start=True, stop=False)
            nc.tensor.matmul(c_ps[:, j, :], ones[:, :], c_row[:, j, 1, :], start=False, stop=True).then_inc(c_ready, 1)

        def states(p, n2, last):
            for j in range(2):
                if j == 0:
                    make_c(p, n2, 1)
                elif not last:
                    make_c(p, n2 + 1, 0)
                for c in range(CI):
                    pe.wait_ge(read_done, step(p, n2, j, c) + 2 * CI + 1)
                    nc.tensor.matmul(acc_ps[:, c, :], ident[:, :], read[:, c, :], start=False, stop=True,
                                     skip_group_check=True).then_inc(acc_done, 1)

        def output(p):
            d, blk = direction(p)
            for i in range(TPB):
                for c in range(CI):
                    t = blk * TPB + i
                    ins = nc.tensor.matmul(c_ps[:, i // TPH, i % TPH * D:(i % TPH + 1) * D],
                                           xc[:, d, c, t * P:(t + 1) * P], wout[:, c, :], start=c == 0, stop=c == CI - 1)
                if i % TPH == TPH - 1:
                    ins.then_inc(out_done, 1)

        for p in range(PASSES):
            d, blk = direction(p)
            for c in range(CI):
                if p > 0:
                    pe.wait_ge(y_done, (p - 1) * CI + c + 1)
                nc.tensor.matmul(acc_ps[:, c, :], wdt[:, d, c * P:(c + 1) * P], xdbl[0:R, d, tokens(p)],
                                 start=True, stop=True).then_inc(step_done, 1)
            if p > 0:
                output(p - 1)
            for c in range(CI):
                pe.wait_ge(relu_done, p * CI + c + 1)
                nc.tensor.matmul(acc_ps[:, c, :], diag[:, d, c, :], xc[:, d, c, tokens(p)], start=True, stop=True)
            if p > 0:
                pe.wait_ge(x_done, p * 2)
            make_c(p, 0, 0)
            with pe.Fori(0, NS // 2 - 1) as n2:
                states(p, n2, False)
            states(p, NS // 2 - 1, True)
        pe.wait_ge(y_done, PASSES * CI)
        output(PASSES - 1)

    @block.scalar
    def _(act):
        nc.scalar.activation(a_neg[:, :, :, :], a_log[:, :, :, :], ACT.Exp).then_inc(a_done, 1)
        for p in range(PASSES):
            d, blk = direction(p)
            if p > 0:
                act.wait_ge(drive_done, p * NCH + 2 * CI)
            bias = vecs[:, d, :, KC + 1:KC + 2]
            for c in range(CI):
                act.wait_ge(step_done, p * CI + c + 1)
                nc.scalar.activation(dtx[:, c, :], acc_ps[:, c, :], ACT.Abs, bias=bias[:, c, :]).then_inc(abs_done, 1)
            for c in range(CI):
                act.wait_ge(abs_done, p * CI + c + 1)
                nc.scalar.activation(dtx[:, c, :], dtx[:, c, :], ACT.Exp, scale=-1.0).then_inc(exp_done, 1)
            for c in range(CI):
                act.wait_ge(exp_done, p * CI + c + 1)
                nc.scalar.activation(dtx[:, c, :], dtx[:, c, :], ACT.Ln, bias=1.0).then_inc(soft_done, 1)
            if p == 0:
                act.wait_ge(a_done, 2)
            nc.scalar.activation(table[:, :], a_neg[:, 0, 0, 0:1], ACT.Exp)
            act.wait_ge(edge_done, d + 1)
            with act.Fori(0, NS // 2) as n2:
                for j in range(2):
                    for c in range(CI):
                        if j == 0:
                            act.wait_ge(dt_done, p * CI + c + 1)
                        act.wait_ge(state_done, step(p, n2, j, c) + 1)
                        nc.scalar.activation(by_sequence(decay_ps[:, c % 2, :])[:, :, inside(p)],
                                             by_sequence(dt[:, c, :])[:, :, inside(p)], ACT.Exp,
                                             scale=a_neg[:, d, c, ds(n2 * 2 + j, 1)]).then_inc(decay_done, 1)

    @block.gpsimd
    def _(pool):
        pool.sem_inc(drive_done, 2 * CI)
        for p in range(PASSES):
            with pool.Fori(0, NS // 2) as n2:
                for j in range(2):
                    for c in range(CI):
                        if c == 0:
                            pool.wait_ge(b_in[j], n2 * 16 + (p * (NS // 2) * 16 + 16))
                        if j == 0:
                            pool.wait_ge(dtx_done, p * CI + c + 1)
                        pool.wait_ge(read_done, step(p, n2, j, c) + CI + 1)
                        nc.gpsimd.tensor_tensor(drive[:, c, :], b_all[:, j, :], dtx[:, c, :], ALU.mult
                                                ).then_inc(drive_done, 1)

    @block.vector
    def _(dve):
        dve.sem_inc(state_done, 2)
        dve.sem_inc(read_done, 2 * CI)
        dve.sem_inc(acc_done, CI)
        nc.vector.memset(ones[:, :].bitcast(F32), 1.0)
        for d in range(2):
            for c in range(CI):
                ins = nc.vector.tensor_scalar(diag[:, d, c, :], ident[:, :], vecs[:, d, c, KC + 2:KC + 3], None, ALU.mult)
        ins.then_inc(const_done, 1)
        dve.wait_ge(a_done, 1)
        nc.vector.tensor_scalar(a_neg[:, :, :, :], a_neg[:, :, :, :], -1.0, None, ALU.mult).then_inc(a_done, 1)

        def scan(p, n2, j, c):
            k = step(p, n2, j, c)
            dve.wait_ge(drive_done, k + 2 * CI + 1)
            dve.wait_ge(decay_done, k + 1)

            def order(ap):
                return ap[:, ::-1] if direction(p)[0] else ap

            nc.vector.tensor_tensor_scan(order(state[:, c, :]), order(decay_ps[:, c % 2, :]), order(drive[:, c, :]),
                                         0.0, ALU.mult, ALU.add).then_inc(state_done, 1)

        def states(p, n2, last):
            for j in range(2):
                for c in range(CI):
                    k = step(p, n2, j, c)
                    if c < CI - 1:
                        scan(p, n2, j, c + 1)
                    elif j == 0:
                        scan(p, n2, 1, 0)
                    elif not last:
                        scan(p, n2 + 1, 0, 0)
                    dve.wait_ge(state_done, k + 3)
                    dve.wait_ge(acc_done, k + 1)
                    if c == 0:
                        dve.wait_ge(c_ready, n2 * 2 + (p * NS + j + 3))
                    nc.vector.tensor_tensor(read[:, c, :], c_ps[:, j, :], state[:, c, :], ALU.mult
                                            ).then_inc(read_done, 1)

        def add_output(p):
            for i in range(2):
                dve.wait_ge(out_done, p * 2 + i + 1)
                t = direction(p)[1] * TPB + i * TPH
                x_t = x_sb[:, t:t + TPH, :].rearrange("p a d -> p (a d)")
                nc.vector.tensor_tensor(x_t, c_ps[:, i, 0:TPH * D], x_t, ALU.add).then_inc(x_done, 1)

        for p in range(PASSES):
            d, blk = direction(p)
            if blk == 0:
                edge = slice(LQ - 1, LQ) if d else slice(0, 1)
                for j in range(2):
                    ins = nc.vector.memset(by_sequence(decay_ps[:, j, :])[:, :, edge], 0.0)
                ins.then_inc(edge_done, 1)
            for c in range(CI):
                dve.wait_ge(abs_done, p * CI + c + 1)
                nc.vector.tensor_scalar(dt[:, c, :], acc_ps[:, c, :], vecs[:, d, c, KC + 1:KC + 2], 0.0,
                                        ALU.add, ALU.max).then_inc(relu_done, 1)
            for c in range(CI + 1):
                if c < CI:
                    dve.wait_ge(relu_done, p * CI + c + 1)
                    dve.wait_ge(soft_done, p * CI + c + 1)
                    nc.vector.tensor_tensor(dt[:, c, :], dt[:, c, :], dtx[:, c, :], ALU.add).then_inc(dt_done, 1)
                if c > 0:
                    dve.wait_ge(dt_done, p * CI + c)
                    nc.vector.tensor_tensor(dtx[:, c - 1, :], dt[:, c - 1, :], xc[:, d, c - 1, tokens(p)], ALU.mult
                                            ).then_inc(dtx_done, 1)
            if p > 0:
                add_output(p - 1)
            scan(p, 0, 0, 0)
            with dve.Fori(0, NS // 2 - 1) as n2:
                states(p, n2, False)
            states(p, NS // 2 - 1, True)
            for c in range(CI):
                dve.wait_ge(acc_done, (p + 1) * NCH + c + 1)
                nc.vector.tensor_tensor(xc[:, d, c, tokens(p)], acc_ps[:, c, :], zs[:, c, tokens(p)], ALU.mult
                                        ).then_inc(y_done, 1)
        add_output(PASSES - 1)


def feed_forward(nc, x_sb, ident, a):
    TOPK = 2
    with ExitStack() as ctx:
        sb, ps, sem = alloc(nc, ctx)
        xnT = normed(nc, ctx, "f")
        wi = sb("f_wi", [P, KD, FF])
        wo = sb("f_wo", [P, CF, D])
        wk = sb("f_wk", [P, TOPK, KD, FF])
        lora_a = sb("f_lora_a", [RANK, TOPK, D])
        lora_b = sb("f_lora_b", [RANK, TOPK, FF])
        index = sb("f_index", [1, TOPK], I32)
        value = sb("f_value", [P, TOPK])
        i_in = sem("f_i_in")
        w_in = sem("f_w_in")
        lora_in = sem("f_lora_in")

        def loads(sp):
            sp.dma_start(index[:, :], a["f_index"]).then_inc(i_in, 16)
            sp.dma_start(wi[:, :, :], a["f_wi"]).then_inc(w_in, 16)
            sp.dma_start(wo[:, :, :], a["f_wo"]).then_inc(w_in, 16)
            sp.dma_start(value[:, :], a["f_value"].partition_broadcast(P)).then_inc(w_in, 16)
            sp.wait_ge(i_in, 16)
            for k in range(TOPK):
                e = sp.value_load(index[0:1, k:k + 1], min_val=0, max_val=NE - 1)
                sp.dma_start(lora_a[:, k, :], a["f_lora_a"][ds(e, 1), :, :].rearrange("e r d -> r (e d)")
                             ).then_inc(lora_in, 16)
                sp.dma_start(lora_b[:, k, :], a["f_lora_b"][ds(e, 1), :, :].rearrange("e r f -> r (e f)")
                             ).then_inc(lora_in, 16)

        layer_norm(nc, "ln_f", x_sb, xnT, ident, loads=loads)
        x_hi = sb("f_x_hi", [P, KD, TOK], F32R)
        x_lo = sb("f_x_lo", [P, KD, TOK], F32R)
        wk_hi = sb("f_wk_hi", [P, TOPK, KD, FF], F32R)
        wk_lo = sb("f_wk_lo", [P, TOPK, KD, FF], F32R)
        wo_hi = sb("f_wo_hi", [P, CF, D], F32R)
        wo_lo = sb("f_wo_lo", [P, CF, D], F32R)
        h0 = sb("f_h0", [P, 2, NB])
        h1 = sb("f_h1", [P, 2, NB])
        h = sb("f_h", [P, 2, NB])
        h_hi = sb("f_h_hi", [P, CF, NB], F32R)
        h_lo = sb("f_h_lo", [P, CF, NB], F32R)
        first_ps = ps("f_first_ps", [P, 2, NB])
        second_ps = ps("f_second_ps", [P, 2, NB])
        out_ps = ps("f_out_ps", [P, TPB, NB])
        lora_done = sem("f_lora_done")
        wk_done = sem("f_wk_done")
        wk_hi_done = sem("f_wk_hi_done")
        wk_lo_done = sem("f_wk_lo_done")
        wo_hi_done = sem("f_wo_hi_done")
        wo_lo_done = sem("f_wo_lo_done")
        x_hi_done = sem("f_x_hi_done")
        x_lo_done = sem("f_x_lo_done")
        up_done = sem("f_up_done")
        h0_done = sem("f_h0_done")
        h1_done = sem("f_h1_done")
        h_done = sem("f_h_done")
        h_hi_done = sem("f_h_hi_done")
        h_lo_done = sem("f_h_lo_done")
        h_used = sem("f_h_used")
        x_done = sem("f_x_done")
        block = open_block(nc, ctx, sem)
        FB = FF // NB
        LORA = [(k, c, slice(j * NB, (j + 1) * NB)) for k in range(TOPK) for c in range(KD) for j in range(FB)]

        def part(blk):
            return slice(blk * NB, (blk + 1) * NB)

        @block.tensor
        def _(pe):
            for free, n in ((h0_done, 2), (h1_done, 2), (h_done, 2), (h_lo_done, 2), (h_used, CF), (x_done, TPB)):
                pe.sem_inc(free, n)
            pe.wait_ge(lora_in, 16 * 2 * TOPK)
            for n, (k, c, cols) in enumerate(LORA):
                if n >= 2:
                    pe.wait_ge(wk_done, n - 1)
                nc.tensor.matmul(first_ps[:, n % 2, :], lora_a[:, k, c * P:(c + 1) * P], lora_b[:, k, cols],
                                 start=True, stop=True).then_inc(lora_done, 1)
            pe.wait_ge(wk_lo_done, len(LORA))
            with pe.Fori(0, NBLK) as blk:
                for c in range(CF):
                    for k, dst in enumerate((first_ps, second_ps)):
                        if c == 0 and k == 0:
                            pe.wait_ge(x_lo_done, blk + 1)
                        pe.wait_ge(h0_done if k == 0 else h1_done, blk * CF + c + 1)
                        for i in range(KD):
                            for m, (w, xs) in enumerate(((wk_hi, x_hi), (wk_hi, x_lo), (wk_lo, x_hi))):
                                ins = nc.tensor.matmul(dst[:, c % 2, :], w[:, k, i, c * P:(c + 1) * P],
                                                       xs[:, i, ds(blk * NB, NB)], start=i == 0 and m == 0,
                                                       stop=i == KD - 1 and m == 2)
                        ins.then_inc(up_done, 1)
                pe.wait_ge(wo_lo_done, 1)
                pe.wait_ge(x_done, blk * TPB + TPB)
                for c in range(CF):
                    pe.wait_ge(h_lo_done, blk * CF + c + 3)
                    for i in range(TPB):
                        rows = slice(i * P, (i + 1) * P)
                        for m, (hs, w) in enumerate(((h_hi, wo_hi), (h_hi, wo_lo), (h_lo, wo_hi))):
                            ins = nc.tensor.matmul(out_ps[:, i, 0:D], hs[:, c, rows], w[:, c, :],
                                                   start=c == 0 and m == 0, stop=c == CF - 1 and m == 2)
                    ins.then_inc(h_used, 1)

        @block.scalar
        def _(act):
            def split_x(blk):
                nc.scalar.activation(x_hi[:, :, part(blk)], xnT[:, :, part(blk)], ACT.Copy).then_inc(x_hi_done, 1)

            split_x(0)
            for n, (k, c, cols) in enumerate(LORA):
                act.wait_ge(wk_done, n + 1)
                nc.scalar.activation(wk_hi[:, k, c, cols], wk[:, k, c, cols], ACT.Copy).then_inc(wk_hi_done, 1)
            act.wait_ge(w_in, 48)
            nc.scalar.activation(wo_hi[:, :, :], wo[:, :, :], ACT.Copy).then_inc(wo_hi_done, 1)
            for blk in range(1, NBLK):
                split_x(blk)

            def split_h(blk, c):
                act.wait_ge(h_done, blk * CF + c + 3)
                act.wait_ge(h_used, blk * CF + c + 1)
                nc.scalar.activation(h_hi[:, c, :], h[:, c % 2, :], ACT.Copy).then_inc(h_hi_done, 1)

            with act.Fori(0, NBLK) as blk:
                for c in range(CF):
                    act.wait_ge(up_done, blk * (2 * CF) + 2 * c + 2)
                    act.wait_ge(h_done, blk * CF + c + 1)
                    nc.scalar.activation(h1[:, c % 2, :], second_ps[:, c % 2, :], ACT.Relu).then_inc(h1_done, 1)
                    if c > 0:
                        split_h(blk, c - 1)
                split_h(blk, CF - 1)

        @block.vector
        def _(dve):
            def split_x(blk):
                dve.wait_ge(x_hi_done, blk + 1)
                nc.vector.tensor_tensor(x_lo[:, :, part(blk)], xnT[:, :, part(blk)], x_hi[:, :, part(blk)].bitcast(F32),
                                        ALU.subtract).then_inc(x_lo_done, 1)

            def split_wk(n):
                k, c, cols = LORA[n]
                dve.wait_ge(wk_hi_done, n + 1)
                nc.vector.tensor_tensor(wk_lo[:, k, c, cols], wk[:, k, c, cols], wk_hi[:, k, c, cols].bitcast(F32),
                                        ALU.subtract).then_inc(wk_lo_done, 1)

            split_x(0)
            dve.wait_ge(w_in, 48)
            for n, (k, c, cols) in enumerate(LORA):
                dve.wait_ge(lora_done, n + 1)
                nc.vector.tensor_tensor(wk[:, k, c, cols], first_ps[:, n % 2, :], wi[:, c, cols], ALU.add
                                        ).then_inc(wk_done, 1)
                if n > 0:
                    split_wk(n - 1)
            split_wk(len(LORA) - 1)
            dve.wait_ge(wo_hi_done, 1)
            nc.vector.tensor_tensor(wo_lo[:, :, :], wo[:, :, :], wo_hi[:, :, :].bitcast(F32), ALU.subtract
                                    ).then_inc(wo_lo_done, 1)
            for blk in range(1, NBLK):
                split_x(blk)

            def split_h(blk, c):
                dve.wait_ge(h_hi_done, blk * CF + c + 1)
                nc.vector.tensor_tensor(h_lo[:, c, :], h[:, c % 2, :], h_hi[:, c, :].bitcast(F32), ALU.subtract
                                        ).then_inc(h_lo_done, 1)

            with dve.Fori(0, NBLK) as blk:
                for c in range(CF):
                    dve.wait_ge(up_done, blk * (2 * CF) + 2 * c + 1)
                    dve.wait_ge(h_done, blk * CF + c + 1)
                    nc.vector.tensor_scalar(h0[:, c % 2, :], first_ps[:, c % 2, :], 0.0, value[:, 0:1],
                                            ALU.max, ALU.mult).then_inc(h0_done, 1)
                    dve.wait_ge(h0_done, blk * CF + c + 3)
                    dve.wait_ge(h1_done, blk * CF + c + 3)
                    dve.wait_ge(h_lo_done, blk * CF + c + 1)
                    nc.vector.scalar_tensor_tensor(h[:, c % 2, :], h1[:, c % 2, :], value[:, 1:2], h0[:, c % 2, :],
                                                   ALU.mult, ALU.add).then_inc(h_done, 1)
                    if c > 0:
                        split_h(blk, c - 1)
                split_h(blk, CF - 1)
                dve.wait_ge(h_used, blk * CF + 2 * CF)
                for i in range(TPB):
                    x_t = x_sb[:, ds(blk * TPB + i, 1), :].rearrange("p a d -> p (a d)")
                    nc.vector.tensor_tensor(x_t, out_ps[:, i, 0:D], x_t, ALU.add).then_inc(x_done, 1)


def program(nc, a, out):
    with ExitStack() as ctx:
        sb, ps, sem = alloc(nc, ctx)
        x_all = sb("x_all", [P, NT + 1, D])
        x_sb = x_all[:, 1:, :]
        ident = sb("ident", [P, P])
        pair_mask = sb("pair_mask", [PAIRS, PAIRS])
        x_in = sem("x_in")
        x_out = sem("x_out")
        with nc.Block() as block:
            @block.vector
            def _(dve):
                nc.vector.memset(x_all[:, 0, :], 0.0)

            @block.sync
            def _(sp):
                sp.dma_start(x_sb[:, :, :], a["x"].rearrange("(t p) d -> p t d", p=P)).then_inc(x_in, 16)
                sp.dma_start(ident[:, :], a["ident"]).then_inc(x_in, 16)
                sp.dma_start(pair_mask[:, :], a["ident"][0:PAIRS, 0:PAIRS]).then_inc(x_in, 16)
                sp.wait_ge(x_in, 48)

        def xattn(i):
            w = {k: a[f"x{i}_{k}"] for k in ("wq", "wk", "wv", "wo", "bq", "bv")}
            cross_attention(nc, f"x{i}", x_all, ident, pair_mask, a["ctxT"], bo=a["x0_bo"] if i == 0 else None, **w)

        xattn(0)
        self_attention(nc, x_sb, ident, a)
        experts(nc, x_sb, ident, a)
        xattn(1)
        mamba(nc, x_sb, ident, a)
        feed_forward(nc, x_sb, ident, a)
        with nc.Block() as block:
            @block.sync
            def _(sp):
                sp.dma_start(out.rearrange("(t p) d -> p t d", p=P), x_sb[:, :, :]).then_inc(x_out, 16)
                sp.wait_ge(x_out, 16)



def more_layouts(i, arr):
    import numpy as np
    f = np.float32
    arr["s_w"] = i["L0_attn_w_qkv"].reshape(KD, P, 3 * D).transpose(1, 0, 2)
    mask = np.zeros((P, 8), f)
    for r in range(P):
        mask[r, r // DH] = D ** -0.5
    arr["s_mask"] = mask
    arr["m_rms_w"] = i["L0_ffn_rms_w"].reshape(KD, P).T
    arr["m_gate_w"] = i["L0_ffn_gate_w"].T.reshape(KD, P, NE).transpose(1, 0, 2)
    const = {"rows_before": np.triu(np.ones((P, P), f), 1), "ones": np.ones(P, f), "experts": np.arange(NE, dtype=f) - NE,
             "tile_chain": np.tile(np.arange(NT) > 0, NE), "whole_blocks": P * np.arange(NT),
             "blocks": np.arange(SLOT_BLOCKS)}
    arr["m_const"] = np.concatenate([np.broadcast_to(const[k], (P, n)).astype(f) for k, n in M_CONST_PARTS], axis=1)
    for n in (1, 2):
        arr[f"m_w{n}"] = i[f"L0_ffn_W{n}"].transpose(0, 2, 1).reshape(NE, KD, P, DE).transpose(0, 2, 1, 3)
    w3 = np.zeros((NE, EC * P, D), f)
    w3[:, :DE] = i["L0_ffn_W3"].transpose(0, 2, 1)
    arr["m_w3"] = w3.reshape(NE, EC, P, D).transpose(0, 2, 1, 3)
    arr["b_win"] = i["L1_attn_W_in"].T.reshape(KD, P, 2 * DI).transpose(1, 0, 2)
    arr["b_wout"] = i["L1_attn_W_out"].T.reshape(CI, P, D).transpose(1, 0, 2)
    for tag, n in (("f", "fwd"), ("r", "rev")):
        def chunks(v):
            return v.reshape(CI, P, -1).transpose(1, 0, 2)
        arr[f"b{tag}_wx"] = chunks(i[f"L1_attn_Wx_{n}"].T)
        arr[f"b{tag}_wdt"] = i[f"L1_attn_Wdt_{n}"].T
        arr[f"b{tag}_a_log"] = chunks(i[f"L1_attn_A_log_{n}"])
        arr[f"b{tag}_vecs"] = np.concatenate(
            [chunks(i[f"L1_attn_{v}_{n}"]) for v in ("conv_w", "conv_b", "bdt", "D")], axis=2)
    arr["f_wi"] = i["L1_ffn_wi_w"].T.reshape(KD, P, FF).transpose(1, 0, 2)
    arr["f_wo"] = i["L1_ffn_wo_w"].T.reshape(CF, P, D).transpose(1, 0, 2)
    arr["f_lora_a"] = i["L1_ffn_lora_As"]
    arr["f_lora_b"] = i["L1_ffn_lora_Bs"].transpose(0, 2, 1)
    arr["f_index"] = i["L1_ffn_top_k_indices"].reshape(1, 2)
    arr["f_value"] = i["L1_ffn_top_k_values"]


def layouts(inputs):
    import numpy as np
    i = {k: np.asarray(v) for k, v in inputs.items()}
    f = np.float32
    arr = {"x": i["x"].reshape(TOK, D), "ident": np.eye(P, dtype=f)}
    ctxT = np.zeros((B + 2, DC, LKV), f)
    ctxT[:B] = i["ctx_512"].transpose(0, 2, 1)
    arr["ctxT"] = ctxT

    def xattn(n, wq, wk, wv, wo, bq, bv):
        arr[f"x{n}_wq"] = wq.reshape(KD, P, D).transpose(1, 0, 2)
        z = np.zeros((P, H, DC), f)
        for h in range(H):
            r = h % 8 * DH
            z[r:r + DH, h, :] = wk[:, h * DH:(h + 1) * DH].T
        arr[f"x{n}_wk"] = z
        arr[f"x{n}_wv"] = wv.reshape(DC, 2, 4, 2, DH).transpose(0, 1, 3, 2, 4).reshape(DC, D)
        arr[f"x{n}_bv"] = (bv if bv is not None else np.zeros(D, f)).reshape(PAIRS, 2, DH).transpose(0, 2, 1).reshape(P, 2)
        arr[f"x{n}_wo"] = wo.reshape(PAIRS, 2, DH, D).transpose(0, 2, 1, 3).reshape(P, 2, D)
        arr[f"x{n}_bq"] = (bq if bq is not None else np.zeros(D, f)).reshape(KD, P).T

    xattn(0, i["L0_xattn_Wq"], i["L0_xattn_Wk"], i["L0_xattn_Wv"], i["L0_xattn_Wo"], i["L0_xattn_bq"], i["L0_xattn_bv"])
    arr["x0_bo"] = i["L0_xattn_bo"]
    kv = i["L1_xattn_Wkv"]
    xattn(1, i["L1_xattn_Wq"].T, kv[:D].T, kv[D:].T, i["L1_xattn_Wo"].T, None, None)
    more_layouts(i, arr)
    return {k: np.ascontiguousarray(v) for k, v in arr.items()}


def kernel(**inputs):
    import concourse.bacc as bacc
    from concourse.bass_utils import run_bass_kernel_spmd

    arrays = layouts(inputs)
    nc = bacc.Bacc("TRN2", target_bir_lowering=False, num_devices=1)
    a = {k: nc.dram_tensor(f"in_{k}", v.shape, mybir.dt.from_np(v.dtype), kind="ExternalInput").ap()
         for k, v in arrays.items()}
    out = nc.dram_tensor("out_x", (TOK, D), F32, kind="ExternalOutput").ap()
    program(nc, a, out)
    r = run_bass_kernel_spmd(nc, [{f"in_{k}": v for k, v in arrays.items()}], core_ids=[0])
    return r.results[0]["out_x"].reshape(B, LQ, D)
```
